# Optimizing a Trainium2 kernel written in Bass

```python
import numpy as np
import jax
import jax.numpy as jnp

def _softmax(x, axis=-1):
    return jax.nn.softmax(x, axis=axis)

def _gelu(x):
    return jax.nn.gelu(x, approximate=True)

def _silu(x):
    return jax.nn.silu(x)

def _sigmoid(x):
    return jax.nn.sigmoid(x)

def _layernorm(x, axis=-1, eps=1e-05):
    m = jnp.mean(x, axis=axis, keepdims=True)
    v = jnp.var(x, axis=axis, keepdims=True)
    return (x - m) / jnp.sqrt(v + eps)

def _scatter_add(tgt, idx, src, axis=0):
    return tgt.at[idx].add(src)

def _segment_sum(src, seg, n):
    return jax.ops.segment_sum(src, seg, n)
kernel_name = 'mk_gnn_preln_d2_gnn_r32_1fde11'

def setup_inputs(seed: int=0):
    np.random.seed(seed)
    _w = jnp.asarray

    def _rec_inputs():
        import jax
        import jax.numpy as jnp
        _gk = jax.random.key(seed)
        x = -8.776e-05 + 1 * jax.random.normal(jax.random.fold_in(_gk, 1), (50000, 128), jnp.float32)
        src = jax.random.randint(jax.random.fold_in(_gk, 2), (25000,), 0, 50000, jnp.int32)
        dst = jax.random.randint(jax.random.fold_in(_gk, 3), (25000,), 0, 50000, jnp.int32)
        _o = jnp.argsort(dst, stable=True)
        src = src[_o]
        dst = dst[_o]
        edge_type_4 = jax.random.randint(jax.random.fold_in(_gk, 13), (25000,), 0, 4, jnp.int32)
        node_type_3 = jax.random.randint(jax.random.fold_in(_gk, 14), (50000,), 0, 3, jnp.int32)
        return (x, src, dst, edge_type_4, node_type_3)
    x, src, dst, edge_type_4, node_type_3 = _rec_inputs()

    def _L0_gnn_setup():
        import jax, jax.numpy as jnp
        import numpy as np
        import math
        N, E, D, T, R, H = (1250, 20000, 128, 3, 4, 8)
        DK = D // H

        def _hgt_forward(node_inp, node_type, edge_index, edge_type, Wk, bk, Wq, bq, Wv, bv, Wa, ba, rel_pri, rel_att, rel_msg, skip, ln_g, ln_b):
            n = node_inp.shape[0]
            out_dim = Wk.shape[2]
            n_heads, d_k = (rel_att.shape[1], rel_att.shape[2])
            sqrt_dk = math.sqrt(d_k)
            rng = jnp.arange(n)

            def type_proj(W, b):
                all_t = jnp.einsum('ni,tio->tno', node_inp, W) + b[:, None, :]
                return all_t[node_type, rng]
            k = type_proj(Wk, bk)
            q = type_proj(Wq, bq)
            v = type_proj(Wv, bv)
            src, dst = (edge_index[0], edge_index[1])
            q_e = q[dst].reshape(-1, n_heads, d_k)
            k_e = k[src].reshape(-1, n_heads, d_k)
            v_e = v[src].reshape(-1, n_heads, d_k)
            k_rot = jnp.zeros_like(k_e)
            msg = jnp.zeros_like(v_e)
            n_rel = rel_att.shape[0]
            for r in range(n_rel):
                m = (edge_type == r)[:, None, None]
                k_rot = k_rot + jnp.where(m, jnp.einsum('ehd,hdf->ehf', k_e, rel_att[r]), 0.0)
                msg = msg + jnp.where(m, jnp.einsum('ehd,hdf->ehf', v_e, rel_msg[r]), 0.0)
            att = (q_e * k_rot).sum(-1) * rel_pri[edge_type] / sqrt_dk
            seg_max = jax.ops.segment_max(att, dst, num_segments=n)
            seg_max = jnp.where(jnp.isfinite(seg_max), seg_max, 0.0)
            ex = jnp.exp(att - seg_max[dst])
            denom = jax.ops.segment_sum(ex, dst, num_segments=n)[dst] + 1e-16
            alpha = ex / denom
            out_e = (msg * alpha[:, :, None]).reshape(-1, out_dim)
            aggr = jax.ops.segment_sum(out_e, dst, num_segments=n)
            h = jax.nn.gelu(aggr, approximate=False)
            trans_all = jnp.einsum('no,top->tnp', h, Wa) + ba[:, None, :]
            trans = trans_all[node_type, rng]
            a = jax.nn.sigmoid(skip)[node_type][:, None]
            res = trans * a + node_inp * (1.0 - a)
            mu = res.mean(-1, keepdims=True)
            var = ((res - mu) ** 2).mean(-1, keepdims=True)
            normed = (res - mu) * jax.lax.rsqrt(var + 1e-05)
            return normed * ln_g[node_type] + ln_b[node_type]
        key = jax.random.key(seed)
        ks = jax.random.split(key, 16)
        glorot = lambda k, shape, fan: jax.random.normal(k, shape, jnp.float32) * math.sqrt(2.0 / fan)
        inp = {'node_inp': jax.random.normal(ks[0], (N, D), jnp.float32), 'node_type': jax.random.randint(ks[1], (N,), 0, T), 'edge_index': jax.random.randint(ks[2], (2, E), 0, N), 'edge_type': jax.random.randint(ks[3], (E,), 0, R), 'Wk': glorot(ks[4], (T, D, D), 2 * D), 'bk': jnp.zeros((T, D), jnp.float32), 'Wq': glorot(ks[5], (T, D, D), 2 * D), 'bq': jnp.zeros((T, D), jnp.float32), 'Wv': glorot(ks[6], (T, D, D), 2 * D), 'bv': jnp.zeros((T, D), jnp.float32), 'Wa': glorot(ks[7], (T, D, D), 2 * D), 'ba': jnp.zeros((T, D), jnp.float32), 'rel_pri': jnp.ones((R, H), jnp.float32), 'rel_att': glorot(ks[8], (R, H, DK, DK), 2 * DK), 'rel_msg': glorot(ks[9], (R, H, DK, DK), 2 * DK), 'skip': jnp.ones((T,), jnp.float32), 'ln_g': jnp.ones((T, D), jnp.float32), 'ln_b': jnp.zeros((T, D), jnp.float32)}
        return inp
    _L0_gnn_all = _L0_gnn_setup()
    _L0_gnn_in = {k: v for k, v in _L0_gnn_all.items() if k in ('Wk', 'bk', 'Wq', 'bq', 'Wv', 'bv', 'Wa', 'ba', 'rel_pri', 'rel_att', 'rel_msg', 'skip', 'ln_g', 'ln_b')}
    del _L0_gnn_all

    def _L1_gnn_setup():
        import jax, jax.numpy as jnp
        import numpy as np
        N_NODES = 3125
        N_EDGES = 50000
        IN_FEATS = 128
        N_HIDDEN = 128

        def _graph_conv(h, src, dst, W, b):
            n = h.shape[0]
            ones = jnp.ones(src.shape[0], dtype=h.dtype)
            out_deg = jnp.clip(jax.ops.segment_sum(ones, src, num_segments=n), 1.0)
            in_deg = jnp.clip(jax.ops.segment_sum(ones, dst, num_segments=n), 1.0)
            h = h * jax.lax.rsqrt(out_deg)[:, None]
            agg = jax.ops.segment_sum(h[src], dst, num_segments=n)
            agg = agg * jax.lax.rsqrt(in_deg)[:, None]
            return jax.nn.relu(agg @ W + b)
        key = jax.random.key(seed)
        ks = jax.random.split(key, 8)
        features = jax.random.normal(ks[0], (N_NODES, IN_FEATS), dtype=jnp.float32)
        src = jax.random.randint(ks[1], (N_EDGES,), 0, N_NODES, dtype=jnp.int64)
        dst = jax.random.randint(ks[2], (N_EDGES,), 0, N_NODES, dtype=jnp.int64)
        W1 = jax.random.normal(ks[3], (IN_FEATS, N_HIDDEN), dtype=jnp.float32) / np.sqrt(IN_FEATS)
        b1 = jnp.zeros((N_HIDDEN,), dtype=jnp.float32)
        W2 = jax.random.normal(ks[4], (N_HIDDEN, N_HIDDEN), dtype=jnp.float32) / np.sqrt(N_HIDDEN)
        b2 = jnp.zeros((N_HIDDEN,), dtype=jnp.float32)
        return {'features': features, 'W1': W1, 'b1': b1, 'W2': W2, 'b2': b2, 'src': src, 'dst': dst}
    _L1_gnn_all = _L1_gnn_setup()
    _L1_gnn_in = {k: v for k, v in _L1_gnn_all.items() if k in ('W1', 'b1', 'W2', 'b2')}
    del _L1_gnn_all
    return {'x': x, 'src': src, 'dst': dst, 'edge_type_4': edge_type_4, 'node_type_3': node_type_3, 'L0_gnn_Wk': _L0_gnn_in['Wk'], 'L0_gnn_bk': _L0_gnn_in['bk'], 'L0_gnn_Wq': _L0_gnn_in['Wq'], 'L0_gnn_bq': _L0_gnn_in['bq'], 'L0_gnn_Wv': _L0_gnn_in['Wv'], 'L0_gnn_bv': _L0_gnn_in['bv'], 'L0_gnn_Wa': _L0_gnn_in['Wa'], 'L0_gnn_ba': _L0_gnn_in['ba'], 'L0_gnn_rel_pri': _L0_gnn_in['rel_pri'], 'L0_gnn_rel_att': _L0_gnn_in['rel_att'], 'L0_gnn_rel_msg': _L0_gnn_in['rel_msg'], 'L0_gnn_skip': _L0_gnn_in['skip'], 'L0_gnn_ln_g': _L0_gnn_in['ln_g'], 'L0_gnn_ln_b': _L0_gnn_in['ln_b'], 'L1_gnn_W1': _L1_gnn_in['W1'], 'L1_gnn_b1': _L1_gnn_in['b1'], 'L1_gnn_W2': _L1_gnn_in['W2'], 'L1_gnn_b2': _L1_gnn_in['b2']}

def reference(x, src, dst, edge_type_4, node_type_3, L0_gnn_Wk, L0_gnn_bk, L0_gnn_Wq, L0_gnn_bq, L0_gnn_Wv, L0_gnn_bv, L0_gnn_Wa, L0_gnn_ba, L0_gnn_rel_pri, L0_gnn_rel_att, L0_gnn_rel_msg, L0_gnn_skip, L0_gnn_ln_g, L0_gnn_ln_b, L1_gnn_W1, L1_gnn_b1, L1_gnn_W2, L1_gnn_b2):
    import jax
    import jax.numpy as jnp

    def _L0_gnn_ref(node_inp, node_type, edge_index, edge_type, Wk, bk, Wq, bq, Wv, bv, Wa, ba, rel_pri, rel_att, rel_msg, skip, ln_g, ln_b):
        import jax, jax.numpy as jnp
        import numpy as np
        import math
        N, E, D, T, R, H = (1250, 20000, 128, 3, 4, 8)
        DK = D // H

        def _hgt_forward(node_inp, node_type, edge_index, edge_type, Wk, bk, Wq, bq, Wv, bv, Wa, ba, rel_pri, rel_att, rel_msg, skip, ln_g, ln_b):
            n = node_inp.shape[0]
            out_dim = Wk.shape[2]
            n_heads, d_k = (rel_att.shape[1], rel_att.shape[2])
            sqrt_dk = math.sqrt(d_k)
            rng = jnp.arange(n)

            def type_proj(W, b):
                all_t = jnp.einsum('ni,tio->tno', node_inp, W) + b[:, None, :]
                return all_t[node_type, rng]
            k = type_proj(Wk, bk)
            q = type_proj(Wq, bq)
            v = type_proj(Wv, bv)
            src, dst = (edge_index[0], edge_index[1])
            q_e = q[dst].reshape(-1, n_heads, d_k)
            k_e = k[src].reshape(-1, n_heads, d_k)
            v_e = v[src].reshape(-1, n_heads, d_k)
            k_rot = jnp.zeros_like(k_e)
            msg = jnp.zeros_like(v_e)
            n_rel = rel_att.shape[0]
            for r in range(n_rel):
                m = (edge_type == r)[:, None, None]
                k_rot = k_rot + jnp.where(m, jnp.einsum('ehd,hdf->ehf', k_e, rel_att[r]), 0.0)
                msg = msg + jnp.where(m, jnp.einsum('ehd,hdf->ehf', v_e, rel_msg[r]), 0.0)
            att = (q_e * k_rot).sum(-1) * rel_pri[edge_type] / sqrt_dk
            seg_max = jax.ops.segment_max(att, dst, num_segments=n)
            seg_max = jnp.where(jnp.isfinite(seg_max), seg_max, 0.0)
            ex = jnp.exp(att - seg_max[dst])
            denom = jax.ops.segment_sum(ex, dst, num_segments=n)[dst] + 1e-16
            alpha = ex / denom
            out_e = (msg * alpha[:, :, None]).reshape(-1, out_dim)
            aggr = jax.ops.segment_sum(out_e, dst, num_segments=n)
            h = jax.nn.gelu(aggr, approximate=False)
            trans_all = jnp.einsum('no,top->tnp', h, Wa) + ba[:, None, :]
            trans = trans_all[node_type, rng]
            a = jax.nn.sigmoid(skip)[node_type][:, None]
            res = trans * a + node_inp * (1.0 - a)
            mu = res.mean(-1, keepdims=True)
            var = ((res - mu) ** 2).mean(-1, keepdims=True)
            normed = (res - mu) * jax.lax.rsqrt(var + 1e-05)
            return normed * ln_g[node_type] + ln_b[node_type]
        return _hgt_forward(node_inp, node_type, edge_index, edge_type, Wk, bk, Wq, bq, Wv, bv, Wa, ba, rel_pri, rel_att, rel_msg, skip, ln_g, ln_b)

    def _L1_gnn_ref(features, W1, b1, W2, b2, src, dst):
        import jax, jax.numpy as jnp
        import numpy as np
        N_NODES = 3125
        N_EDGES = 50000
        IN_FEATS = 128
        N_HIDDEN = 128

        def _graph_conv(h, src, dst, W, b):
            n = h.shape[0]
            ones = jnp.ones(src.shape[0], dtype=h.dtype)
            out_deg = jnp.clip(jax.ops.segment_sum(ones, src, num_segments=n), 1.0)
            in_deg = jnp.clip(jax.ops.segment_sum(ones, dst, num_segments=n), 1.0)
            h = h * jax.lax.rsqrt(out_deg)[:, None]
            agg = jax.ops.segment_sum(h[src], dst, num_segments=n)
            agg = agg * jax.lax.rsqrt(in_deg)[:, None]
            return jax.nn.relu(agg @ W + b)
        h = _graph_conv(features, src, dst, W1, b1)
        h = _graph_conv(h, src, dst, W2, b2)
        return h
    edge_index = jnp.stack([src, dst])
    h = jnp.maximum(_layernorm(x, axis=-1), 0.0)
    x = x + _L0_gnn_ref(h, node_type_3, edge_index, edge_type_4, L0_gnn_Wk, L0_gnn_bk, L0_gnn_Wq, L0_gnn_bq, L0_gnn_Wv, L0_gnn_bv, L0_gnn_Wa, L0_gnn_ba, L0_gnn_rel_pri, L0_gnn_rel_att, L0_gnn_rel_msg, L0_gnn_skip, L0_gnn_ln_g, L0_gnn_ln_b)
    h = jnp.maximum(_layernorm(x, axis=-1), 0.0)
    x = x + _L1_gnn_ref(h, L1_gnn_W1, L1_gnn_b1, L1_gnn_W2, L1_gnn_b2, src, dst)
    return x

_drawn_inputs = setup_inputs


def setup_inputs(seed=0):
    import zlib

    import numpy as np

    out = dict(_drawn_inputs(seed))
    spreads = {'L0_gnn_bk': (0.0, 0.8),
     'L0_gnn_bq': (0.0, 0.8),
     'L0_gnn_bv': (0.0, 0.1),
     'L0_gnn_ba': (0.0, 0.1),
     'L0_gnn_rel_pri': (1.0, 0.6),
     'L0_gnn_skip': (1.0, 0.2),
     'L0_gnn_ln_g': (1.0, 0.2),
     'L0_gnn_ln_b': (0.0, 0.1),
     'L1_gnn_b1': (0.0, 0.471),
     'L1_gnn_b2': (0.0, 0.1)}
    factors = {}
    for name, (base, spread) in spreads.items():
        noise = np.random.default_rng([zlib.crc32(name.encode()), seed]).standard_normal(out[name].shape)
        drawn = base * np.exp(spread * noise) if base else spread * noise
        out[name] = jnp.asarray(drawn.astype(out[name].dtype))
    for name, factor in factors.items():
        out[name] = (out[name] * factor).astype(out[name].dtype)
    return out
```

```python
from contextlib import ExitStack

import concourse.bass as bass
from concourse import mybir

F32 = mybir.dt.float32
BF16 = mybir.dt.bfloat16
FP16 = mybir.dt.float16
I32 = mybir.dt.int32
ALU = mybir.AluOpType
ACT = mybir.ActivationFunctionType
AX = mybir.AxisListType

P = 128
D = 128
N = 50000
E = 25000
TYPES = 3
RELS = 4
HEADS = 8
DK = D // HEADS
ET = -(-E // P)
EP = ET * P
HALF = ET // 2
U = 4
EG = ET // U
NT = -(-N // P)
NP = NT * P
LO = NT
NG = 17
NGROUPS = NT // NG
GN = NG * P
LASTN = N - (NGROUPS - 1) * GN
LASTFULL = LASTN // NG
LASTREST = LASTN - LASTFULL * NG
TG = 7
TGROUPS = ET // TG
RW = 136
C_RSTD, C_NMR, C_TYPE, C_SO, C_SI, C_IDX = 128, 129, 130, 133, 134, 135
SKIP = 100000
RESET = -1.0e38
EPS = 1e-5
SPLIT = 3
K9 = TYPES * SPLIT
CW = 129
GW = 256

assert ET == 2 * HALF and ET == U * EG and NT == NG * NGROUPS and ET == TG * TGROUPS


def bcast(ap, shape):
    return ap.to_broadcast(shape)


def hgt_then_graphconv(nc, x, src, dst, edge_type, node_type, Wk, bk, Wq, bq, Wv, bv, Wa, ba, rel_pri, rel_att,
                       rel_msg, skip, ln_g, ln_b, W1, b1, W2, b2, out):
    top = ExitStack()
    with top, nc.allow_non_contiguous_dma(reason="small parameter and index lists"):
        def dram(name, shape, dt):
            return nc.dram_tensor(name, shape, dt, kind="Internal").ap()

        xt = dram("xt", [NP, RW], F32)
        xd_rows = dram("xd_rows", [EP, RW], F32)
        ta = dram("ta", [EP + NP, D], F32)
        t1 = dram("t1", [EP + 1, D], F32)
        x1_rows = dram("x1_rows", [EP, D], F32)
        attr = dram("attr", [3, NP], F32)
        reset_row = dram("reset_row", [EP], F32)
        keep_row = dram("keep_row", [EP], F32)
        dst_pad = dram("dst_pad", [EP + P], I32)
        src_pad = dram("src_pad", [EP + P], I32)
        et_pad = dram("et_pad", [EP + P], I32)
        type_pad = dram("type_pad", [NP], I32)

        def sb_in(ctx):
            return lambda name, shape, dt: ctx.enter_context(nc.sbuf_tensor(name, shape, dt))

        def ps_in(ctx):
            return lambda name, shape, dt: ctx.enter_context(nc.psum_tensor(name, shape, dt))

        def sem_in(ctx):
            return lambda name: ctx.enter_context(nc.semaphore(name))

        def phase_sems(prefix=""):
            held = []

            def take(name):
                held.append(nc.alloc_semaphore(prefix + name))
                return held[-1]

            def clear():
                nc.all_engine_barrier()
                nc.clear_and_free_semaphores(held)
                nc.all_engine_barrier()
            return take, clear

        sb, sem = sb_in(top), sem_in(top)
        ident = sb("ident", [P, P], F32)
        identb = sb("identb", [P, P], BF16)
        ends_i = sb("ends_i", [P, ET, 2], I32)
        out_i = sb("out_i", [P, ET], I32)
        rel_mask = sb("rel_mask", [P, ET, RELS], F32)
        kk9 = sb("kk9", [P, K9], F32)
        typ9 = sb("typ9", [K9, 1], F32)
        a3 = sb("a3", [P, TYPES], F32)
        w_kv = sb("w_kv", [P, TYPES, 2, D], F32)
        w_q = sb("w_q", [P, TYPES, D], F32)
        w_a = sb("w_a", [P, TYPES, D], F32)
        rel_k = sb("rel_k", [P, RELS, D], F32)
        rel_v = sb("rel_v", [P, RELS, D], F32)
        w_1 = sb("w_1", [P, D], F32)
        w_2 = sb("w_2", [P, D], F32)
        b1_all = sb("b1_all", [P, D], F32)
        b2_all = sb("b2_all", [P, D], F32)
        rb2_all = sb("rb2_all", [P, D], F32)
        ones3 = sb("ones3", [SPLIT, P], BF16)
        bias3 = sb("bias3", [SPLIT, TYPES * 3 * D], BF16)
        tab9 = sb("tab9", [K9, CW + GW], BF16)
        ats = sb("ats", [P, ET, 4], F32)
        iota3 = sb("iota3", [P, 4], F32)

        def edge_groups(eng, body):
            body(0, True, False)
            with eng.Fori(1, EG - 1) as i:
                body(i, False, False)
            body(EG - 1, False, True)

        def aggregate(st, tmp, mean, var, link):
            nc.vector.tensor_tensor(tmp[:, 0], st[:, :, 1], st[:, :, 4], ALU.add)
            nc.vector.tensor_tensor(tmp[:, 1], st[:, :, 1], st[:, :, 4], ALU.subtract)
            link(nc.vector.tensor_tensor(tmp[:, 2], st[:, :, 2], st[:, :, 5], ALU.add))
            nc.vector.tensor_scalar(mean, tmp[:, 0], 0.5, None, ALU.mult)
            nc.vector.tensor_scalar(tmp[:, 2], tmp[:, 2], 1.0 / D, EPS, ALU.mult, ALU.add)
            link(nc.vector.scalar_tensor_tensor(tmp[:, 1], tmp[:, 1], 0.25, tmp[:, 1], ALU.mult, ALU.mult))
            return nc.vector.tensor_tensor(var, tmp[:, 1], tmp[:, 2], ALU.add)

        turn = {}

        def settle(eng, name):
            if name not in turn:
                turn[name] = sem(f"turn_{name}")
            eng.sem_inc(turn[name], 1)

        with ExitStack() as ctx:
            lb, lp = sb_in(ctx), ps_in(ctx)
            ls, clear = phase_sems()
            pad_i = lb("pad_i", [1, 2, P], I32)
            rows = lb("rows", [HALF, 5, 2, P], I32)
            rowf = lb("rowf", [HALF, 5, 2, P], F32)
            flag = lb("flag", [HALF, 3, 2, P], F32)
            cols = lb("cols", [P, 4, ET], F32)
            hilo = lb("hilo", [P, 2, 2, ET], F32)
            hi_i = lb("hi_i", [P, 2, ET], I32)
            iota_i = lb("iota_i", [P, LO], I32)
            iota_h = lb("iota_h", [P, LO], FP16)
            kk_i = lb("kk_i", [P, K9], I32)
            row_i = lb("row_i", [K9, 1], I32)
            rowk = lb("rowk", [K9, 4], F32)
            rowk_i = lb("rowk_i", [K9, 1], I32)
            hot_hi = lb("hot_hi", [P, U, 2, P], BF16)
            hot_lo = lb("hot_lo", [P, U, 2, LO], BF16)
            deg = lb("deg", [P, 2, LO], F32)
            node_f = lb("node_f", [P, LO], F32)
            node_i = lb("node_i", [P, LO], I32)
            cum = lb("cum", [P, LO], F32)
            has = lb("has", [P, LO], F32)
            zero = lb("zero", [P, LO], F32)
            power = lb("power", [P, 2, LO], F32)
            at3 = lb("at3", [P, 3, LO], F32)
            upper = lb("upper", [P, P], F32)
            pri = lb("pri", [P, RELS], F32)
            bias_f = lb("bias_f", [SPLIT, TYPES * 3 * D], F32)
            bias_r = lb("bias_r", [SPLIT, TYPES * 3 * D], F32)
            bias_p = lb("bias_p", [SPLIT, SPLIT, TYPES * 3 * D], BF16)
            tab_f = lb("tab_f", [K9, CW + GW], F32)
            tab_r = lb("tab_r", [K9, CW + GW], F32)
            tab_p = lb("tab_p", [K9, SPLIT, CW + GW], BF16)
            sk9 = lb("sk9", [K9, 1], F32)
            t1d = lb("t1d", [1, D], F32)
            tp = [lp(f"tp{i}", [P, 4, HALF], F32) for i in range(2)]
            hist = [lp(f"hist{i}", [P, LO], F32) for i in range(2)]
            offs = lp("offs", [P, 1], F32)
            padded = ls("padded")
            pads_set = ls("pads_set")
            rows_in = ls("rows_in")
            weights_in = ls("weights_in")
            rel_zero = ls("rel_zero")
            pool_c = ls("pool_c")
            vec = ls("vec")
            exps = ls("exps")
            sk_in = ls("sk_in")
            rows_ready = ls("rows_ready")
            tps = ls("tps")
            hots = ls("hots")
            hists = ls("hists")
            tot_ready = ls("tot_ready")
            offs_ready = ls("offs_ready")
            powed = ls("powed")
            deg_ready = ls("deg_ready")
            flags_ready = ls("flags_ready")
            stored = ls("stored")
            with nc.Block() as block:
                @block.sync
                def _(sp):
                    for pad, given in ((dst_pad, dst), (src_pad, src), (et_pad, edge_type)):
                        sp.dma_start(pad[1:1 + E].rearrange("(a b) -> a b", b=25),
                                     given.rearrange("(a b) -> a b", b=25)).then_inc(padded, 16)
                    sp.wait_ge(pads_set, 3)
                    for pad, k in ((dst_pad, 0), (src_pad, 0), (et_pad, 1)):
                        sp.dma_start(pad[0:1].rearrange("(o b) -> o b", o=1), pad_i[:, 1, 0:1]).then_inc(padded, 16)
                        sp.dma_start(pad[1 + E:EP + 3].rearrange("(o b) -> o b", o=1),
                                     pad_i[:, k, 0:EP + 2 - E]).then_inc(padded, 16)
                    sp.dma_start(type_pad[0:N].rearrange("(a b) -> a b", b=50),
                                 node_type.rearrange("(a b) -> a b", b=50)).then_inc(padded, 16)
                    sp.dma_start(type_pad[N:NP].rearrange("(o b) -> o b", o=1), pad_i[:, 1, 1:1 + NP - N]).then_inc(padded, 16)
                    sp.wait_ge(padded, 16 * 11)
                    for k, (pad, at) in enumerate(((dst_pad, 1), (dst_pad, 0), (dst_pad, 2), (src_pad, 1), (et_pad, 1))):
                        sp.dma_start(rows[:, k], pad[at:at + EP].rearrange("(c q r) -> q c r", c=2, q=HALF)).then_inc(rows_in, 16)
                    sp.wait_ge(flags_ready, 1)
                    sp.dma_start(reset_row.rearrange("(c q r) -> q c r", c=2, q=HALF), flag[:, 0]).then_inc(stored, 16)
                    sp.dma_start(keep_row.rearrange("(c q r) -> q c r", c=2, q=HALF), flag[:, 1]).then_inc(stored, 16)
                    sp.wait_ge(deg_ready, 1)
                    for k in range(3):
                        sp.dma_start(attr[k].rearrange("(p l) -> p l", p=P), at3[:, k]).then_inc(stored, 16)
                    sp.wait_ge(stored, 16 * 5)

                @block.scalar
                def _(act):
                    for t in range(TYPES):
                        act.dma_start(w_kv[:, t, 0], Wk[t]).then_inc(weights_in, 16)
                        act.dma_start(w_kv[:, t, 1], Wv[t]).then_inc(weights_in, 16)
                        act.dma_start(w_q[:, t], Wq[t]).then_inc(weights_in, 16)
                        act.dma_start(w_a[:, t], Wa[t]).then_inc(weights_in, 16)
                    act.dma_start(w_1[:], W1).then_inc(weights_in, 16)
                    act.dma_start(w_2[:], W2).then_inc(weights_in, 16)
                    act.dma_start(b1_all[:], b1.partition_broadcast(P)).then_inc(weights_in, 16)
                    act.dma_start(b2_all[:], b2.partition_broadcast(P)).then_inc(weights_in, 16)
                    act.dma_start(a3[:], skip.partition_broadcast(P)).then_inc(sk_in, 16)
                    for t in range(TYPES):
                        r9 = slice(SPLIT * t, SPLIT * t + SPLIT)
                        act.dma_start(sk9[r9], skip[t:t + 1].partition_broadcast(SPLIT)).then_inc(sk_in, 16)
                        act.dma_start(tab_f[r9, 0:D], ba[t].partition_broadcast(SPLIT)).then_inc(weights_in, 16)
                        act.dma_start(tab_f[r9, CW:CW + D], ln_g[t].partition_broadcast(SPLIT)).then_inc(weights_in, 16)
                        act.dma_start(tab_f[r9, CW + D:CW + GW], ln_b[t].partition_broadcast(SPLIT)).then_inc(weights_in, 16)
                        at = 2 * D * t
                        act.dma_start(bias_f[:, at:at + D], bk[t].partition_broadcast(SPLIT)).then_inc(weights_in, 16)
                        act.dma_start(bias_f[:, at + D:at + 2 * D], bv[t].partition_broadcast(SPLIT)).then_inc(weights_in, 16)
                        at = 2 * D * TYPES + D * t
                        act.dma_start(bias_f[:, at:at + D], bq[t].partition_broadcast(SPLIT)).then_inc(weights_in, 16)
                    act.wait_ge(rel_zero, 2)
                    for h in range(HEADS):
                        hs = slice(DK * h, DK * h + DK)
                        act.dma_start(rel_k[hs, :, hs], rel_att[:, h].rearrange("r d f -> d r f")).then_inc(weights_in, 16)
                        act.dma_start(rel_v[hs, :, hs], rel_msg[:, h].rearrange("r d f -> d r f")).then_inc(weights_in, 16)
                        act.dma_start(pri[hs, :], rel_pri[:, h].partition_broadcast(DK)).then_inc(weights_in, 16)
                    act.wait_ge(sk_in, 16 * 4)
                    nc.scalar.activation(a3[:], a3[:], ACT.Exp, scale=-1.0).then_inc(exps, 1)
                    nc.scalar.activation(sk9[:], sk9[:], ACT.Exp, scale=-1.0).then_inc(exps, 1)

                @block.gpsimd
                def _(pool):
                    pool.memset(pad_i[:, 0], N).then_inc(pads_set, 1)
                    pool.memset(pad_i[:, 1, 0:1], -1).then_inc(pads_set, 1)
                    pool.memset(pad_i[:, 1, 1:P], 0).then_inc(pads_set, 1)
                    pool.memset(rel_k[:], 0.0).then_inc(rel_zero, 1)
                    pool.memset(rel_v[:], 0.0).then_inc(rel_zero, 1)
                    pool.memset(ident[:], 0.0).then_inc(pool_c, 1)
                    pool.memset(identb[:], 0.0).then_inc(pool_c, 1)
                    pool.memset(upper[:], 1.0).then_inc(pool_c, 1)
                    pool.wait_ge(pool_c, 3)
                    for m in (ident, identb):
                        pool.affine_select(out=m[:], in_=m[:], compare_op=ALU.not_equal, fill=1.0, base=0,
                                           pattern=[[-1, P]], channel_multiplier=1).then_inc(pool_c, 1)
                    pool.affine_select(out=upper[:], in_=upper[:], compare_op=ALU.is_ge, fill=0.0, base=-1,
                                       pattern=[[1, P]], channel_multiplier=-1).then_inc(pool_c, 1)
                    pool.iota(iota_i[:], [[1, LO]], base=0, channel_multiplier=0).then_inc(pool_c, 1)
                    pool.iota(kk_i[:], [[1, TYPES], [0, SPLIT]], base=0, channel_multiplier=0).then_inc(pool_c, 1)
                    pool.iota(row_i[:], [[1, 1]], base=0, channel_multiplier=1).then_inc(pool_c, 1)
                    pool.iota(node_i[:], [[1, LO]], base=EP, channel_multiplier=LO).then_inc(pool_c, 1)
                    pool.memset(power[:], -0.5).then_inc(pool_c, 1)
                    pool.wait_ge(tot_ready, 1)
                    pool.tensor_tensor(at3[:, 0:2], deg[:], power[:], ALU.pow).then_inc(powed, 1)

                @block.vector
                def _(dve):
                    n = [0]

                    def link(ins):
                        n[0] += 1
                        ins.then_inc(vec, 1)
                        dve.wait_ge(vec, n[0])

                    dve.memset(zero[:], 0.0).then_inc(vec, 1)
                    dve.memset(ones3[:], 1.0).then_inc(vec, 1)
                    n[0] = 2
                    dve.wait_ge(pool_c, 11)
                    dve.tensor_copy(iota_h[:], iota_i[:]).then_inc(vec, 1)
                    dve.tensor_copy(iota3[:], iota_i[:, 0:4]).then_inc(vec, 1)
                    dve.tensor_copy(kk9[:], kk_i[:]).then_inc(vec, 1)
                    dve.tensor_copy(node_f[:], node_i[:]).then_inc(vec, 1)
                    n[0] += 4
                    link(dve.tensor_copy(rowk[:, 0:1], row_i[:]))
                    link(dve.tensor_scalar(rowk_i[:], rowk[:, 0:1], -1.0, 1.0 / SPLIT, ALU.add, ALU.mult))
                    link(dve.tensor_copy(typ9[:], rowk_i[:]))
                    link(dve.scalar_tensor_tensor(rowk[:, 1:2], typ9[:], -float(SPLIT), rowk[:, 0:1], ALU.mult, ALU.add))
                    dve.wait_ge(rows_in, 16 * 5)
                    link(dve.tensor_copy(rowf[:], rows[:]))
                    link(dve.tensor_tensor(flag[:, 1], rowf[:, 0], rowf[:, 1], ALU.is_equal))
                    link(dve.tensor_scalar(flag[:, 0], flag[:, 1], -RESET, RESET, ALU.mult, ALU.add))
                    link(dve.tensor_tensor(flag[:, 2], rowf[:, 0], rowf[:, 2], ALU.is_equal))
                    dve.scalar_tensor_tensor(rowf[:, 1], flag[:, 2], float(SKIP), rowf[:, 0], ALU.mult,
                                             ALU.add).then_inc(flags_ready, 1)
                    dve.wait_ge(tps, 8)
                    for c in range(2):
                        dve.tensor_copy(cols[:, :, c * HALF:(c + 1) * HALF], tp[c][:]).then_inc(vec, 1)
                    n[0] += 2
                    dve.wait_ge(vec, n[0])
                    for to, k in ((ends_i[:, :, 1], 0), (out_i[:], 1), (ends_i[:, :, 0], 2)):
                        dve.tensor_copy(to, cols[:, k]).then_inc(vec, 1)
                    dve.tensor_tensor(rel_mask[:], cols[:, 3].rearrange("p (t o) -> p t o", o=1).to_broadcast([P, ET, RELS]),
                                      iota3[:].rearrange("p (o r) -> p o r", o=1).to_broadcast([P, ET, RELS]),
                                      ALU.is_equal).then_inc(vec, 1)
                    n[0] += 4
                    for s, k in ((0, 2), (1, 0)):
                        link(dve.tensor_scalar(hi_i[:, s], cols[:, k], -(LO - 1) / 2.0, 1.0 / LO, ALU.add, ALU.mult))
                        link(dve.tensor_copy(hilo[:, s, 0], hi_i[:, s]))
                        link(dve.scalar_tensor_tensor(hilo[:, s, 1], hilo[:, s, 0], -float(LO), cols[:, k], ALU.mult, ALU.add))

                    def hot(g, first, last):
                        for u in range(U):
                            t = g * U + u
                            if not first:
                                dve.wait_ge(hists, t - U + 1)
                            for s in range(2):
                                dve.tensor_scalar(hot_hi[:, u, s], iota_h[:, 0:P], hilo[:, s, 0, bass.ds(t, 1)], None,
                                                  ALU.is_equal).then_inc(hots, 1)
                                dve.tensor_scalar(hot_lo[:, u, s], iota_h[:], hilo[:, s, 1, bass.ds(t, 1)], None,
                                                  ALU.is_equal).then_inc(hots, 1)
                    edge_groups(dve, hot)
                    dve.wait_ge(exps, 2)
                    link(dve.tensor_scalar_add(a3[:], a3[:], 1.0))
                    link(dve.reciprocal(a3[:], a3[:]))
                    link(dve.tensor_scalar_add(sk9[:], sk9[:], 1.0))
                    link(dve.reciprocal(sk9[:], sk9[:]))
                    dve.wait_ge(weights_in, 16 * (16 + 18 + 3 * HEADS))
                    link(dve.tensor_scalar(pri[:], pri[:], DK ** -0.5, None, ALU.mult))
                    for r in range(RELS):
                        link(dve.tensor_scalar(rel_k[:, r], rel_k[:, r], pri[:, r:r + 1], None, ALU.mult))
                    link(dve.tensor_scalar_max(rb2_all[:], b2_all[:], 0.0))
                    link(dve.tensor_scalar_max(t1d[:], b1_all[0:1], 0.0))
                    link(dve.tensor_scalar(tab_f[:, 0:D], tab_f[:, 0:D], sk9[:], None, ALU.mult))
                    link(dve.tensor_scalar(tab_f[:, D:CW], sk9[:], -1.0, 1.0, ALU.mult, ALU.add))
                    for f, r, p, o, part in ((bias_f, bias_r, bias_p, bias3, 0), (tab_f, tab_r, tab_p, tab9, 1)):
                        link(dve.tensor_copy(p[:, 0], f[:]))
                        link(dve.tensor_tensor(r[:], f[:], p[:, 0], ALU.subtract))
                        link(dve.tensor_copy(p[:, 1], r[:]))
                        link(dve.tensor_tensor(r[:], r[:], p[:, 1], ALU.subtract))
                        link(dve.tensor_copy(p[:, 2], r[:]))
                        rows_n = f.shape[0]
                        for k in range(SPLIT):
                            link(dve.tensor_scalar(rowk[0:rows_n, 2:3], rowk[0:rows_n, part:part + 1], float(k), None, ALU.is_equal))
                            if k == 0:
                                link(dve.tensor_scalar(o[:], p[:, k], rowk[0:rows_n, 2:3], None, ALU.mult))
                            else:
                                link(dve.scalar_tensor_tensor(o[:], p[:, k], rowk[0:rows_n, 2:3], o[:], ALU.mult, ALU.add))
                    dve.wait_ge(hists, ET)
                    for s in range(2):
                        link(dve.tensor_scalar_max(deg[:, s], hist[s][:], 1.0))
                    dve.tensor_scalar_min(has[:], hist[1][:], 1.0).then_inc(vec, 1)
                    n[0] += 1
                    link(dve.tensor_tensor_scan(cum[:], hist[1][:], zero[:], 0.0, ALU.add, ALU.add))
                    dve.sem_inc(tot_ready, 1)
                    dve.wait_ge(offs_ready, 1)
                    link(dve.tensor_scalar(cum[:], cum[:], offs[:], -1.0, ALU.add, ALU.add))
                    link(dve.tensor_tensor(cum[:], cum[:], node_f[:], ALU.subtract))
                    link(dve.tensor_tensor(cum[:], cum[:], has[:], ALU.mult))
                    link(dve.tensor_tensor(at3[:, 2], cum[:], node_f[:], ALU.add))
                    dve.wait_ge(powed, 1)
                    dve.sem_inc(deg_ready, 1)

                @block.tensor
                def _(pe):
                    pe.wait_ge(pool_c, 6)
                    pe.wait_ge(flags_ready, 1)
                    for c in range(2):
                        for k, at in enumerate((0, 1, 3, 4)):
                            nc.tensor.transpose(tp[c][:, k], rowf[:, at, c], ident[0:HALF, 0:HALF]).then_inc(tps, 1)

                    def product(g, first, last):
                        for u in range(U):
                            t = g * U + u
                            pe.wait_ge(hots, 4 * t + 4)
                            for s in range(2):
                                m = nc.tensor.matmul(hist[s][:], hot_hi[:, u, s], hot_lo[:, u, s],
                                                     start=first and u == 0, stop=last and u == U - 1)
                            m.then_inc(hists, 1)
                    edge_groups(pe, product)
                    pe.wait_ge(tot_ready, 1)
                    nc.tensor.matmul(offs[:], upper[:], cum[:, LO - 1:LO], start=True, stop=True).then_inc(offs_ready, 1)
            with nc.Block() as block:
                @block.sync
                def _(sp):
                    sp.dma_start(t1[EP:EP + 1], t1d[:]).then_inc(stored, 16)
                    sp.wait_ge(stored, 16 * 6)
            clear()

        def node_groups(eng, body):
            body(0, 0, True, False)
            body(1, 1, True, False)
            with eng.Fori(1, (NGROUPS - 1) // 2) as i:
                body(2 * i, 0, False, False)
                body(2 * i + 1, 1, False, False)
            body(NGROUPS - 1, 0, False, True)

        with ExitStack() as ctx:
            lb = sb_in(ctx)
            ls, clear = phase_sems()
            xr = [lb(f"xr{b}", [P, NG, RW], F32) for b in range(2)]
            ar = [lb(f"ar{b}", [P, 3, NG], F32) for b in range(2)]
            ty = [lb(f"ty{b}", [P, NG], I32) for b in range(2)]
            st = [lb(f"st{b}", [P, NG, 6], F32) for b in range(2)]
            mv = [lb(f"mv{b}", [P, NG], F32) for b in range(2)]
            ve = [lb(f"ve{b}", [P, NG], F32) for b in range(2)]
            mh = lb("mh", [P, NG], F32)
            tmp = lb("tmp", [P, 3, NG], F32)
            half_set = ls("half_set")
            loaded = [ls(f"loaded{b}") for b in range(2)]
            written = [ls(f"written{b}") for b in range(2)]
            stats = ls("stats")
            var_ready = ls("var_ready")
            rstd_ready = ls("rstd_ready")
            row_ready = ls("row_ready")
            pad_set = ls("pad_set")
            with nc.Block() as block:
                @block.sync
                def _(sp):
                    def load(g, b, first, last):
                        if not first:
                            sp.wait_ge(written[b], wr(g, b))
                        if not last:
                            sp.dma_start(xr[b][:, :, 0:D], x[bass.ds(g * GN, GN)].rearrange("(p j) d -> p j d", p=P)).then_inc(loaded[b], 16)
                            sp.dma_start(ty[b][:], node_type[bass.ds(g * GN, GN)].rearrange("(p j) -> p j", p=P)).then_inc(loaded[b], 16)
                        else:
                            sp.wait_ge(pad_set, 1)
                            n0 = g * GN
                            n1 = n0 + LASTFULL * NG
                            sp.dma_start(xr[b][0:LASTFULL, :, 0:D], x[n0:n1].rearrange("(p j) d -> p j d", j=NG)).then_inc(loaded[b], 16)
                            sp.dma_start(xr[b][LASTFULL:LASTFULL + 1, 0:LASTREST, 0:D], x[n1:N].rearrange("(p j) d -> p j d", p=1)).then_inc(loaded[b], 16)
                            sp.dma_start(ty[b][0:LASTFULL], node_type[n0:n1].rearrange("(p j) -> p j", j=NG)).then_inc(loaded[b], 16)
                            sp.dma_start(ty[b][LASTFULL:LASTFULL + 1, 0:LASTREST], node_type[n1:N].rearrange("(p j) -> p j", p=1)).then_inc(loaded[b], 16)
                        sp.dma_start(ar[b][:], attr[:, bass.ds(g * GN, GN)].rearrange("k (p j) -> p k j", p=P)).then_inc(loaded[b], 16)

                    def wr(g, b):
                        return (g - b) * 8

                    node_groups(sp, load)

                @block.scalar
                def _(act):
                    def write(g, b, first, last):
                        act.wait_ge(row_ready, g + 1)
                        act.dma_start(xt[bass.ds(g * GN, GN)].rearrange("(p j) w -> p j w", p=P), xr[b][:]).then_inc(written[b], 16)
                    node_groups(act, write)
                    act.wait_ge(written[0], 16 * (NGROUPS // 2 + 1))
                    act.wait_ge(written[1], 16 * (NGROUPS // 2))

                @block.gpsimd
                def _(pool):
                    pool.memset(mh[:], -0.5).then_inc(half_set, 1)
                    pool.wait_ge(half_set, 1)

                    def rstd(g, b, first, last):
                        pool.wait_ge(var_ready, g + 1)
                        settle(pool, "pool")
                        pool.tensor_tensor(xr[b][:, :, C_RSTD], ve[b][:], mh[:], ALU.pow).then_inc(rstd_ready, 1)
                    node_groups(pool, rstd)

                @block.vector
                def _(dve):
                    def norm(g, b, first, last):
                        if last:
                            dve.wait_ge(written[b], 16 * (g // 2))
                            dve.memset(xr[b][:], 0.0).then_inc(stats, 1)
                            dve.memset(ty[b][:], 0).then_inc(stats, 1)
                            dve.wait_ge(stats, 6 * g + 2)
                            dve.sem_inc(pad_set, 1)
                        s0 = g * 6 + (2 if last else 0)
                        dve.wait_ge(loaded[b], (g - b) * 24 + (16 * 5 if last else 48))
                        for j in range(NG):
                            i = dve.bn_stats(st[b][:, j], xr[b][:, j, 0:D])
                        i.then_inc(stats, 1)
                        dve.wait_ge(stats, s0 + 1)

                        k = [s0 + 1]

                        def link(ins):
                            k[0] += 1
                            ins.then_inc(stats, 1)
                            dve.wait_ge(stats, k[0])
                        aggregate(st[b], tmp, mv[b][:], ve[b][:], link).then_inc(var_ready, 1)
                        dve.tensor_tensor(xr[b][:, :, C_TYPE:C_TYPE + TYPES],
                                          ty[b][:].rearrange("p (j o) -> p j o", o=1).to_broadcast([P, NG, TYPES]),
                                          iota3[:, 0:TYPES].rearrange("p (o t) -> p o t", o=1).to_broadcast([P, NG, TYPES]),
                                          ALU.is_equal).then_inc(stats, 1)
                        dve.tensor_copy(xr[b][:, :, C_SO:C_IDX + 1].rearrange("p j k -> p k j"), ar[b][:]).then_inc(stats, 1)
                        dve.wait_ge(rstd_ready, g + 1)
                        dve.scalar_tensor_tensor(xr[b][:, :, C_NMR], mv[b][:], -1.0, xr[b][:, :, C_RSTD], ALU.mult,
                                                 ALU.mult).then_inc(stats, 1)
                        dve.wait_ge(stats, s0 + 6)
                        dve.sem_inc(row_ready, 1)
                    node_groups(dve, norm)
            clear()

        def rows_phase(edges):
            G, groups = (TG, TGROUPS) if edges else (NG, NGROUPS)
            name = "edge" if edges else "node"
            CB = 1 if edges else 3
            banks = 4 if edges else 6
            cols = 4 * D if edges else CW
            parts = -(-G // CB)
            pairs = -(-G // 2)
            ctx = ExitStack()
            with ctx:
                def lb(n, shape, dt):
                    return ctx.enter_context(nc.sbuf_tensor(f"{name}_{n}", shape, dt))

                def lp(n, shape, dt):
                    return ctx.enter_context(nc.psum_tensor(f"{name}_{n}", shape, dt))

                ls, clear = phase_sems(name + "_")

                two = range(2)
                xr = [lb(f"xr{b}", [P, G, RW], F32) for b in two]
                hb = [lb(f"hb{b}", [P, G, D], F32) for b in two]
                rs = [lb(f"rs{b}", [P, G, D], F32) for b in two]
                hs = [lb(f"hs{b}", [P, G, D], F32) for b in two]
                ot = [lb(f"ot{b}", [P, G, D], F32) for b in two]
                oh = [lb(f"oh{b}", [K9, G * P], BF16) for b in two]
                st = lb("st", [P, G, 6], F32)
                tmp = lb("tmp", [P, 3, G], F32)
                mean = [[lb(f"mean{k}{b}", [P, G], F32) for b in two] for k in two]
                var = [[lb(f"var{k}{b}", [P, G], F32) for b in two] for k in two]
                rstd = [[lb(f"rstd{k}{b}", [P, G], F32) for b in two] for k in two]
                nmr = [[lb(f"nmr{k}{b}", [P, G], F32) for b in two] for k in two]
                sc3 = [lb(f"sc3{b}", [P, G], F32) for b in two]
                mh = lb("mh", [P, G], F32)
                if edges:
                    gl = [lb(f"gl{b}", [P, G * P], F32) for b in two]
                    oc = lb("oc", [P, G, TYPES, SPLIT], BF16)
                    am = lb("am", [P, G, TYPES], F32)
                    om = lb("om", [P, G], F32)
                    ohp = lp("ohp", [K9, G * P], BF16)
                else:
                    t9 = [lb(f"t9{b}", [K9, G * P], I32) for b in two]
                pc = lp("pc", [P, banks, 512], F32)
                pg = lp("pg", [P, 2, 2, GW], F32)
                loaded = [ls(f"loaded{b}") for b in two]
                half_set, gl_done, h_done, oc_ready, ohp_ready, oh_ready = (
                    ls("half_set"), ls("gl_done"), ls("h_done"), ls("oc_ready"), ls("ohp_ready"), ls("oh_ready"))
                c_ready, c_read, c1, c2 = ls("c_ready"), ls("c_read"), ls("c1"), ls("c2")
                var2_ready, rstd2_ready, nm2_ready, y_done = ls("var2"), ls("rstd2"), ls("nm2"), ls("y_done")
                g_ready, g_read = ls("g_ready"), ls("g_read")
                var3_ready, rstd3_ready, nm3_ready, hs_done, ot_done = (
                    ls("var3"), ls("rstd3"), ls("nm3"), ls("hs_done"), ls("ot_done"))
                hs_out = [ls(f"hs_out{b}") for b in two]
                ot_out = [ls(f"ot_out{b}") for b in two]
                per_load = 16 if edges else 32

                def steps(eng, body):
                    for g in range(4):
                        body(g, g % 2)
                    with eng.Fori(2, (groups - 1) // 2) as i:
                        body(i * 2, 0)
                        body(i * 2 + 1, 1)
                    for g in range((groups - 1) // 2 * 2, groups + 1):
                        body(g, g % 2)

                def real(g):
                    return not isinstance(g, int) or 0 <= g < groups

                def later(g, k):
                    return not isinstance(g, int) or g >= k

                with nc.Block() as block:
                    @block.sync
                    def _(sp):
                        def step(g, b):
                            if real(g):
                                if later(g, 2):
                                    sp.wait_ge(nm3_ready, g - 1)
                                    settle(sp, "sp")
                                    sp.wait_ge(h_done, (g - 1) * G)
                                    settle(sp, "sp")
                                if edges:
                                    sp.dma_start(xr[b][:], xd_rows[bass.ds(g * (G * P), G * P)].rearrange("(t p) w -> p t w", p=P)).then_inc(loaded[b], 16)
                                else:
                                    sp.dma_start(xr[b][:], xt[bass.ds(g * GN, GN)].rearrange("(p j) w -> p j w", p=P)).then_inc(loaded[b], 16)
                                    if later(g, 2):
                                        sp.wait_ge(oh_ready, g - 1)
                                        settle(sp, "sp")
                                    sp.dma_start(t9[b][:], type_pad[bass.ds(g * GN, GN)].partition_broadcast(K9)).then_inc(loaded[b], 16)
                            if real(g - 1):
                                sp.wait_ge(ot_done, g)
                                settle(sp, "sp")
                                if edges:
                                    sp.dma_start(x1_rows[bass.ds((g - 1) * (G * P), G * P)].rearrange("(t p) w -> p t w", p=P), ot[1 - b][:]).then_inc(ot_out[1 - b], 16)
                                elif isinstance(g, int) and g == groups:
                                    n0 = (g - 1) * GN
                                    n1 = n0 + LASTFULL * NG
                                    sp.dma_start(out[n0:n1].rearrange("(p j) d -> p j d", j=NG), ot[1 - b][0:LASTFULL]).then_inc(ot_out[1 - b], 16)
                                    sp.dma_start(out[n1:N].rearrange("(p j) d -> p j d", p=1), ot[1 - b][LASTFULL:LASTFULL + 1, 0:LASTREST]).then_inc(ot_out[1 - b], 16)
                                else:
                                    sp.dma_start(out[bass.ds((g - 1) * GN, GN)].rearrange("(p j) d -> p j d", p=P), ot[1 - b][:]).then_inc(ot_out[1 - b], 16)
                        steps(sp, step)
                        for b in two:
                            n = (groups + 1 - b) // 2
                            sp.wait_ge(hs_out[b], 16 * n)
                            sp.wait_ge(ot_out[b], 16 * (n + (not edges and (groups - 1) % 2 == b)))

                    @block.gpsimd
                    def _(pool):
                        pool.memset(mh[:], -0.5).then_inc(half_set, 1)
                        pool.wait_ge(half_set, 1)

                        def step(g, b):
                            if real(g):
                                pool.wait_ge(var2_ready, g + 1)
                                settle(pool, "pool")
                                pool.tensor_tensor(rstd[0][b][:], var[0][b][:], mh[:], ALU.pow).then_inc(rstd2_ready, 1)
                            if real(g - 1):
                                pool.wait_ge(var3_ready, g)
                                settle(pool, "pool")
                                pool.tensor_tensor(rstd[1][1 - b][:], var[1][1 - b][:], mh[:], ALU.pow).then_inc(rstd3_ready, 1)
                        steps(pool, step)

                    @block.scalar
                    def _(act):
                        def clipped(g, b):
                            act.wait_ge(loaded[b], (g - b) * (per_load // 2) + per_load)
                            if later(g, 2):
                                act.wait_ge(c_read, (g - 1) * parts)
                            for j in range(G):
                                nc.scalar.activation(hb[b][:, j], xr[b][:, j, 0:D], ACT.Relu, bias=xr[b][:, j, C_NMR:C_NMR + 1],
                                                     scale=xr[b][:, j, C_RSTD:C_RSTD + 1]).then_inc(h_done, 1)
                            if edges:
                                settle(act, "act")
                                nc.scalar.activation(gl[b][:], agg[:, bass.ds(g * (G * P), G * P)], ACT.Gelu).then_inc(gl_done, 1)

                        def step(g, b):
                            if isinstance(g, int) and g == 0:
                                clipped(0, 0)
                            if edges and real(g):
                                act.wait_ge(ohp_ready, g + 1)
                                nc.scalar.activation(oh[b][:], ohp[:], ACT.Copy).then_inc(oh_ready, 1)
                            if real(g + 1):
                                clipped(g + 1, 1 - b)
                            if real(g):
                                act.wait_ge(nm2_ready, g + 1)
                                for j in range(G):
                                    nc.scalar.activation(rs[b][:, j], rs[b][:, j], ACT.Identity, bias=nmr[0][b][:, j:j + 1],
                                                         scale=rstd[0][b][:, j:j + 1]).then_inc(y_done, 1)
                            if real(g - 1):
                                act.wait_ge(nm3_ready, g)
                                if later(g, 3):
                                    act.wait_ge(hs_out[1 - b], (g - 1 - (1 - b)) * 8)
                                for j in range(G):
                                    m = nc.scalar.activation(hs[1 - b][:, j], rs[1 - b][:, j], ACT.Relu, bias=nmr[1][1 - b][:, j:j + 1],
                                                             scale=sc3[1 - b][:, j:j + 1])
                                m.then_inc(hs_done, 1)
                                act.wait_ge(hs_done, g)
                                settle(act, "act")
                                if edges:
                                    act.dma_start(ta[bass.ds((g - 1) * (G * P), G * P)].rearrange("(t p) d -> p t d", p=P), hs[1 - b][:]).then_inc(hs_out[1 - b], 16)
                                else:
                                    act.dma_start(ta[bass.ds((g - 1) * GN + EP, GN)].rearrange("(p j) d -> p j d", p=P), hs[1 - b][:]).then_inc(hs_out[1 - b], 16)
                        steps(act, step)

                    @block.tensor
                    def _(pe):
                        def step(g, b):
                            if real(g):
                                if edges:
                                    pe.wait_ge(oc_ready, g + 1)
                                    if later(g, 1):
                                        pe.wait_ge(oh_ready, g)
                                    for j in range(G):
                                        m = nc.tensor.transpose(ohp[:, j * P:(j + 1) * P], oc[:, j].rearrange("p t k -> p (t k)"), identb[:])
                                    m.then_inc(ohp_ready, 1)
                                    pe.wait_ge(gl_done, g + 1)
                                pe.wait_ge(oh_ready, g + 1)
                                for k in range(parts):
                                    bank = k % banks
                                    if k >= banks:
                                        pe.wait_ge(c_read, g * parts + k - banks + 1)
                                    elif later(g, 1):
                                        pe.wait_ge(c_read, g * parts)
                                    for j in range(k * CB, min(G, k * CB + CB)):
                                        at = (j % CB) * cols
                                        lhs = oh[b][:, j * P:(j + 1) * P] if edges else oh[b][:, bass.DynSlice(j, P, step=G)]
                                        if edges:
                                            nc.tensor.matmul(pc[:, bank, D:4 * D], gl[b][:, j * P:(j + 1) * P], w_a[:], start=True, stop=True)
                                        m = nc.tensor.matmul(pc[:, bank, at:at + (D if edges else CW)], lhs, tab9[:, 0:D if edges else CW], start=True, stop=True)
                                    m.then_inc(c_ready, 1)
                            if real(g - 1):
                                for k in range(pairs):
                                    if k >= 2:
                                        pe.wait_ge(g_read, (g - 1) * pairs + k - 1)
                                    elif later(g, 2):
                                        pe.wait_ge(g_read, (g - 1) * pairs)
                                    for j in range(2 * k, min(G, 2 * k + 2)):
                                        lhs = oh[1 - b][:, j * P:(j + 1) * P] if edges else oh[1 - b][:, bass.DynSlice(j, P, step=G)]
                                        m = nc.tensor.matmul(pg[:, k % 2, j % 2], lhs, tab9[:, CW:CW + GW], start=True, stop=True)
                                    m.then_inc(g_ready, 1)
                        steps(pe, step)

                    @block.vector
                    def _(dve):
                        K1 = 3 + (G * TYPES + 3 if edges else 0)
                        K2 = 5 + pairs

                        def chain(sem_, base, count, total):
                            def link(ins):
                                count[0] += 1
                                assert count[0] <= total
                                ins.then_inc(sem_, 1)
                                dve.wait_ge(sem_, base + count[0])
                            return link

                        def first_half(g, b):
                            k = [0]
                            link = chain(c1, g * K1, k, K1)
                            dve.wait_ge(loaded[b], (g - b) * (per_load // 2) + per_load)
                            if edges:
                                if later(g, 1):
                                    dve.wait_ge(ohp_ready, g)
                                hot = xr[b][:, :, C_TYPE:C_TYPE + TYPES]
                                dve.tensor_copy(oc[:], hot.rearrange("p j (t o) -> p j t o", o=1).to_broadcast([P, G, TYPES, SPLIT])).then_inc(oc_ready, 1)
                                link(dve.tensor_tensor(am[:], hot, a3[:].rearrange("p (o t) -> p o t", o=1).to_broadcast([P, G, TYPES]), ALU.mult))
                                link(dve.reduce_sum(om[:], am[:], AX.X))
                                link(dve.tensor_scalar(om[:], om[:], -1.0, 1.0, ALU.mult, ALU.add))
                            else:
                                if later(g, 2):
                                    dve.wait_ge(g_ready, (g - 1) * pairs)
                                dve.tensor_scalar(oh[b][:], t9[b][:], typ9[:], None, ALU.is_equal).then_inc(oh_ready, 1)
                            if later(g, 2):
                                dve.wait_ge(hs_done, g - 1)
                            for q in range(parts):
                                dve.wait_ge(c_ready, g * parts + q + 1)
                                for j in range(q * CB, min(G, q * CB + CB)):
                                    at = (j % CB) * cols
                                    dve.wait_ge(h_done, g * G + j + 1)
                                    keep = om[:, j:j + 1] if edges else pc[:, q % banks, at + D:at + CW]
                                    m = dve.scalar_tensor_tensor(rs[b][:, j], hb[b][:, j], keep, pc[:, q % banks, at:at + D], ALU.mult, ALU.add)
                                    if edges:
                                        for t in range(TYPES):
                                            link(m)
                                            m = dve.scalar_tensor_tensor(rs[b][:, j], pc[:, q % banks, D * (t + 1):D * (t + 2)], am[:, j, t:t + 1], rs[b][:, j], ALU.mult, ALU.add)
                                m.then_inc(c_read, 1)
                            dve.wait_ge(c_read, g * parts + parts)
                            for j in range(G):
                                m = dve.bn_stats(st[:, j], rs[b][:, j])
                            link(m)
                            aggregate(st, tmp, mean[0][b][:], var[0][b][:], link).then_inc(var2_ready, 1)

                        def slope(g, b):
                            dve.wait_ge(rstd2_ready, g + 1)
                            dve.scalar_tensor_tensor(nmr[0][b][:], mean[0][b][:], -1.0, rstd[0][b][:], ALU.mult, ALU.mult).then_inc(nm2_ready, 1)

                        def second_half(g, b):
                            k = [0]
                            link = chain(c2, g * K2, k, K2)
                            for q in range(pairs):
                                js = slice(2 * q, min(G, 2 * q + 2))
                                w = min(G, 2 * q + 2) - 2 * q
                                dve.wait_ge(g_ready, g * pairs + q + 1)
                                dve.wait_ge(y_done, g * G + min(G, 2 * q + 2))
                                link(dve.tensor_tensor(rs[b][:, js], rs[b][:, js], pg[:, q % 2, 0:w, 0:D], ALU.mult))
                                dve.tensor_tensor(rs[b][:, js], rs[b][:, js], pg[:, q % 2, 0:w, D:GW], ALU.add).then_inc(g_read, 1)
                            dve.wait_ge(g_read, g * pairs + pairs)
                            link(dve.tensor_tensor(rs[b][:], rs[b][:], xr[b][:, :, 0:D], ALU.add))
                            for j in range(G):
                                m = dve.bn_stats(st[:, j], rs[b][:, j])
                            link(m)
                            aggregate(st, tmp, mean[1][b][:], var[1][b][:], link).then_inc(var3_ready, 1)
                            if later(g, 2):
                                dve.wait_ge(ot_out[b], (g - b) * 8)
                            if edges:
                                dve.tensor_copy(ot[b][:], rs[b][:]).then_inc(ot_done, 1)
                            else:
                                dve.tensor_tensor(ot[b][:], rs[b][:], rb2_all[:].rearrange("p (o d) -> p o d", o=1).to_broadcast([P, G, D]), ALU.add).then_inc(ot_done, 1)
                            dve.wait_ge(rstd3_ready, g + 1)
                            link(dve.tensor_tensor(sc3[b][:], rstd[1][b][:], xr[b][:, :, C_SO], ALU.mult))
                            dve.scalar_tensor_tensor(nmr[1][b][:], mean[1][b][:], -1.0, sc3[b][:], ALU.mult, ALU.mult).then_inc(nm3_ready, 1)
                            assert k[0] == K2

                        def step(g, b):
                            if real(g):
                                first_half(g, b)
                                slope(g, b)
                            if real(g - 1):
                                second_half(g - 1, 1 - b)
                        steps(dve, step)
                clear()

        rows_phase(False)

        agg_ctx = ExitStack()
        agg = sb_in(agg_ctx)("agg", [P, EP], F32)

        def edge_steps(eng, body, lag, ring=U):
            head = -(-(lag + ring) // ring)
            for i in range(head):
                for u in range(ring):
                    body(i, u)
            with eng.Fori(head, ET // ring) as i:
                for u in range(ring):
                    body(i, u)
            for n in range(ET, ET + lag):
                body(n // ring, n % ring)

        def lagged(i, u, k, ring=U):
            gi, v = i + (u - k) // ring, (u - k) % ring
            n = gi * ring + v
            if isinstance(i, int):
                return gi, v, n, 0 <= n < ET, n >= ring
            return gi, v, n, True, True

        with ExitStack() as ctx:
            lb, lp = sb_in(ctx), ps_in(ctx)
            ls, clear = phase_sems()
            index = lb("index", [P, U, 2], I32)
            xs = lb("xs", [P, U, RW], F32)
            xd = lb("xd", [P, U, RW], F32)
            mask = lb("mask", [P, U, RELS], F32)
            hh = lb("hh", [P, U, 2, D], F32)
            hT = lb("hT", [P, U, 2, P], F32)
            kv = lb("kv", [P, U, 2, D], F32)
            qq = lb("qq", [P, U, D], F32)
            kvT = lb("kvT", [P, U, 2, P], F32)
            rk = lb("rk", [P, U, 2, D], F32)
            prod = lb("prod", [P, D], F32)
            attr_h = lb("attr_h", [P, HEADS], F32)
            att = lb("att", [P, U, D], F32)
            reset = lb("reset", [P, U * P], F32)
            run = lb("run", [P, 3, U * P + 1], F32)
            diff = lb("diff", [P, 2, U * P], F32)
            expd = lb("expd", [P, 2, U * P], F32)
            wm = lb("wm", [P, U * P], F32)
            den = lb("den", [P, U * P], F32)
            tpb = lp("tpb", [P, 4, P], F32)
            pj = lp("pj", [P, TYPES, 4, D], F32)
            pr = lp("pr", [P, 2, RELS, D], F32)
            attT = lp("attT", [P, U * P], F32)
            msgT = lp("msgT", [P, U * P], F32)
            idx_set = ls("idx_set")
            got = [ls(f"got{u}") for u in range(U)]
            spilled = [ls(f"spilled{u}") for u in range(U)]
            reset_in = ls("reset_in")
            masks_ready = ls("masks_ready")
            h_ready, h_seen = ls("h_ready"), ls("h_seen")
            hT_ready, proj_ready = ls("hT_ready"), ls("proj_ready")
            kv0_ready, kv1_ready, kv_ready = ls("kv0_ready"), ls("kv1_ready"), ls("kv_ready")
            kvT_seen, kvT_ready, rel_ready = ls("kvT_seen"), ls("kvT_ready"), ls("rel_ready")
            rk0_ready, rk_step, att_ready = ls("rk0_ready"), ls("rk_step"), ls("att_ready")
            attT_ready, run_set, diff_ready = ls("attT_ready"), ls("run_set"), ls("diff_ready")
            exp_ready, group_step, group_done = ls("exp_ready"), ls("group_step"), ls("group_done")
            sum_ready, sum2_step = ls("sum_ready"), ls("sum2_step")

            with nc.Block() as block:
                @block.gpsimd
                def _(pool):
                    def masks(g, v, n, again):
                        pool.wait_ge(got[v], g * 32 + 32)
                        if again:
                            pool.wait_ge(att_ready, n - U + 1)
                        settle(pool, "pool")
                        pool.tensor_copy(mask[:, v:v + 1], rel_mask[:, bass.ds(n, 1)]).then_inc(masks_ready, 1)
                        pool.tensor_copy(ats[:, bass.ds(n, 1), 0:3], xs[:, v:v + 1, C_SO:C_IDX + 1]).then_inc(masks_ready, 1)
                        pool.tensor_copy(ats[:, bass.ds(n, 1), 3:4], xd[:, v:v + 1, C_SI:C_SI + 1]).then_inc(masks_ready, 1)

                    def step(i, u):
                        g, v, n, real, again = lagged(i, u, 0)
                        if real:
                            if again:
                                pool.wait_ge(kv_ready, (n - U) * 2 + 2)
                                pool.wait_ge(masks_ready, (n - U) * 3 + 3)
                                pool.wait_ge(spilled[v], g * 16)
                                settle(pool, "pool")
                            pool.tensor_copy(index[:, v:v + 1], ends_i[:, bass.ds(n, 1)]).then_inc(idx_set, 1)
                            pool.wait_ge(idx_set, n + 1)
                            settle(pool, "pool")
                            for to, k in ((xs, 0), (xd, 1)):
                                pool.indirect_dma_start(
                                    out=to[:, v, :], out_offset=None, in_=xt,
                                    in_offset=bass.IndirectOffsetOnAxis(ap=index[:, v, k:k + 1], axis=0)).then_inc(got[v], 16)
                        g, v, n, real, again = lagged(i, u, 2)
                        if real:
                            masks(g, v, n, again)
                    edge_steps(pool, step, 2)

                @block.sync
                def _(sp):
                    def step(i, u):
                        n = i * U + u
                        if u == 0:
                            if not isinstance(i, int) or i >= 1:
                                sp.wait_ge(diff_ready, i * 2)
                            sp.dma_start(reset[:], reset_row[bass.ds(n * P, U * P)].partition_broadcast(P)).then_inc(reset_in, 16)
                        sp.wait_ge(got[u], i * 32 + 32)
                        sp.dma_start(xd_rows[bass.ds(n * P, P)], xd[:, u]).then_inc(spilled[u], 16)
                    edge_steps(sp, step, 0)
                    for u in range(U):
                        sp.wait_ge(spilled[u], 16 * EG)

                @block.scalar
                def _(act):
                    def step(i, u):
                        g, v, n, real, again = lagged(i, u, 0)
                        if real:
                            act.wait_ge(got[v], g * 32 + 32)
                            if again:
                                act.wait_ge(hT_ready, n - U + 1)
                            for k, of in ((0, xs), (1, xd)):
                                nc.scalar.activation(hh[:, v, k], of[:, v, 0:D], ACT.Relu, bias=of[:, v, C_NMR:C_NMR + 1],
                                                     scale=of[:, v, C_RSTD:C_RSTD + 1]).then_inc(h_ready, 1)
                            act.wait_ge(h_seen, n + 1)
                            if again:
                                act.wait_ge(proj_ready, n - U + 1)
                            nc.scalar.activation(hT[:, v], tpb[:, 0:2], ACT.Copy).then_inc(hT_ready, 1)
                        g, v, n, real, again = lagged(i, u, 1)
                        if real:
                            act.wait_ge(proj_ready, n + 1)
                            if again:
                                act.wait_ge(att_ready, n - U + 1)
                            nc.scalar.activation(kv[:, v], pj[:, 0, 0:2], ACT.Copy, scale=xs[:, v, C_TYPE:C_TYPE + 1]).then_inc(kv0_ready, 1)
                            nc.scalar.activation(qq[:, v], pj[:, 0, 2], ACT.Copy, scale=xd[:, v, C_TYPE:C_TYPE + 1]).then_inc(kv0_ready, 1)
                        g, v, n, real, again = lagged(i, u, 2)
                        if real:
                            act.wait_ge(kvT_seen, n + 1)
                            if again:
                                act.wait_ge(rel_ready, n - U + 1)
                            nc.scalar.activation(kvT[:, v], tpb[:, 2:4], ACT.Copy).then_inc(kvT_ready, 1)
                        g, v, n, real, again = lagged(i, u, 3)
                        if real:
                            act.wait_ge(rel_ready, n + 1)
                            act.wait_ge(masks_ready, n * 3 + 3)
                            if again:
                                act.wait_ge(attT_ready, n - U + 1)
                            nc.scalar.activation(rk[:, v], pr[:, :, 0], ACT.Copy, scale=mask[:, v, 0:1]).then_inc(rk0_ready, 1)
                        if u == 0 and (not isinstance(i, int) or i >= 2):
                            act.wait_ge(diff_ready, (i - 2) * 2 + 2)
                            if not isinstance(i, int) or i >= 3:
                                act.wait_ge(group_done, i - 2)
                            nc.scalar.activation(expd[:], diff[:], ACT.Exp).then_inc(exp_ready, 1)
                    edge_steps(act, step, 5)

                @block.tensor
                def _(pe):
                    def step(i, u):
                        g, v, n, real, again = lagged(i, u, 0)
                        if real:
                            pe.wait_ge(h_ready, n * 2 + 2)
                            if not isinstance(n, int) or n >= 1:
                                pe.wait_ge(hT_ready, n)
                            if not isinstance(n, int) or n >= 3:
                                pe.wait_ge(kvT_ready, n - 2)
                            nc.tensor.transpose(tpb[:, 0], hh[:, v, 0], ident[:])
                            nc.tensor.transpose(tpb[:, 1], hh[:, v, 1], ident[:]).then_inc(h_seen, 1)
                        g, v, n, real, again = lagged(i, u, 1)
                        if real:
                            pe.wait_ge(hT_ready, n + 1)
                            if not isinstance(n, int) or n >= 1:
                                pe.wait_ge(kv_ready, n * 2)
                            for t in range(TYPES):
                                nc.tensor.matmul(pj[:, t, 0:2], hT[:, v, 0], w_kv[:, t], start=True, stop=False)
                                nc.tensor.matmul(pj[:, t, 0:2], ones3[:], bias3[:, 2 * D * t:2 * D * (t + 1)], start=False, stop=True)
                                nc.tensor.matmul(pj[:, t, 2], hT[:, v, 1], w_q[:, t], start=True, stop=False)
                                at = 2 * D * TYPES + D * t
                                m = nc.tensor.matmul(pj[:, t, 2], ones3[:], bias3[:, at:at + D], start=False, stop=True)
                            m.then_inc(proj_ready, 1)
                        g, v, n, real, again = lagged(i, u, 2)
                        if real:
                            pe.wait_ge(kv_ready, n * 2 + 2)
                            pe.wait_ge(hT_ready, n + 3 if not isinstance(n, int) else min(n + 3, ET))
                            if not isinstance(n, int) or n >= 1:
                                pe.wait_ge(kvT_ready, n)
                            nc.tensor.transpose(tpb[:, 2], kv[:, v, 0], ident[:])
                            nc.tensor.transpose(tpb[:, 3], kv[:, v, 1], ident[:]).then_inc(kvT_seen, 1)
                        g, v, n, real, again = lagged(i, u, 3)
                        if real:
                            pe.wait_ge(kvT_ready, n + 1)
                            if not isinstance(n, int) or n >= 1:
                                pe.wait_ge(att_ready, n)
                            nc.tensor.matmul(pr[:, 0], kvT[:, v, 0], rel_k[:], start=True, stop=True)
                            nc.tensor.matmul(pr[:, 1], kvT[:, v, 1], rel_v[:], start=True, stop=True).then_inc(rel_ready, 1)
                        g, v, n, real, again = lagged(i, u, 4)
                        if real:
                            pe.wait_ge(att_ready, n + 1)
                            if v == 0 and (not isinstance(g, int) or g >= 1):
                                pe.wait_ge(group_done, g)
                            cs = slice(v * P, v * P + P)
                            nc.tensor.matmul(attT[:, cs], att[:, v], ident[:], start=True, stop=True)
                            nc.tensor.transpose(msgT[:, cs], rk[:, v, 1], ident[:]).then_inc(attT_ready, 1)
                    edge_steps(pe, step, 4)

                @block.vector
                def _(dve):
                    dve.memset(run[:], 0.0).then_inc(run_set, 1)
                    dve.wait_ge(run_set, 1)
                    C_KV, C_RK, C_GR = 2, 4, 5

                    def step(i, u):
                        g, v, n, real, again = lagged(i, u, 1)
                        if real:
                            dve.wait_ge(kv0_ready, n * 2 + 2)
                            dve.scalar_tensor_tensor(kv[:, v], pj[:, 1, 0:2], xs[:, v, C_TYPE + 1:C_TYPE + 2], kv[:, v], ALU.mult, ALU.add).then_inc(kv1_ready, 1)
                            dve.scalar_tensor_tensor(qq[:, v], pj[:, 1, 2], xd[:, v, C_TYPE + 1:C_TYPE + 2], qq[:, v], ALU.mult, ALU.add).then_inc(kv1_ready, 1)
                            dve.wait_ge(kv1_ready, n * C_KV + 2)
                            dve.scalar_tensor_tensor(kv[:, v], pj[:, 2, 0:2], xs[:, v, C_TYPE + 2:C_TYPE + 3], kv[:, v], ALU.mult, ALU.add).then_inc(kv_ready, 1)
                            dve.scalar_tensor_tensor(qq[:, v], pj[:, 2, 2], xd[:, v, C_TYPE + 2:C_TYPE + 3], qq[:, v], ALU.mult, ALU.add).then_inc(kv_ready, 1)
                        g, v, n, real, again = lagged(i, u, 3)
                        if real:
                            dve.wait_ge(rk0_ready, n + 1)
                            for r in range(1, RELS):
                                dve.scalar_tensor_tensor(rk[:, v], pr[:, :, r], mask[:, v, r:r + 1], rk[:, v], ALU.mult, ALU.add).then_inc(rk_step, 1)
                                dve.wait_ge(rk_step, n * C_RK + r)
                            dve.tensor_tensor(prod[:], rk[:, v, 0], qq[:, v], ALU.mult).then_inc(rk_step, 1)
                            if again:
                                dve.wait_ge(attT_ready, n - U + 1)
                            dve.wait_ge(rk_step, n * C_RK + 4)
                            dve.reduce_sum(attr_h[:], prod[:].rearrange("p (h f) -> p h f", h=HEADS), AX.X).then_inc(sum_ready, 1)
                            dve.wait_ge(sum_ready, n + 1)
                            dve.tensor_copy(att[:, v].rearrange("p (h f) -> p h f", h=HEADS),
                                            attr_h[:].rearrange("p (h o) -> p h o", o=1).to_broadcast([P, HEADS, DK])).then_inc(att_ready, 1)
                        if u == 3 and (not isinstance(i, int) or 1 <= i <= EG):
                            first_half(i - 1)
                        if u == 0 and (not isinstance(i, int) or 2 <= i):
                            second_half(i - 2)

                    def first_half(g):
                        s0 = g * C_GR
                        dve.tensor_copy(run[:, :, 0], run[:, :, U * P]).then_inc(group_step, 1)
                        dve.wait_ge(reset_in, g * 16 + 16)
                        dve.wait_ge(attT_ready, g * U + U)
                        dve.wait_ge(group_step, s0 + 1)
                        dve.tensor_tensor_scan(run[:, 0, 1:U * P + 1], reset[:], attT[:], run[:, 0, 0:1], ALU.add, ALU.max).then_inc(group_step, 1)
                        dve.wait_ge(group_step, s0 + 2)
                        dve.tensor_tensor(diff[:, 0], run[:, 0, 0:U * P], reset[:], ALU.add).then_inc(group_step, 1)
                        dve.tensor_tensor(diff[:, 1], attT[:], run[:, 0, 1:U * P + 1], ALU.subtract).then_inc(diff_ready, 1)
                        dve.wait_ge(group_step, s0 + 3)
                        dve.tensor_tensor(diff[:, 0], diff[:, 0], run[:, 0, 1:U * P + 1], ALU.subtract).then_inc(diff_ready, 1)

                    def second_half(g):
                        s0 = g * C_GR
                        dve.wait_ge(exp_ready, g + 1)
                        dve.tensor_tensor_scan(run[:, 2, 1:U * P + 1], expd[:, 0], expd[:, 1], run[:, 2, 0:1], ALU.mult, ALU.add).then_inc(sum2_step, 1)
                        dve.tensor_tensor(wm[:], expd[:, 1], msgT[:], ALU.mult).then_inc(group_step, 1)
                        dve.wait_ge(sum2_step, g * 3 + 1)
                        dve.tensor_scalar_add(den[:], run[:, 2, 1:U * P + 1], 1e-16).then_inc(sum2_step, 1)
                        dve.wait_ge(group_step, s0 + 4)
                        dve.tensor_tensor_scan(run[:, 1, 1:U * P + 1], expd[:, 0], wm[:], run[:, 1, 0:1], ALU.mult, ALU.add).then_inc(group_step, 1)
                        dve.wait_ge(sum2_step, g * 3 + 2)
                        dve.reciprocal(den[:], den[:]).then_inc(sum2_step, 1)
                        dve.wait_ge(sum2_step, g * 3 + 3)
                        dve.wait_ge(group_step, s0 + 5)
                        dve.tensor_tensor(agg[:, bass.ds(g * U * P, U * P)], run[:, 1, 1:U * P + 1], den[:], ALU.mult).then_inc(group_done, 1)
                    edge_steps(dve, step, 5)
            clear()
        rows_phase(True)

        agg_ctx.close()
        R = 14

        def conv_phase(second):
            name = "conv2" if second else "conv1"
            ctx = ExitStack()
            with ctx:
                def lb(n, shape, dt):
                    return ctx.enter_context(nc.sbuf_tensor(f"{name}_{n}", shape, dt))

                def lp(n, shape, dt):
                    return ctx.enter_context(nc.psum_tensor(f"{name}_{n}", shape, dt))

                ls, clear = phase_sems(name + "_")

                table, w, b_all = (t1, w_2, b2_all) if second else (ta, w_1, b1_all)
                idx = lb("idx", [P, ET], I32)
                ring = lb("ring", [P, R, 1], I32)
                oring = lb("oring", [P, R, 1], I32)
                row = lb("row", [P, R, D], F32)
                sT = lb("sT", [P, R, P], F32)
                keep = lb("keep", [P, R, P], F32)
                res = lb("res", [P, R, D], F32)
                rx = lb("rx", [P, R, D], F32)
                pT = lp("pT", [P, 2, 512], F32)
                pm = lp("pm", [P, 2, 512], F32)
                idx_ready, ring_set, scaled = ls("idx_ready"), ls("ring_set"), ls("scaled")
                got = [ls(f"got{u}") for u in range(R)]
                keep_in = [ls(f"keep_in{u}") for u in range(R)]
                stored = [ls(f"stored{u}") for u in range(R)]
                t_ready, s_ready, m_ready, v_ready, res_ready = (
                    ls("t_ready"), ls("s_ready"), ls("m_ready"), ls("v_ready"), ls("res_ready"))
                x_in = [ls(f"x_in{u}") for u in range(R)] if second else None

                with nc.Block() as block:
                    @block.gpsimd
                    def _(pool):
                        pool.wait_ge(idx_ready, 1)
                        settle(pool, "pool")

                        def step(i, u):
                            g, v, n, real, again = lagged(i, u, 0, R)
                            if real:
                                if again:
                                    pool.wait_ge(t_ready, n - R + 1)
                                    settle(pool, "pool")
                                pool.tensor_copy(ring[:, v], idx[:, bass.ds(n, 1)]).then_inc(ring_set, 1)
                                if second:
                                    if again:
                                        pool.wait_ge(stored[v], g * 16)
                                        settle(pool, "pool")
                                    pool.tensor_copy(oring[:, v], out_i[:, bass.ds(n, 1)]).then_inc(ring_set, 1)
                                pool.wait_ge(ring_set, n * (1 + second) + 1 + second)
                                settle(pool, "pool")
                                pool.indirect_dma_start(out=row[:, v, :], out_offset=None, in_=table,
                                                        in_offset=bass.IndirectOffsetOnAxis(ap=ring[:, v], axis=0)).then_inc(got[v], 16)
                            g, v, n, real, again = lagged(i, u, 8, R)
                            if second and real:
                                pool.wait_ge(res_ready, n + 1)
                                settle(pool, "pool")
                                pool.indirect_dma_start(out=out, out_offset=bass.IndirectOffsetOnAxis(ap=oring[:, v], axis=0),
                                                        in_=res[:, v, :], in_offset=None, bounds_check=N - 1,
                                                        oob_is_err=False).then_inc(stored[v], 16)
                        edge_steps(pool, step, 8 if second else 0, R)
                        if second:
                            for u in range(R):
                                pool.wait_ge(stored[u], 16 * (ET // R))

                    @block.sync
                    def _(sp):
                        def step(i, u):
                            g, v, n, real, again = lagged(i, u, 0, R)
                            if real:
                                if again:
                                    sp.wait_ge(s_ready, n - R + 1)
                                    settle(sp, "sp")
                                sp.dma_start(keep[:, v], keep_row[bass.ds(n * P, P)].partition_broadcast(P)).then_inc(keep_in[v], 16)
                                if second:
                                    if again:
                                        sp.wait_ge(res_ready, n - R + 1)
                                        settle(sp, "sp")
                                    sp.dma_start(rx[:, v], x1_rows[bass.ds(n * P, P)]).then_inc(x_in[v], 16)
                            g, v, n, real, again = lagged(i, u, 8, R)
                            if real and not second:
                                sp.wait_ge(res_ready, n + 1)
                                settle(sp, "sp")
                                sp.dma_start(t1[bass.ds(n * P, P)], res[:, v]).then_inc(stored[v], 16)
                        edge_steps(sp, step, 8, R)
                        if not second:
                            for u in range(R):
                                sp.wait_ge(stored[u], 16 * (ET // R))

                    @block.scalar
                    def _(act):
                        def step(i, u):
                            g, v, n, real, again = lagged(i, u, 0, R)
                            if second and real:
                                act.wait_ge(got[v], g * 16 + 16)
                                settle(act, "act")
                                nc.scalar.activation(row[:, v], row[:, v], ACT.Copy, scale=ats[:, bass.ds(n, 1), 0]).then_inc(scaled, 1)
                            g, v, n, real, again = lagged(i, u, 2, R)
                            if not second and real:
                                act.wait_ge(v_ready, n + 1)
                                nc.scalar.activation(res[:, v], res[:, v], ACT.Relu).then_inc(res_ready, 1)
                        edge_steps(act, step, 2, R)

                    @block.tensor
                    def _(pe):
                        def step(i, u):
                            g, v, n, real, again = lagged(i, u, 0, R)
                            if real:
                                if second:
                                    pe.wait_ge(scaled, n + 1)
                                else:
                                    pe.wait_ge(got[v], g * 16 + 16)
                                if not isinstance(n, int) or n >= 2:
                                    pe.wait_ge(s_ready, n - 1)
                                nc.tensor.transpose(pT[:, v % 2, 0:P], row[:, v], ident[:]).then_inc(t_ready, 1)
                            g, v, n, real, again = lagged(i, u, 1, R)
                            if real:
                                pe.wait_ge(s_ready, n + 1)
                                if not isinstance(n, int) or n >= 2:
                                    pe.wait_ge(v_ready, n - 1)
                                nc.tensor.matmul(pm[:, v % 2, 0:D], sT[:, v], w[:], start=True, stop=True).then_inc(m_ready, 1)
                        edge_steps(pe, step, 1, R)

                    @block.vector
                    def _(dve):
                        dve.tensor_scalar(idx[:], ats[:, :, 2], float(EP) if second else float(EP + NP), None, ALU.min).then_inc(idx_ready, 1)

                        def step(i, u):
                            g, v, n, real, again = lagged(i, u, 0, R)
                            if real:
                                dve.wait_ge(t_ready, n + 1)
                                dve.wait_ge(keep_in[v], g * 16 + 16)
                                if again:
                                    dve.wait_ge(m_ready, n - R + 1)
                                if isinstance(n, int) and n == 0:
                                    before = 0.0
                                else:
                                    dve.wait_ge(s_ready, n)
                                    before = sT[:, (v - 1) % R, P - 1:P]
                                dve.tensor_tensor_scan(sT[:, v], keep[:, v], pT[:, v % 2, 0:P], before, ALU.mult, ALU.add).then_inc(s_ready, 1)
                            g, v, n, real, again = lagged(i, u, 2, R)
                            if real:
                                dve.wait_ge(m_ready, n + 1)
                                if again:
                                    dve.wait_ge(stored[v], g * 16)
                                dve.scalar_tensor_tensor(res[:, v], pm[:, v % 2, 0:D], ats[:, bass.ds(n, 1), 3], b_all[:], ALU.mult, ALU.add).then_inc(v_ready, 1)
                                if second:
                                    dve.wait_ge(x_in[v], g * 16 + 16)
                                    dve.wait_ge(v_ready, n + 1)
                                    dve.scalar_tensor_tensor(res[:, v], res[:, v], 0.0, rx[:, v], ALU.max, ALU.add).then_inc(res_ready, 1)
                        edge_steps(dve, step, 2, R)
                clear()

        conv_phase(False)
        conv_phase(True)


_INS = ['x', 'src', 'dst', 'edge_type_4', 'node_type_3', 'L0_gnn_Wk', 'L0_gnn_bk', 'L0_gnn_Wq', 'L0_gnn_bq', 'L0_gnn_Wv',
        'L0_gnn_bv', 'L0_gnn_Wa', 'L0_gnn_ba', 'L0_gnn_rel_pri', 'L0_gnn_rel_att', 'L0_gnn_rel_msg', 'L0_gnn_skip',
        'L0_gnn_ln_g', 'L0_gnn_ln_b', 'L1_gnn_W1', 'L1_gnn_b1', 'L1_gnn_W2', 'L1_gnn_b2']
_OUTS = [((N, D), 'float32')]


def kernel(**inputs):
    import numpy as _np
    import concourse.bacc as _bacc
    from concourse import mybir as _mybir
    from concourse.bass_utils import run_bass_kernel_spmd as _run

    nc = _bacc.Bacc("TRN2", target_bir_lowering=False, num_devices=1)
    arrays, args = {}, []
    for name in _INS:
        a = _np.ascontiguousarray(inputs[name])
        arrays[f"in_{name}_dram"] = a
        args.append(nc.dram_tensor(f"in_{name}_dram", a.shape, _mybir.dt.from_np(a.dtype), kind="ExternalInput").ap())
    for i, (shape, dtype) in enumerate(_OUTS):
        dt = _mybir.dt.from_np(_np.dtype(dtype))
        args.append(nc.dram_tensor(f"out_{i}_dram", shape, dt, kind="ExternalOutput").ap())
    hgt_then_graphconv(nc, *args)
    r = _run(nc, [arrays], core_ids=[0])
    got = tuple(r.results[0][f"out_{i}_dram"] for i in range(len(_OUTS)))
    return got[0]
```

```python
from contextlib import ExitStack

import concourse.bass as bass
from concourse import mybir

F32 = mybir.dt.float32
BF16 = mybir.dt.bfloat16
FP16 = mybir.dt.float16
I32 = mybir.dt.int32
ALU = mybir.AluOpType
ACT = mybir.ActivationFunctionType
AX = mybir.AxisListType

P = 128
D = 128
N = 50000
E = 25000
TYPES = 3
RELS = 4
HEADS = 8
DK = D // HEADS
ET = -(-E // P)
EP = ET * P
HALF = ET // 2
U = 4
EG = ET // U
NT = -(-N // P)
NP = NT * P
LO = NT
NG = 17
NGROUPS = NT // NG
GN = NG * P
LASTN = N - (NGROUPS - 1) * GN
LASTFULL = LASTN // NG
LASTREST = LASTN - LASTFULL * NG
TG = 7
TGROUPS = ET // TG
RW = 136
C_RSTD, C_NMR, C_TYPE, C_SO, C_SI, C_IDX = 128, 129, 130, 133, 134, 135
SKIP = 100000
RESET = -1.0e38
EPS = 1e-5
SPLIT = 3
K9 = TYPES * SPLIT
CW = 129
GW = 256

assert ET == 2 * HALF and ET == U * EG and NT == NG * NGROUPS and ET == TG * TGROUPS


def bcast(ap, shape):
    return ap.to_broadcast(shape)


def hgt_then_graphconv(nc, x, src, dst, edge_type, node_type, Wk, bk, Wq, bq, Wv, bv, Wa, ba, rel_pri, rel_att,
                       rel_msg, skip, ln_g, ln_b, W1, b1, W2, b2, out):
    top = ExitStack()
    with top, nc.allow_non_contiguous_dma(reason="small parameter and index lists"):
        def dram(name, shape, dt):
            return nc.dram_tensor(name, shape, dt, kind="Internal").ap()

        xt = dram("xt", [NP, RW], F32)
        xd_rows = dram("xd_rows", [EP, RW], F32)
        ta = dram("ta", [EP + NP, D], F32)
        t1 = dram("t1", [EP + 1, D], F32)
        x1_rows = dram("x1_rows", [EP, D], F32)
        attr = dram("attr", [3, NP], F32)
        reset_row = dram("reset_row", [EP], F32)
        keep_row = dram("keep_row", [EP], F32)
        dst_pad = dram("dst_pad", [EP + P], I32)
        src_pad = dram("src_pad", [EP + P], I32)
        et_pad = dram("et_pad", [EP + P], I32)
        type_pad = dram("type_pad", [NP], I32)

        def sb_in(ctx):
            return lambda name, shape, dt: ctx.enter_context(nc.sbuf_tensor(name, shape, dt))

        def ps_in(ctx):
            return lambda name, shape, dt: ctx.enter_context(nc.psum_tensor(name, shape, dt))

        def sem_in(ctx):
            return lambda name: ctx.enter_context(nc.semaphore(name))

        def phase_sems(prefix=""):
            held = []

            def take(name):
                held.append(nc.alloc_semaphore(prefix + name))
                return held[-1]

            def clear():
                nc.all_engine_barrier()
                nc.clear_and_free_semaphores(held)
                nc.all_engine_barrier()
            return take, clear

        sb, sem = sb_in(top), sem_in(top)
        ident = sb("ident", [P, P], F32)
        identb = sb("identb", [P, P], BF16)
        ends_i = sb("ends_i", [P, ET, 2], I32)
        out_i = sb("out_i", [P, ET], I32)
        rel_mask = sb("rel_mask", [P, ET, RELS], F32)
        kk9 = sb("kk9", [P, K9], F32)
        typ9 = sb("typ9", [K9, 1], F32)
        a3 = sb("a3", [P, TYPES], F32)
        w_kv = sb("w_kv", [P, TYPES, 2, D], F32)
        w_q = sb("w_q", [P, TYPES, D], F32)
        w_a = sb("w_a", [P, TYPES, D], F32)
        rel_k = sb("rel_k", [P, RELS, D], F32)
        rel_v = sb("rel_v", [P, RELS, D], F32)
        w_1 = sb("w_1", [P, D], F32)
        w_2 = sb("w_2", [P, D], F32)
        b1_all = sb("b1_all", [P, D], F32)
        b2_all = sb("b2_all", [P, D], F32)
        rb2_all = sb("rb2_all", [P, D], F32)
        ones3 = sb("ones3", [SPLIT, P], BF16)
        bias3 = sb("bias3", [SPLIT, TYPES * 3 * D], BF16)
        tab9 = sb("tab9", [K9, CW + GW], BF16)
        ats = sb("ats", [P, ET, 4], F32)
        iota3 = sb("iota3", [P, 4], F32)
        count = sb("count", [1, 1], I32)

        def edge_groups(eng, body):
            body(0, True, False)
            with eng.Fori(1, EG - 1) as i:
                body(i, False, False)
            body(EG - 1, False, True)

        def aggregate(st, tmp, mean, var, link):
            nc.vector.tensor_tensor(tmp[:, 0], st[:, :, 1], st[:, :, 4], ALU.add)
            nc.vector.tensor_tensor(tmp[:, 1], st[:, :, 1], st[:, :, 4], ALU.subtract)
            link(nc.vector.tensor_tensor(tmp[:, 2], st[:, :, 2], st[:, :, 5], ALU.add))
            nc.vector.tensor_scalar(mean, tmp[:, 0], 0.5, None, ALU.mult)
            nc.vector.tensor_scalar(tmp[:, 2], tmp[:, 2], 1.0 / D, EPS, ALU.mult, ALU.add)
            link(nc.vector.scalar_tensor_tensor(tmp[:, 1], tmp[:, 1], 0.25, tmp[:, 1], ALU.mult, ALU.mult))
            return nc.vector.tensor_tensor(var, tmp[:, 1], tmp[:, 2], ALU.add)

        turn = {}

        def settle(eng, name):
            if name not in turn:
                turn[name] = sem(f"turn_{name}")
            eng.sem_inc(turn[name], 1)

        def sort_edges():
            with ExitStack() as ctx:
                lb = sb_in(ctx)
                ls, clear = phase_sems("sort_")
                col_i = lb("col_i", [P, 3, ET], I32)
                col_f = lb("col_f", [P, ET], F32)
                all_i = lb("all_i", [P, P], I32)
                all_f = lb("all_f", [P, EP], F32)
                less = lb("less", [P, EP], BF16)
                same = lb("same", [P, P], F32)
                earlier = lb("earlier", [P, P], F32)
                rank = lb("rank", [P, 3], F32)
                place = lb("place", [P, 1], I32)
                moved = lb("moved", [P, 3], I32)
                cols_in, row_in, row_set, tri, step_v, sent = (
                    ls("cols_in"), ls("row_in"), ls("row_set"), ls("tri"), ls("step_v"), ls("sent"))
                ready = ls("ready")
                K = 7
                with nc.Block() as block:
                    @block.sync
                    def _(sp):
                        sp.dma_start(all_i[:], dst_pad[1:1 + P].partition_broadcast(P)).then_inc(row_in, 16)
                        with sp.Fori(1, ET) as t:
                            sp.wait_ge(row_set, t)
                            settle(sp, "sp")
                            sp.dma_start(all_i[:], dst_pad[bass.ds(t * P + 1, P)].partition_broadcast(P)).then_inc(row_in, 16)

                    @block.scalar
                    def _(act):
                        for k, pad in enumerate((dst_pad, src_pad, et_pad)):
                            act.dma_start(col_i[:, k], pad[1:1 + EP].rearrange("(t p) -> p t", p=P)).then_inc(cols_in, 16)

                    @block.tensor
                    def _(pe):
                        pe.wait_ge(cols_in, 48)
                        pe.nop()

                    @block.gpsimd
                    def _(pool):
                        pool.memset(earlier[:], 1.0).then_inc(tri, 1)
                        pool.wait_ge(tri, 1)
                        pool.affine_select(out=earlier[:], in_=earlier[:], compare_op=ALU.is_ge, fill=0.0, base=-1,
                                           pattern=[[-1, P]], channel_multiplier=1).then_inc(tri, 1)
                        with pool.Fori(0, ET) as t:
                            pool.wait_ge(ready, t + 1)
                            settle(pool, "pool")
                            for k, pad in enumerate((dst_pad, src_pad, et_pad)):
                                pool.indirect_dma_start(out=pad.rearrange("(n o) -> n o", o=1),
                                                        out_offset=bass.IndirectOffsetOnAxis(ap=place[:], axis=0),
                                                        in_=moved[:, k:k + 1], in_offset=None).then_inc(sent, 16)
                        pool.wait_ge(sent, 48 * ET)

                    @block.vector
                    def _(dve):
                        with dve.Fori(0, ET) as t:
                            dve.wait_ge(row_in, t * 16 + 16)
                            dve.tensor_scalar(all_f[:, bass.ds(t * P, P)], all_i[:], 0.5, None, ALU.add).then_inc(row_set, 1)
                        dve.wait_ge(cols_in, 48)
                        dve.wait_ge(tri, 2)
                        dve.tensor_scalar(col_f[:], col_i[:, 0], 0.25, None, ALU.add).then_inc(row_set, 1)
                        dve.wait_ge(row_set, ET + 1)

                        def tile(t, first):
                            n = [0]

                            def link(ins):
                                n[0] += 1
                                ins.then_inc(step_v, 1)
                                dve.wait_ge(step_v, t * K + n[0])

                            d = col_f[:, bass.ds(t, 1)]
                            link(dve.tensor_scalar(less[:], all_f[:], d, 0.0, ALU.is_lt, ALU.add, accum_out=rank[:, 0:1]))
                            link(dve.tensor_scalar(rank[:, 2:3], d, 0.25, None, ALU.add))
                            link(dve.scalar_tensor_tensor(same[:], all_f[:, bass.ds(t * P, P)], rank[:, 2:3], earlier[:], ALU.is_equal, ALU.mult))
                            link(dve.reduce_sum(rank[:, 1:2], same[:], AX.X))
                            if not first:
                                dve.wait_ge(sent, t * 48)
                            link(dve.scalar_tensor_tensor(place[:], rank[:, 0:1], 1.0, rank[:, 1:2], ALU.add, ALU.add))
                            link(dve.tensor_copy(moved[:], col_i[:, :, bass.ds(t, 1)].rearrange("p k o -> p (k o)")))
                            dve.sem_inc(ready, 1)
                            link(dve.tensor_scalar(all_f[:, bass.ds(t * P, P)], all_f[:, bass.ds(t * P, P)], -0.5, None, ALU.add))
                            assert n[0] == K
                        tile(0, True)
                        with dve.Fori(1, ET) as t:
                            tile(t, False)
                clear()

        with ExitStack() as ctx:
            lb, lp = sb_in(ctx), ps_in(ctx)
            ls, clear = phase_sems("list_")
            pad_i = lb("pad_i", [1, 2, P], I32)
            pair_i = lb("pair_i", [P, 2, ET], I32)
            pair_f = lb("pair_f", [P, 2, ET], F32)
            falls = lb("falls", [P, ET], F32)
            falls_p = lb("falls_p", [P, 1], F32)
            ones = lb("ones", [P, 1], F32)
            total = lp("total", [1, 1], F32)
            padded = ls("padded")
            pads_set = ls("pads_set")
            pairs_in = ls("pairs_in")
            falls_step = ls("falls_step")
            summed = ls("summed")
            with nc.Block() as block:
                @block.sync
                def _(sp):
                    for pad, given in ((dst_pad, dst), (src_pad, src), (et_pad, edge_type)):
                        sp.dma_start(pad[1:1 + E].rearrange("(a b) -> a b", b=25),
                                     given.rearrange("(a b) -> a b", b=25)).then_inc(padded, 16)
                    sp.wait_ge(pads_set, 3)
                    for pad, k in ((dst_pad, 0), (src_pad, 0), (et_pad, 1)):
                        sp.dma_start(pad[0:1].rearrange("(o b) -> o b", o=1), pad_i[:, 1, 0:1]).then_inc(padded, 16)
                        sp.dma_start(pad[1 + E:EP + 3].rearrange("(o b) -> o b", o=1),
                                     pad_i[:, k, 0:EP + 2 - E]).then_inc(padded, 16)
                    sp.dma_start(type_pad[0:N].rearrange("(a b) -> a b", b=50),
                                 node_type.rearrange("(a b) -> a b", b=50)).then_inc(padded, 16)
                    sp.dma_start(type_pad[N:NP].rearrange("(o b) -> o b", o=1), pad_i[:, 1, 1:1 + NP - N]).then_inc(padded, 16)
                    sp.wait_ge(padded, 16 * 11)
                    for k in range(2):
                        sp.dma_start(pair_i[:, k], dst_pad[1 + k:1 + k + EP].rearrange("(p t) -> p t", p=P)).then_inc(pairs_in, 16)

                @block.gpsimd
                def _(pool):
                    pool.memset(pad_i[:, 0], N).then_inc(pads_set, 1)
                    pool.memset(pad_i[:, 1, 0:1], -1).then_inc(pads_set, 1)
                    pool.memset(pad_i[:, 1, 1:P], 0).then_inc(pads_set, 1)

                @block.vector
                def _(dve):
                    dve.memset(ones[:], 1.0).then_inc(falls_step, 1)
                    dve.wait_ge(pairs_in, 32)
                    dve.tensor_copy(pair_f[:], pair_i[:]).then_inc(falls_step, 1)
                    dve.wait_ge(falls_step, 2)
                    dve.tensor_tensor(falls[:], pair_f[:, 0], pair_f[:, 1], ALU.is_gt).then_inc(falls_step, 1)
                    dve.wait_ge(falls_step, 3)
                    dve.reduce_sum(falls_p[:], falls[:], AX.X).then_inc(falls_step, 1)
                    dve.wait_ge(summed, 1)
                    dve.tensor_copy(count[:], total[:]).then_inc(falls_step, 1)
                    dve.wait_ge(falls_step, 5)

                @block.tensor
                def _(pe):
                    pe.wait_ge(falls_step, 4)
                    nc.tensor.matmul(total[:], falls_p[:], ones[:], start=True, stop=True).then_inc(summed, 1)
            clear()
        falling = nc.values_load(count[0:1, 0:1], min_val=0, max_val=EP)
        with nc.If(falling > 0):
            sort_edges()

        with ExitStack() as ctx:
            lb, lp = sb_in(ctx), ps_in(ctx)
            ls, clear = phase_sems()
            rows = lb("rows", [HALF, 5, 2, P], I32)
            rowf = lb("rowf", [HALF, 5, 2, P], F32)
            flag = lb("flag", [HALF, 3, 2, P], F32)
            cols = lb("cols", [P, 4, ET], F32)
            hilo = lb("hilo", [P, 2, 2, ET], F32)
            hi_i = lb("hi_i", [P, 2, ET], I32)
            iota_i = lb("iota_i", [P, LO], I32)
            iota_h = lb("iota_h", [P, LO], FP16)
            kk_i = lb("kk_i", [P, K9], I32)
            row_i = lb("row_i", [K9, 1], I32)
            rowk = lb("rowk", [K9, 4], F32)
            rowk_i = lb("rowk_i", [K9, 1], I32)
            hot_hi = lb("hot_hi", [P, U, 2, P], BF16)
            hot_lo = lb("hot_lo", [P, U, 2, LO], BF16)
            deg = lb("deg", [P, 2, LO], F32)
            node_f = lb("node_f", [P, LO], F32)
            node_i = lb("node_i", [P, LO], I32)
            cum = lb("cum", [P, LO], F32)
            has = lb("has", [P, LO], F32)
            zero = lb("zero", [P, LO], F32)
            power = lb("power", [P, 2, LO], F32)
            at3 = lb("at3", [P, 3, LO], F32)
            upper = lb("upper", [P, P], F32)
            pri = lb("pri", [P, RELS], F32)
            bias_f = lb("bias_f", [SPLIT, TYPES * 3 * D], F32)
            bias_r = lb("bias_r", [SPLIT, TYPES * 3 * D], F32)
            bias_p = lb("bias_p", [SPLIT, SPLIT, TYPES * 3 * D], BF16)
            tab_f = lb("tab_f", [K9, CW + GW], F32)
            tab_r = lb("tab_r", [K9, CW + GW], F32)
            tab_p = lb("tab_p", [K9, SPLIT, CW + GW], BF16)
            sk9 = lb("sk9", [K9, 1], F32)
            t1d = lb("t1d", [1, D], F32)
            tp = [lp(f"tp{i}", [P, 4, HALF], F32) for i in range(2)]
            hist = [lp(f"hist{i}", [P, LO], F32) for i in range(2)]
            offs = lp("offs", [P, 1], F32)
            rows_in = ls("rows_in")
            weights_in = ls("weights_in")
            rel_zero = ls("rel_zero")
            pool_c = ls("pool_c")
            vec = ls("vec")
            exps = ls("exps")
            sk_in = ls("sk_in")
            rows_ready = ls("rows_ready")
            tps = ls("tps")
            hots = ls("hots")
            hists = ls("hists")
            tot_ready = ls("tot_ready")
            offs_ready = ls("offs_ready")
            powed = ls("powed")
            deg_ready = ls("deg_ready")
            flags_ready = ls("flags_ready")
            stored = ls("stored")
            with nc.Block() as block:
                @block.sync
                def _(sp):
                    for k, (pad, at) in enumerate(((dst_pad, 1), (dst_pad, 0), (dst_pad, 2), (src_pad, 1), (et_pad, 1))):
                        sp.dma_start(rows[:, k], pad[at:at + EP].rearrange("(c q r) -> q c r", c=2, q=HALF)).then_inc(rows_in, 16)
                    sp.wait_ge(flags_ready, 1)
                    sp.dma_start(reset_row.rearrange("(c q r) -> q c r", c=2, q=HALF), flag[:, 0]).then_inc(stored, 16)
                    sp.dma_start(keep_row.rearrange("(c q r) -> q c r", c=2, q=HALF), flag[:, 1]).then_inc(stored, 16)
                    sp.wait_ge(deg_ready, 1)
                    for k in range(3):
                        sp.dma_start(attr[k].rearrange("(p l) -> p l", p=P), at3[:, k]).then_inc(stored, 16)
                    sp.wait_ge(stored, 16 * 5)

                @block.scalar
                def _(act):
                    for t in range(TYPES):
                        act.dma_start(w_kv[:, t, 0], Wk[t]).then_inc(weights_in, 16)
                        act.dma_start(w_kv[:, t, 1], Wv[t]).then_inc(weights_in, 16)
                        act.dma_start(w_q[:, t], Wq[t]).then_inc(weights_in, 16)
                        act.dma_start(w_a[:, t], Wa[t]).then_inc(weights_in, 16)
                    act.dma_start(w_1[:], W1).then_inc(weights_in, 16)
                    act.dma_start(w_2[:], W2).then_inc(weights_in, 16)
                    act.dma_start(b1_all[:], b1.partition_broadcast(P)).then_inc(weights_in, 16)
                    act.dma_start(b2_all[:], b2.partition_broadcast(P)).then_inc(weights_in, 16)
                    act.dma_start(a3[:], skip.partition_broadcast(P)).then_inc(sk_in, 16)
                    for t in range(TYPES):
                        r9 = slice(SPLIT * t, SPLIT * t + SPLIT)
                        act.dma_start(sk9[r9], skip[t:t + 1].partition_broadcast(SPLIT)).then_inc(sk_in, 16)
                        act.dma_start(tab_f[r9, 0:D], ba[t].partition_broadcast(SPLIT)).then_inc(weights_in, 16)
                        act.dma_start(tab_f[r9, CW:CW + D], ln_g[t].partition_broadcast(SPLIT)).then_inc(weights_in, 16)
                        act.dma_start(tab_f[r9, CW + D:CW + GW], ln_b[t].partition_broadcast(SPLIT)).then_inc(weights_in, 16)
                        at = 2 * D * t
                        act.dma_start(bias_f[:, at:at + D], bk[t].partition_broadcast(SPLIT)).then_inc(weights_in, 16)
                        act.dma_start(bias_f[:, at + D:at + 2 * D], bv[t].partition_broadcast(SPLIT)).then_inc(weights_in, 16)
                        at = 2 * D * TYPES + D * t
                        act.dma_start(bias_f[:, at:at + D], bq[t].partition_broadcast(SPLIT)).then_inc(weights_in, 16)
                    act.wait_ge(rel_zero, 2)
                    for h in range(HEADS):
                        hs = slice(DK * h, DK * h + DK)
                        act.dma_start(rel_k[hs, :, hs], rel_att[:, h].rearrange("r d f -> d r f")).then_inc(weights_in, 16)
                        act.dma_start(rel_v[hs, :, hs], rel_msg[:, h].rearrange("r d f -> d r f")).then_inc(weights_in, 16)
                        act.dma_start(pri[hs, :], rel_pri[:, h].partition_broadcast(DK)).then_inc(weights_in, 16)
                    act.wait_ge(sk_in, 16 * 4)
                    nc.scalar.activation(a3[:], a3[:], ACT.Exp, scale=-1.0).then_inc(exps, 1)
                    nc.scalar.activation(sk9[:], sk9[:], ACT.Exp, scale=-1.0).then_inc(exps, 1)
                    act.wait_ge(tot_ready, 1)
                    nc.scalar.activation(power[:], deg[:], ACT.Sqrt).then_inc(powed, 1)

                @block.gpsimd
                def _(pool):
                    pool.memset(rel_k[:], 0.0).then_inc(rel_zero, 1)
                    pool.memset(rel_v[:], 0.0).then_inc(rel_zero, 1)
                    pool.memset(ident[:], 0.0).then_inc(pool_c, 1)
                    pool.memset(identb[:], 0.0).then_inc(pool_c, 1)
                    pool.memset(upper[:], 1.0).then_inc(pool_c, 1)
                    pool.wait_ge(pool_c, 3)
                    for m in (ident, identb):
                        pool.affine_select(out=m[:], in_=m[:], compare_op=ALU.not_equal, fill=1.0, base=0,
                                           pattern=[[-1, P]], channel_multiplier=1).then_inc(pool_c, 1)
                    pool.affine_select(out=upper[:], in_=upper[:], compare_op=ALU.is_ge, fill=0.0, base=-1,
                                       pattern=[[1, P]], channel_multiplier=-1).then_inc(pool_c, 1)
                    pool.iota(iota_i[:], [[1, LO]], base=0, channel_multiplier=0).then_inc(pool_c, 1)
                    pool.iota(kk_i[:], [[1, TYPES], [0, SPLIT]], base=0, channel_multiplier=0).then_inc(pool_c, 1)
                    pool.iota(row_i[:], [[1, 1]], base=0, channel_multiplier=1).then_inc(pool_c, 1)
                    pool.iota(node_i[:], [[1, LO]], base=EP, channel_multiplier=LO).then_inc(pool_c, 1)

                @block.vector
                def _(dve):
                    n = [0]

                    def link(ins):
                        n[0] += 1
                        ins.then_inc(vec, 1)
                        dve.wait_ge(vec, n[0])

                    dve.memset(zero[:], 0.0).then_inc(vec, 1)
                    dve.memset(ones3[:], 1.0).then_inc(vec, 1)
                    n[0] = 2
                    dve.wait_ge(pool_c, 10)
                    dve.tensor_copy(iota_h[:], iota_i[:]).then_inc(vec, 1)
                    dve.tensor_copy(iota3[:], iota_i[:, 0:4]).then_inc(vec, 1)
                    dve.tensor_copy(kk9[:], kk_i[:]).then_inc(vec, 1)
                    dve.tensor_copy(node_f[:], node_i[:]).then_inc(vec, 1)
                    n[0] += 4
                    link(dve.tensor_copy(rowk[:, 0:1], row_i[:]))
                    link(dve.tensor_scalar(rowk_i[:], rowk[:, 0:1], -1.0, 1.0 / SPLIT, ALU.add, ALU.mult))
                    link(dve.tensor_copy(typ9[:], rowk_i[:]))
                    link(dve.scalar_tensor_tensor(rowk[:, 1:2], typ9[:], -float(SPLIT), rowk[:, 0:1], ALU.mult, ALU.add))
                    dve.wait_ge(rows_in, 16 * 5)
                    link(dve.tensor_copy(rowf[:], rows[:]))
                    link(dve.tensor_tensor(flag[:, 1], rowf[:, 0], rowf[:, 1], ALU.is_equal))
                    link(dve.tensor_scalar(flag[:, 0], flag[:, 1], -RESET, RESET, ALU.mult, ALU.add))
                    link(dve.tensor_tensor(flag[:, 2], rowf[:, 0], rowf[:, 2], ALU.is_equal))
                    dve.scalar_tensor_tensor(rowf[:, 1], flag[:, 2], float(SKIP), rowf[:, 0], ALU.mult,
                                             ALU.add).then_inc(flags_ready, 1)
                    dve.wait_ge(tps, 8)
                    for c in range(2):
                        dve.tensor_copy(cols[:, :, c * HALF:(c + 1) * HALF], tp[c][:]).then_inc(vec, 1)
                    n[0] += 2
                    dve.wait_ge(vec, n[0])
                    for to, k in ((ends_i[:, :, 1], 0), (out_i[:], 1), (ends_i[:, :, 0], 2)):
                        dve.tensor_copy(to, cols[:, k]).then_inc(vec, 1)
                    dve.tensor_tensor(rel_mask[:], cols[:, 3].rearrange("p (t o) -> p t o", o=1).to_broadcast([P, ET, RELS]),
                                      iota3[:].rearrange("p (o r) -> p o r", o=1).to_broadcast([P, ET, RELS]),
                                      ALU.is_equal).then_inc(vec, 1)
                    n[0] += 4
                    for s, k in ((0, 2), (1, 0)):
                        link(dve.tensor_scalar(hi_i[:, s], cols[:, k], -(LO - 1) / 2.0, 1.0 / LO, ALU.add, ALU.mult))
                        link(dve.tensor_copy(hilo[:, s, 0], hi_i[:, s]))
                        link(dve.scalar_tensor_tensor(hilo[:, s, 1], hilo[:, s, 0], -float(LO), cols[:, k], ALU.mult, ALU.add))

                    def hot(g, first, last):
                        for u in range(U):
                            t = g * U + u
                            if not first:
                                dve.wait_ge(hists, t - U + 1)
                            for s in range(2):
                                dve.tensor_scalar(hot_hi[:, u, s], iota_h[:, 0:P], hilo[:, s, 0, bass.ds(t, 1)], None,
                                                  ALU.is_equal).then_inc(hots, 1)
                                dve.tensor_scalar(hot_lo[:, u, s], iota_h[:], hilo[:, s, 1, bass.ds(t, 1)], None,
                                                  ALU.is_equal).then_inc(hots, 1)
                    edge_groups(dve, hot)
                    dve.wait_ge(exps, 2)
                    link(dve.tensor_scalar_add(a3[:], a3[:], 1.0))
                    link(dve.reciprocal(a3[:], a3[:]))
                    link(dve.tensor_scalar_add(sk9[:], sk9[:], 1.0))
                    link(dve.reciprocal(sk9[:], sk9[:]))
                    dve.wait_ge(weights_in, 16 * (16 + 18 + 3 * HEADS))
                    link(dve.tensor_scalar(pri[:], pri[:], DK ** -0.5, None, ALU.mult))
                    for r in range(RELS):
                        link(dve.tensor_scalar(rel_k[:, r], rel_k[:, r], pri[:, r:r + 1], None, ALU.mult))
                    link(dve.tensor_scalar_max(rb2_all[:], b2_all[:], 0.0))
                    link(dve.tensor_scalar_max(t1d[:], b1_all[0:1], 0.0))
                    link(dve.tensor_scalar(tab_f[:, 0:D], tab_f[:, 0:D], sk9[:], None, ALU.mult))
                    link(dve.tensor_scalar(tab_f[:, D:CW], sk9[:], -1.0, 1.0, ALU.mult, ALU.add))
                    for f, r, p, o, part in ((bias_f, bias_r, bias_p, bias3, 0), (tab_f, tab_r, tab_p, tab9, 1)):
                        link(dve.tensor_copy(p[:, 0], f[:]))
                        link(dve.tensor_tensor(r[:], f[:], p[:, 0], ALU.subtract))
                        link(dve.tensor_copy(p[:, 1], r[:]))
                        link(dve.tensor_tensor(r[:], r[:], p[:, 1], ALU.subtract))
                        link(dve.tensor_copy(p[:, 2], r[:]))
                        rows_n = f.shape[0]
                        for k in range(SPLIT):
                            link(dve.tensor_scalar(rowk[0:rows_n, 2:3], rowk[0:rows_n, part:part + 1], float(k), None, ALU.is_equal))
                            if k == 0:
                                link(dve.tensor_scalar(o[:], p[:, k], rowk[0:rows_n, 2:3], None, ALU.mult))
                            else:
                                link(dve.scalar_tensor_tensor(o[:], p[:, k], rowk[0:rows_n, 2:3], o[:], ALU.mult, ALU.add))
                    dve.wait_ge(hists, ET)
                    for s in range(2):
                        link(dve.tensor_scalar_max(deg[:, s], hist[s][:], 1.0))
                    dve.tensor_scalar_min(has[:], hist[1][:], 1.0).then_inc(vec, 1)
                    n[0] += 1
                    link(dve.tensor_tensor_scan(cum[:], hist[1][:], zero[:], 0.0, ALU.add, ALU.add))
                    dve.sem_inc(tot_ready, 1)
                    dve.wait_ge(offs_ready, 1)
                    link(dve.tensor_scalar(cum[:], cum[:], offs[:], -1.0, ALU.add, ALU.add))
                    link(dve.tensor_tensor(cum[:], cum[:], node_f[:], ALU.subtract))
                    link(dve.tensor_tensor(cum[:], cum[:], has[:], ALU.mult))
                    link(dve.tensor_tensor(at3[:, 2], cum[:], node_f[:], ALU.add))
                    dve.wait_ge(powed, 1)
                    link(dve.reciprocal(power[:], power[:]))
                    link(dve.tensor_tensor(at3[:, 0:2], power[:], power[:], ALU.mult))
                    link(dve.tensor_tensor(at3[:, 0:2], at3[:, 0:2], deg[:], ALU.mult))
                    link(dve.tensor_scalar(at3[:, 0:2], at3[:, 0:2], -0.5, 1.5, ALU.mult, ALU.add))
                    link(dve.tensor_tensor(at3[:, 0:2], at3[:, 0:2], power[:], ALU.mult))
                    dve.sem_inc(deg_ready, 1)

                @block.tensor
                def _(pe):
                    pe.wait_ge(pool_c, 6)
                    pe.wait_ge(flags_ready, 1)
                    for c in range(2):
                        for k, at in enumerate((0, 1, 3, 4)):
                            nc.tensor.transpose(tp[c][:, k], rowf[:, at, c], ident[0:HALF, 0:HALF]).then_inc(tps, 1)

                    def product(g, first, last):
                        for u in range(U):
                            t = g * U + u
                            pe.wait_ge(hots, 4 * t + 4)
                            for s in range(2):
                                m = nc.tensor.matmul(hist[s][:], hot_hi[:, u, s], hot_lo[:, u, s],
                                                     start=first and u == 0, stop=last and u == U - 1)
                            m.then_inc(hists, 1)
                    edge_groups(pe, product)
                    pe.wait_ge(tot_ready, 1)
                    nc.tensor.matmul(offs[:], upper[:], cum[:, LO - 1:LO], start=True, stop=True).then_inc(offs_ready, 1)
            with nc.Block() as block:
                @block.sync
                def _(sp):
                    sp.dma_start(t1[EP:EP + 1], t1d[:]).then_inc(stored, 16)
                    sp.wait_ge(stored, 16 * 6)
            clear()

        def node_groups(eng, body):
            body(0, 0, True, False)
            body(1, 1, True, False)
            with eng.Fori(1, (NGROUPS - 1) // 2) as i:
                body(2 * i, 0, False, False)
                body(2 * i + 1, 1, False, False)
            body(NGROUPS - 1, 0, False, True)

        with ExitStack() as ctx:
            lb = sb_in(ctx)
            ls, clear = phase_sems()
            xr = [lb(f"xr{b}", [P, NG, RW], F32) for b in range(2)]
            ar = [lb(f"ar{b}", [P, 3, NG], F32) for b in range(2)]
            ty = [lb(f"ty{b}", [P, NG], I32) for b in range(2)]
            st = [lb(f"st{b}", [P, NG, 6], F32) for b in range(2)]
            mv = [lb(f"mv{b}", [P, NG], F32) for b in range(2)]
            ve = [lb(f"ve{b}", [P, NG], F32) for b in range(2)]
            mh = lb("mh", [P, NG], F32)
            tmp = lb("tmp", [P, 3, NG], F32)
            half_set = ls("half_set")
            loaded = [ls(f"loaded{b}") for b in range(2)]
            written = [ls(f"written{b}") for b in range(2)]
            stats = ls("stats")
            var_ready = ls("var_ready")
            rstd_ready = ls("rstd_ready")
            row_ready = ls("row_ready")
            pad_set = ls("pad_set")
            with nc.Block() as block:
                @block.sync
                def _(sp):
                    def load(g, b, first, last):
                        if not first:
                            sp.wait_ge(written[b], wr(g, b))
                        if not last:
                            sp.dma_start(xr[b][:, :, 0:D], x[bass.ds(g * GN, GN)].rearrange("(p j) d -> p j d", p=P)).then_inc(loaded[b], 16)
                            sp.dma_start(ty[b][:], node_type[bass.ds(g * GN, GN)].rearrange("(p j) -> p j", p=P)).then_inc(loaded[b], 16)
                        else:
                            sp.wait_ge(pad_set, 1)
                            n0 = g * GN
                            n1 = n0 + LASTFULL * NG
                            sp.dma_start(xr[b][0:LASTFULL, :, 0:D], x[n0:n1].rearrange("(p j) d -> p j d", j=NG)).then_inc(loaded[b], 16)
                            sp.dma_start(xr[b][LASTFULL:LASTFULL + 1, 0:LASTREST, 0:D], x[n1:N].rearrange("(p j) d -> p j d", p=1)).then_inc(loaded[b], 16)
                            sp.dma_start(ty[b][0:LASTFULL], node_type[n0:n1].rearrange("(p j) -> p j", j=NG)).then_inc(loaded[b], 16)
                            sp.dma_start(ty[b][LASTFULL:LASTFULL + 1, 0:LASTREST], node_type[n1:N].rearrange("(p j) -> p j", p=1)).then_inc(loaded[b], 16)
                        sp.dma_start(ar[b][:], attr[:, bass.ds(g * GN, GN)].rearrange("k (p j) -> p k j", p=P)).then_inc(loaded[b], 16)

                    def wr(g, b):
                        return (g - b) * 8

                    node_groups(sp, load)

                @block.scalar
                def _(act):
                    def write(g, b, first, last):
                        act.wait_ge(row_ready, g + 1)
                        act.dma_start(xt[bass.ds(g * GN, GN)].rearrange("(p j) w -> p j w", p=P), xr[b][:]).then_inc(written[b], 16)
                    node_groups(act, write)
                    act.wait_ge(written[0], 16 * (NGROUPS // 2 + 1))
                    act.wait_ge(written[1], 16 * (NGROUPS // 2))

                @block.gpsimd
                def _(pool):
                    pool.memset(mh[:], -0.5).then_inc(half_set, 1)
                    pool.wait_ge(half_set, 1)

                    def rstd(g, b, first, last):
                        pool.wait_ge(var_ready, g + 1)
                        settle(pool, "pool")
                        pool.tensor_tensor(xr[b][:, :, C_RSTD], ve[b][:], mh[:], ALU.pow).then_inc(rstd_ready, 1)
                    node_groups(pool, rstd)

                @block.vector
                def _(dve):
                    def norm(g, b, first, last):
                        if last:
                            dve.wait_ge(written[b], 16 * (g // 2))
                            dve.memset(xr[b][:], 0.0).then_inc(stats, 1)
                            dve.memset(ty[b][:], 0).then_inc(stats, 1)
                            dve.wait_ge(stats, 6 * g + 2)
                            dve.sem_inc(pad_set, 1)
                        s0 = g * 6 + (2 if last else 0)
                        dve.wait_ge(loaded[b], (g - b) * 24 + (16 * 5 if last else 48))
                        for j in range(NG):
                            i = dve.bn_stats(st[b][:, j], xr[b][:, j, 0:D])
                        i.then_inc(stats, 1)
                        dve.wait_ge(stats, s0 + 1)

                        k = [s0 + 1]

                        def link(ins):
                            k[0] += 1
                            ins.then_inc(stats, 1)
                            dve.wait_ge(stats, k[0])
                        aggregate(st[b], tmp, mv[b][:], ve[b][:], link).then_inc(var_ready, 1)
                        dve.tensor_tensor(xr[b][:, :, C_TYPE:C_TYPE + TYPES],
                                          ty[b][:].rearrange("p (j o) -> p j o", o=1).to_broadcast([P, NG, TYPES]),
                                          iota3[:, 0:TYPES].rearrange("p (o t) -> p o t", o=1).to_broadcast([P, NG, TYPES]),
                                          ALU.is_equal).then_inc(stats, 1)
                        dve.tensor_copy(xr[b][:, :, C_SO:C_IDX + 1].rearrange("p j k -> p k j"), ar[b][:]).then_inc(stats, 1)
                        dve.wait_ge(rstd_ready, g + 1)
                        dve.scalar_tensor_tensor(xr[b][:, :, C_NMR], mv[b][:], -1.0, xr[b][:, :, C_RSTD], ALU.mult,
                                                 ALU.mult).then_inc(stats, 1)
                        dve.wait_ge(stats, s0 + 6)
                        dve.sem_inc(row_ready, 1)
                    node_groups(dve, norm)
            clear()

        def rows_phase(edges):
            G, groups = (TG, TGROUPS) if edges else (NG, NGROUPS)
            name = "edge" if edges else "node"
            CB = 1 if edges else 3
            banks = 4 if edges else 6
            cols = 4 * D if edges else CW
            parts = -(-G // CB)
            pairs = -(-G // 2)
            ctx = ExitStack()
            with ctx:
                def lb(n, shape, dt):
                    return ctx.enter_context(nc.sbuf_tensor(f"{name}_{n}", shape, dt))

                def lp(n, shape, dt):
                    return ctx.enter_context(nc.psum_tensor(f"{name}_{n}", shape, dt))

                ls, clear = phase_sems(name + "_")

                three = range(3)
                xr = [lb(f"xr{b}", [P, G, RW], F32) for b in three]
                hb = [lb(f"hb{b}", [P, G, D], F32) for b in three]
                rs = [lb(f"rs{b}", [P, G, D], F32) for b in three]
                hs = [lb(f"hs{b}", [P, G, D], F32) for b in three]
                ot = [lb(f"ot{b}", [P, G, D], F32) for b in three]
                oh = [lb(f"oh{b}", [K9, G * P], BF16) for b in three]
                st = lb("st", [P, G, 6], F32)
                tmp = lb("tmp", [P, 3, G], F32)
                mean = [[lb(f"mean{k}{b}", [P, G], F32) for b in three] for k in range(2)]
                var = [[lb(f"var{k}{b}", [P, G], F32) for b in three] for k in range(2)]
                rstd = [[lb(f"rstd{k}{b}", [P, G], F32) for b in three] for k in range(2)]
                nmr = [[lb(f"nmr{k}{b}", [P, G], F32) for b in three] for k in range(2)]
                sc3 = [lb(f"sc3{b}", [P, G], F32) for b in three]
                mh = lb("mh", [P, G], F32)
                if edges:
                    gl = [lb(f"gl{b}", [P, G * P], F32) for b in three]
                    oc = lb("oc", [P, G, TYPES, SPLIT], BF16)
                    am = lb("am", [P, G, TYPES], F32)
                    om = lb("om", [P, G], F32)
                    ohp = lp("ohp", [K9, G * P], BF16)
                else:
                    t9 = [lb(f"t9{b}", [K9, G * P], I32) for b in three]
                pc = lp("pc", [P, banks, 512], F32)
                pg = lp("pg", [P, 2, 2, GW], F32)
                loaded = [ls(f"loaded{b}") for b in three]
                half_set, gl_done, h_done, oc_ready, ohp_ready, oh_ready = (
                    ls("half_set"), ls("gl_done"), ls("h_done"), ls("oc_ready"), ls("ohp_ready"), ls("oh_ready"))
                c_ready, c_read, c1, c2 = ls("c_ready"), ls("c_read"), ls("c1"), ls("c2")
                var2_ready, rstd2_ready, nm2_ready, y_done = ls("var2"), ls("rstd2"), ls("nm2"), ls("y_done")
                g_ready, g_read = ls("g_ready"), ls("g_read")
                var3_ready, rstd3_ready, nm3_ready, hs_done, ot_done = (
                    ls("var3"), ls("rstd3"), ls("nm3"), ls("hs_done"), ls("ot_done"))
                hs_out = [ls(f"hs_out{b}") for b in three]
                ot_out = [ls(f"ot_out{b}") for b in three]
                per_load = 16 if edges else 32

                def steps(eng, body):
                    for i in range(2):
                        for b in three:
                            body(i, b)
                    with eng.Fori(2, (groups - 1) // 3) as i:
                        for b in three:
                            body(i, b)
                    for g in range((groups - 1) // 3 * 3, groups + 1):
                        body(g // 3, g % 3)

                def real(g):
                    return not isinstance(g, int) or 0 <= g < groups

                def later(g, k):
                    return not isinstance(g, int) or g >= k

                with nc.Block() as block:
                    @block.sync
                    def _(sp):
                        def load(g, b):
                            if later(g, 3):
                                sp.wait_ge(nm3_ready, g - 2)
                                settle(sp, "sp")
                                sp.wait_ge(h_done, (g - 2) * G)
                                settle(sp, "sp")
                            if edges:
                                sp.dma_start(xr[b][:], xd_rows[bass.ds(g * (G * P), G * P)].rearrange("(t p) w -> p t w", p=P)).then_inc(loaded[b], 16)
                            else:
                                sp.dma_start(xr[b][:], xt[bass.ds(g * GN, GN)].rearrange("(p j) w -> p j w", p=P)).then_inc(loaded[b], 16)
                                if later(g, 3):
                                    sp.wait_ge(oh_ready, g - 2)
                                    settle(sp, "sp")
                                sp.dma_start(t9[b][:], type_pad[bass.ds(g * GN, GN)].partition_broadcast(K9)).then_inc(loaded[b], 16)

                        def step(i, b):
                            g = i * 3 + b
                            p = (b - 1) % 3
                            ip = i - (b == 0)
                            if isinstance(g, int) and g == 0:
                                load(0, 0)
                            if real(g + 1):
                                load(g + 1, (b + 1) % 3)
                            if real(g - 1):
                                sp.wait_ge(ot_done, g)
                                settle(sp, "sp")
                                if edges:
                                    sp.dma_start(x1_rows[bass.ds((g - 1) * (G * P), G * P)].rearrange("(t p) w -> p t w", p=P), ot[p][:]).then_inc(ot_out[p], 16)
                                elif isinstance(g, int) and g == groups:
                                    n0 = (g - 1) * GN
                                    n1 = n0 + LASTFULL * NG
                                    sp.dma_start(out[n0:n1].rearrange("(p j) d -> p j d", j=NG), ot[p][0:LASTFULL]).then_inc(ot_out[p], 16)
                                    sp.dma_start(out[n1:N].rearrange("(p j) d -> p j d", p=1), ot[p][LASTFULL:LASTFULL + 1, 0:LASTREST]).then_inc(ot_out[p], 16)
                                else:
                                    sp.dma_start(out[bass.ds((g - 1) * GN, GN)].rearrange("(p j) d -> p j d", p=P), ot[p][:]).then_inc(ot_out[p], 16)
                        steps(sp, step)
                        for b in three:
                            n = (groups - b + 2) // 3
                            sp.wait_ge(hs_out[b], 16 * n)
                            sp.wait_ge(ot_out[b], 16 * (n + (not edges and (groups - 1) % 3 == b)))

                    @block.gpsimd
                    def _(pool):
                        pool.memset(mh[:], -0.5).then_inc(half_set, 1)
                        pool.wait_ge(half_set, 1)

                        def step(i, b):
                            g = i * 3 + b
                            p = (b - 1) % 3
                            ip = i - (b == 0)
                            if real(g):
                                pool.wait_ge(var2_ready, g + 1)
                                settle(pool, "pool")
                                pool.tensor_tensor(rstd[0][b][:], var[0][b][:], mh[:], ALU.pow).then_inc(rstd2_ready, 1)
                            if real(g - 1):
                                pool.wait_ge(var3_ready, g)
                                settle(pool, "pool")
                                pool.tensor_tensor(rstd[1][p][:], var[1][p][:], mh[:], ALU.pow).then_inc(rstd3_ready, 1)
                        steps(pool, step)

                    @block.scalar
                    def _(act):
                        def clipped(i, g, b):
                            act.wait_ge(loaded[b], i * per_load + per_load)
                            if later(g, 3):
                                act.wait_ge(c_read, (g - 2) * parts)
                            for j in range(G):
                                nc.scalar.activation(hb[b][:, j], xr[b][:, j, 0:D], ACT.Relu, bias=xr[b][:, j, C_NMR:C_NMR + 1],
                                                     scale=xr[b][:, j, C_RSTD:C_RSTD + 1]).then_inc(h_done, 1)
                            if edges:
                                settle(act, "act")
                                nc.scalar.activation(gl[b][:], agg[:, bass.ds(g * (G * P), G * P)], ACT.Gelu).then_inc(gl_done, 1)

                        def step(i, b):
                            g = i * 3 + b
                            p = (b - 1) % 3
                            ip = i - (b == 0)
                            if isinstance(g, int) and g == 0:
                                clipped(0, 0, 0)
                            if edges and real(g):
                                act.wait_ge(ohp_ready, g + 1)
                                if later(g, 3):
                                    act.wait_ge(g_ready, (g - 2) * pairs)
                                nc.scalar.activation(oh[b][:], ohp[:], ACT.Copy).then_inc(oh_ready, 1)
                            if real(g + 1):
                                clipped(i + (b == 2), g + 1, (b + 1) % 3)
                            if real(g):
                                act.wait_ge(nm2_ready, g + 1)
                                for j in range(G):
                                    nc.scalar.activation(rs[b][:, j], rs[b][:, j], ACT.Identity, bias=nmr[0][b][:, j:j + 1],
                                                         scale=rstd[0][b][:, j:j + 1]).then_inc(y_done, 1)
                            if real(g - 1):
                                act.wait_ge(nm3_ready, g)
                                if later(g, 4):
                                    act.wait_ge(hs_out[p], ip * 16)
                                for j in range(G):
                                    m = nc.scalar.activation(hs[p][:, j], rs[p][:, j], ACT.Relu, bias=nmr[1][p][:, j:j + 1],
                                                             scale=sc3[p][:, j:j + 1])
                                m.then_inc(hs_done, 1)
                                act.wait_ge(hs_done, g)
                                settle(act, "act")
                                if edges:
                                    act.dma_start(ta[bass.ds((g - 1) * (G * P), G * P)].rearrange("(t p) d -> p t d", p=P), hs[p][:]).then_inc(hs_out[p], 16)
                                else:
                                    act.dma_start(ta[bass.ds((g - 1) * GN + EP, GN)].rearrange("(p j) d -> p j d", p=P), hs[p][:]).then_inc(hs_out[p], 16)
                        steps(act, step)

                    @block.tensor
                    def _(pe):
                        def step(i, b):
                            g = i * 3 + b
                            p = (b - 1) % 3
                            ip = i - (b == 0)
                            if real(g):
                                if edges:
                                    pe.wait_ge(oc_ready, g + 1)
                                    if later(g, 1):
                                        pe.wait_ge(oh_ready, g)
                                    for j in range(G):
                                        m = nc.tensor.transpose(ohp[:, j * P:(j + 1) * P], oc[:, j].rearrange("p t k -> p (t k)"), identb[:])
                                    m.then_inc(ohp_ready, 1)
                                    pe.wait_ge(gl_done, g + 1)
                                pe.wait_ge(oh_ready, g + 1)
                                for k in range(parts):
                                    bank = k % banks
                                    if k >= banks:
                                        pe.wait_ge(c_read, g * parts + k - banks + 1)
                                    elif later(g, 1):
                                        pe.wait_ge(c_read, g * parts)
                                    for j in range(k * CB, min(G, k * CB + CB)):
                                        at = (j % CB) * cols
                                        lhs = oh[b][:, j * P:(j + 1) * P] if edges else oh[b][:, bass.DynSlice(j, P, step=G)]
                                        if edges:
                                            nc.tensor.matmul(pc[:, bank, D:4 * D], gl[b][:, j * P:(j + 1) * P], w_a[:], start=True, stop=True)
                                        m = nc.tensor.matmul(pc[:, bank, at:at + (D if edges else CW)], lhs, tab9[:, 0:D if edges else CW], start=True, stop=True)
                                    m.then_inc(c_ready, 1)
                            if real(g - 1):
                                for k in range(pairs):
                                    if k >= 2:
                                        pe.wait_ge(g_read, (g - 1) * pairs + k - 1)
                                    elif later(g, 2):
                                        pe.wait_ge(g_read, (g - 1) * pairs)
                                    for j in range(2 * k, min(G, 2 * k + 2)):
                                        lhs = oh[p][:, j * P:(j + 1) * P] if edges else oh[p][:, bass.DynSlice(j, P, step=G)]
                                        m = nc.tensor.matmul(pg[:, k % 2, j % 2], lhs, tab9[:, CW:CW + GW], start=True, stop=True)
                                    m.then_inc(g_ready, 1)
                        steps(pe, step)

                    @block.vector
                    def _(dve):
                        K1 = 3 + (G * TYPES + 3 if edges else 0)
                        K2 = 5 + pairs

                        def chain(sem_, base, count, total):
                            def link(ins):
                                count[0] += 1
                                assert count[0] <= total
                                ins.then_inc(sem_, 1)
                                dve.wait_ge(sem_, base + count[0])
                            return link

                        def first_half(i, g, b):
                            k = [0]
                            link = chain(c1, g * K1, k, K1)
                            dve.wait_ge(loaded[b], i * per_load + per_load)
                            if edges:
                                if later(g, 1):
                                    dve.wait_ge(ohp_ready, g)
                                hot = xr[b][:, :, C_TYPE:C_TYPE + TYPES]
                                dve.tensor_copy(oc[:], hot.rearrange("p j (t o) -> p j t o", o=1).to_broadcast([P, G, TYPES, SPLIT])).then_inc(oc_ready, 1)
                                link(dve.tensor_tensor(am[:], hot, a3[:].rearrange("p (o t) -> p o t", o=1).to_broadcast([P, G, TYPES]), ALU.mult))
                                link(dve.reduce_sum(om[:], am[:], AX.X))
                                link(dve.tensor_scalar(om[:], om[:], -1.0, 1.0, ALU.mult, ALU.add))
                            else:
                                if later(g, 3):
                                    dve.wait_ge(g_ready, (g - 2) * pairs)
                                dve.tensor_scalar(oh[b][:], t9[b][:], typ9[:], None, ALU.is_equal).then_inc(oh_ready, 1)
                            if later(g, 3):
                                dve.wait_ge(hs_done, g - 2)
                            for q in range(parts):
                                dve.wait_ge(c_ready, g * parts + q + 1)
                                for j in range(q * CB, min(G, q * CB + CB)):
                                    at = (j % CB) * cols
                                    dve.wait_ge(h_done, g * G + j + 1)
                                    keep = om[:, j:j + 1] if edges else pc[:, q % banks, at + D:at + CW]
                                    m = dve.scalar_tensor_tensor(rs[b][:, j], hb[b][:, j], keep, pc[:, q % banks, at:at + D], ALU.mult, ALU.add)
                                    if edges:
                                        for t in range(TYPES):
                                            link(m)
                                            m = dve.scalar_tensor_tensor(rs[b][:, j], pc[:, q % banks, D * (t + 1):D * (t + 2)], am[:, j, t:t + 1], rs[b][:, j], ALU.mult, ALU.add)
                                m.then_inc(c_read, 1)
                            dve.wait_ge(c_read, g * parts + parts)
                            for j in range(G):
                                m = dve.bn_stats(st[:, j], rs[b][:, j])
                            link(m)
                            aggregate(st, tmp, mean[0][b][:], var[0][b][:], link).then_inc(var2_ready, 1)

                        def slope(g, b):
                            dve.wait_ge(rstd2_ready, g + 1)
                            dve.scalar_tensor_tensor(nmr[0][b][:], mean[0][b][:], -1.0, rstd[0][b][:], ALU.mult, ALU.mult).then_inc(nm2_ready, 1)

                        def second_half(i, g, b, between):
                            k = [0]
                            link = chain(c2, g * K2, k, K2)
                            for q in range(pairs):
                                js = slice(2 * q, min(G, 2 * q + 2))
                                w = min(G, 2 * q + 2) - 2 * q
                                dve.wait_ge(g_ready, g * pairs + q + 1)
                                dve.wait_ge(y_done, g * G + min(G, 2 * q + 2))
                                link(dve.tensor_tensor(rs[b][:, js], rs[b][:, js], pg[:, q % 2, 0:w, 0:D], ALU.mult))
                                dve.tensor_tensor(rs[b][:, js], rs[b][:, js], pg[:, q % 2, 0:w, D:GW], ALU.add).then_inc(g_read, 1)
                            dve.wait_ge(g_read, g * pairs + pairs)
                            between()
                            link(dve.tensor_tensor(rs[b][:], rs[b][:], xr[b][:, :, 0:D], ALU.add))
                            for j in range(G):
                                m = dve.bn_stats(st[:, j], rs[b][:, j])
                            link(m)
                            aggregate(st, tmp, mean[1][b][:], var[1][b][:], link).then_inc(var3_ready, 1)
                            if later(g, 3):
                                dve.wait_ge(ot_out[b], i * 16)
                            if edges:
                                dve.tensor_copy(ot[b][:], rs[b][:]).then_inc(ot_done, 1)
                            else:
                                dve.tensor_tensor(ot[b][:], rs[b][:], rb2_all[:].rearrange("p (o d) -> p o d", o=1).to_broadcast([P, G, D]), ALU.add).then_inc(ot_done, 1)
                            dve.wait_ge(rstd3_ready, g + 1)
                            link(dve.tensor_tensor(sc3[b][:], rstd[1][b][:], xr[b][:, :, C_SO], ALU.mult))
                            dve.scalar_tensor_tensor(nmr[1][b][:], mean[1][b][:], -1.0, sc3[b][:], ALU.mult, ALU.mult).then_inc(nm3_ready, 1)
                            assert k[0] == K2

                        def step(i, b):
                            g = i * 3 + b
                            p = (b - 1) % 3
                            ip = i - (b == 0)
                            if real(g):
                                first_half(i, g, b)
                            if real(g - 1):
                                second_half(ip, g - 1, p, (lambda: slope(g, b)) if real(g) else (lambda: None))
                            elif real(g):
                                slope(g, b)
                        steps(dve, step)
                clear()

        rows_phase(False)

        agg_ctx = ExitStack()
        agg = sb_in(agg_ctx)("agg", [P, EP], F32)

        def edge_steps(eng, body, lag, ring=U):
            head = -(-(lag + ring) // ring)
            for i in range(head):
                for u in range(ring):
                    body(i, u)
            with eng.Fori(head, ET // ring) as i:
                for u in range(ring):
                    body(i, u)
            for n in range(ET, ET + lag):
                body(n // ring, n % ring)

        def lagged(i, u, k, ring=U):
            gi, v = i + (u - k) // ring, (u - k) % ring
            n = gi * ring + v
            if isinstance(i, int):
                return gi, v, n, 0 <= n < ET, n >= ring
            return gi, v, n, True, True

        with ExitStack() as ctx:
            lb, lp = sb_in(ctx), ps_in(ctx)
            ls, clear = phase_sems()
            index = lb("index", [P, U, 2], I32)
            xs = lb("xs", [P, U, RW], F32)
            xd = lb("xd", [P, U, RW], F32)
            mask = lb("mask", [P, U, RELS], F32)
            hh = lb("hh", [P, U, 2, D], F32)
            hT = lb("hT", [P, U, 2, P], F32)
            kv = lb("kv", [P, U, 2, D], F32)
            qq = lb("qq", [P, U, D], F32)
            kvT = lb("kvT", [P, U, 2, P], F32)
            rk = lb("rk", [P, U, 2, D], F32)
            prod = lb("prod", [P, D], F32)
            attr_h = lb("attr_h", [P, HEADS], F32)
            att = lb("att", [P, U, D], F32)
            reset = lb("reset", [P, U * P], F32)
            run = lb("run", [P, 3, U * P + 1], F32)
            diff = lb("diff", [P, 2, U * P], F32)
            expd = lb("expd", [P, 2, U * P], F32)
            wm = lb("wm", [P, U * P], F32)
            den = lb("den", [P, U * P], F32)
            tpb = lp("tpb", [P, 4, P], F32)
            pj = lp("pj", [P, TYPES, 4, D], F32)
            pr = lp("pr", [P, 2, RELS, D], F32)
            attT = lp("attT", [P, U * P], F32)
            msgT = lp("msgT", [P, U * P], F32)
            idx_set = ls("idx_set")
            got = [ls(f"got{u}") for u in range(U)]
            spilled = [ls(f"spilled{u}") for u in range(U)]
            reset_in = ls("reset_in")
            masks_ready = ls("masks_ready")
            h_ready, h_seen = ls("h_ready"), ls("h_seen")
            hT_ready, proj_ready = ls("hT_ready"), ls("proj_ready")
            kv0_ready, kv1_ready, kv_ready = ls("kv0_ready"), ls("kv1_ready"), ls("kv_ready")
            kvT_seen, kvT_ready, rel_ready = ls("kvT_seen"), ls("kvT_ready"), ls("rel_ready")
            rk0_ready, rk_step, att_ready = ls("rk0_ready"), ls("rk_step"), ls("att_ready")
            attT_ready, run_set, diff_ready = ls("attT_ready"), ls("run_set"), ls("diff_ready")
            exp_ready, group_step, group_done = ls("exp_ready"), ls("group_step"), ls("group_done")
            sum_ready, sum2_step = ls("sum_ready"), ls("sum2_step")

            with nc.Block() as block:
                @block.gpsimd
                def _(pool):
                    def masks(g, v, n, again):
                        pool.wait_ge(got[v], g * 32 + 32)
                        if again:
                            pool.wait_ge(att_ready, n - U + 1)
                        settle(pool, "pool")
                        pool.tensor_copy(mask[:, v:v + 1], rel_mask[:, bass.ds(n, 1)]).then_inc(masks_ready, 1)
                        pool.tensor_copy(ats[:, bass.ds(n, 1), 0:3], xs[:, v:v + 1, C_SO:C_IDX + 1]).then_inc(masks_ready, 1)
                        pool.tensor_copy(ats[:, bass.ds(n, 1), 3:4], xd[:, v:v + 1, C_SI:C_SI + 1]).then_inc(masks_ready, 1)

                    def step(i, u):
                        g, v, n, real, again = lagged(i, u, 0)
                        if real:
                            if again:
                                pool.wait_ge(kv_ready, (n - U) * 2 + 2)
                                pool.wait_ge(masks_ready, (n - U) * 3 + 3)
                                pool.wait_ge(spilled[v], g * 16)
                                settle(pool, "pool")
                            pool.tensor_copy(index[:, v:v + 1], ends_i[:, bass.ds(n, 1)]).then_inc(idx_set, 1)
                            pool.wait_ge(idx_set, n + 1)
                            settle(pool, "pool")
                            for to, k in ((xs, 0), (xd, 1)):
                                pool.indirect_dma_start(
                                    out=to[:, v, :], out_offset=None, in_=xt,
                                    in_offset=bass.IndirectOffsetOnAxis(ap=index[:, v, k:k + 1], axis=0)).then_inc(got[v], 16)
                        g, v, n, real, again = lagged(i, u, 2)
                        if real:
                            masks(g, v, n, again)
                    edge_steps(pool, step, 2)

                @block.sync
                def _(sp):
                    def step(i, u):
                        n = i * U + u
                        sp.wait_ge(got[u], i * 32 + 32)
                        sp.dma_start(xd_rows[bass.ds(n * P, P)], xd[:, u]).then_inc(spilled[u], 16)
                    sp.dma_start(reset[:], reset_row[0:U * P].partition_broadcast(P)).then_inc(reset_in, 16)
                    edge_steps(sp, step, 0)
                    for u in range(U):
                        sp.wait_ge(spilled[u], 16 * EG)

                @block.scalar
                def _(act):
                    def clipped(g, v, n, again):
                        act.wait_ge(got[v], g * 32 + 32)
                        if again:
                            act.wait_ge(hT_ready, n - U + 1)
                        for k, of in ((0, xs), (1, xd)):
                            nc.scalar.activation(hh[:, v, k], of[:, v, 0:D], ACT.Relu, bias=of[:, v, C_NMR:C_NMR + 1],
                                                 scale=of[:, v, C_RSTD:C_RSTD + 1]).then_inc(h_ready, 1)

                    def step(i, u):
                        g, v, n, real, again = lagged(i, u, 1)
                        if real:
                            act.wait_ge(h_seen, n + 1)
                            if again:
                                act.wait_ge(proj_ready, n - U + 1)
                            nc.scalar.activation(hT[:, v], tpb[:, 0:2], ACT.Copy).then_inc(hT_ready, 1)
                        g, v, n, real, again = lagged(i, u, 0)
                        if real:
                            clipped(g, v, n, again)
                        g, v, n, real, again = lagged(i, u, 2)
                        if real:
                            act.wait_ge(proj_ready, n + 1)
                            if again:
                                act.wait_ge(att_ready, n - U + 1)
                            nc.scalar.activation(kv[:, v], pj[:, 0, 0:2], ACT.Copy, scale=xs[:, v, C_TYPE:C_TYPE + 1]).then_inc(kv0_ready, 1)
                            nc.scalar.activation(qq[:, v], pj[:, 0, 2], ACT.Copy, scale=xd[:, v, C_TYPE:C_TYPE + 1]).then_inc(kv0_ready, 1)
                        g, v, n, real, again = lagged(i, u, 3)
                        if real:
                            act.wait_ge(kvT_seen, n + 1)
                            if again:
                                act.wait_ge(rel_ready, n - U + 1)
                            nc.scalar.activation(kvT[:, v], tpb[:, 2:4], ACT.Copy).then_inc(kvT_ready, 1)
                        g, v, n, real, again = lagged(i, u, 4)
                        if real:
                            act.wait_ge(rel_ready, n + 1)
                            act.wait_ge(masks_ready, n * 3 + 3)
                            if again:
                                act.wait_ge(attT_ready, n - U + 1)
                            nc.scalar.activation(rk[:, v], pr[:, :, 0], ACT.Copy, scale=mask[:, v, 0:1]).then_inc(rk0_ready, 1)
                        if u == 1 and (not isinstance(i, int) or i >= 2):
                            act.wait_ge(diff_ready, (i - 2) * 2 + 2)
                            if not isinstance(i, int) or i >= 3:
                                act.wait_ge(group_done, i - 2)
                            nc.scalar.activation(expd[:], diff[:], ACT.Exp).then_inc(exp_ready, 1)
                            if not isinstance(i, int) or i <= EG:
                                act.dma_start(reset[:], reset_row[bass.ds((i - 1) * (U * P), U * P)].partition_broadcast(P)).then_inc(reset_in, 16)
                    edge_steps(act, step, 6)

                @block.tensor
                def _(pe):
                    def step(i, u):
                        g, v, n, real, again = lagged(i, u, 0)
                        if real:
                            pe.wait_ge(h_ready, n * 2 + 2)
                            if not isinstance(n, int) or n >= 1:
                                pe.wait_ge(hT_ready, n)
                            if not isinstance(n, int) or n >= 3:
                                pe.wait_ge(kvT_ready, n - 2)
                            nc.tensor.transpose(tpb[:, 0], hh[:, v, 0], ident[:])
                            nc.tensor.transpose(tpb[:, 1], hh[:, v, 1], ident[:]).then_inc(h_seen, 1)
                        g, v, n, real, again = lagged(i, u, 1)
                        if real:
                            pe.wait_ge(hT_ready, n + 1)
                            if not isinstance(n, int) or n >= 1:
                                pe.wait_ge(kv_ready, n * 2)
                            for t in range(TYPES):
                                nc.tensor.matmul(pj[:, t, 0:2], hT[:, v, 0], w_kv[:, t], start=True, stop=False)
                                nc.tensor.matmul(pj[:, t, 0:2], ones3[:], bias3[:, 2 * D * t:2 * D * (t + 1)], start=False, stop=True)
                                nc.tensor.matmul(pj[:, t, 2], hT[:, v, 1], w_q[:, t], start=True, stop=False)
                                at = 2 * D * TYPES + D * t
                                m = nc.tensor.matmul(pj[:, t, 2], ones3[:], bias3[:, at:at + D], start=False, stop=True)
                            m.then_inc(proj_ready, 1)
                        g, v, n, real, again = lagged(i, u, 2)
                        if real:
                            pe.wait_ge(kv_ready, n * 2 + 2)
                            pe.wait_ge(hT_ready, n + 3 if not isinstance(n, int) else min(n + 3, ET))
                            if not isinstance(n, int) or n >= 1:
                                pe.wait_ge(kvT_ready, n)
                            nc.tensor.transpose(tpb[:, 2], kv[:, v, 0], ident[:])
                            nc.tensor.transpose(tpb[:, 3], kv[:, v, 1], ident[:]).then_inc(kvT_seen, 1)
                        g, v, n, real, again = lagged(i, u, 3)
                        if real:
                            pe.wait_ge(kvT_ready, n + 1)
                            if not isinstance(n, int) or n >= 1:
                                pe.wait_ge(att_ready, n)
                            nc.tensor.matmul(pr[:, 0], kvT[:, v, 0], rel_k[:], start=True, stop=True)
                            nc.tensor.matmul(pr[:, 1], kvT[:, v, 1], rel_v[:], start=True, stop=True).then_inc(rel_ready, 1)
                        g, v, n, real, again = lagged(i, u, 4)
                        if real:
                            pe.wait_ge(att_ready, n + 1)
                            if v == 0 and (not isinstance(g, int) or g >= 1):
                                pe.wait_ge(group_done, g)
                            cs = slice(v * P, v * P + P)
                            nc.tensor.matmul(attT[:, cs], att[:, v], ident[:], start=True, stop=True)
                            nc.tensor.transpose(msgT[:, cs], rk[:, v, 1], ident[:]).then_inc(attT_ready, 1)
                    edge_steps(pe, step, 4)

                @block.vector
                def _(dve):
                    dve.memset(run[:], 0.0).then_inc(run_set, 1)
                    dve.wait_ge(run_set, 1)
                    C_KV, C_RK, C_GR = 2, 4, 5

                    def step(i, u):
                        g, v, n, real, again = lagged(i, u, 1)
                        if real:
                            dve.wait_ge(kv0_ready, n * 2 + 2)
                            dve.scalar_tensor_tensor(kv[:, v], pj[:, 1, 0:2], xs[:, v, C_TYPE + 1:C_TYPE + 2], kv[:, v], ALU.mult, ALU.add).then_inc(kv1_ready, 1)
                            dve.scalar_tensor_tensor(qq[:, v], pj[:, 1, 2], xd[:, v, C_TYPE + 1:C_TYPE + 2], qq[:, v], ALU.mult, ALU.add).then_inc(kv1_ready, 1)
                            dve.wait_ge(kv1_ready, n * C_KV + 2)
                            dve.scalar_tensor_tensor(kv[:, v], pj[:, 2, 0:2], xs[:, v, C_TYPE + 2:C_TYPE + 3], kv[:, v], ALU.mult, ALU.add).then_inc(kv_ready, 1)
                            dve.scalar_tensor_tensor(qq[:, v], pj[:, 2, 2], xd[:, v, C_TYPE + 2:C_TYPE + 3], qq[:, v], ALU.mult, ALU.add).then_inc(kv_ready, 1)
                        g, v, n, real, again = lagged(i, u, 3)
                        if real:
                            dve.wait_ge(rk0_ready, n + 1)
                            for r in range(1, RELS):
                                dve.scalar_tensor_tensor(rk[:, v], pr[:, :, r], mask[:, v, r:r + 1], rk[:, v], ALU.mult, ALU.add).then_inc(rk_step, 1)
                                dve.wait_ge(rk_step, n * C_RK + r)
                            dve.tensor_tensor(prod[:], rk[:, v, 0], qq[:, v], ALU.mult).then_inc(rk_step, 1)
                            if again:
                                dve.wait_ge(attT_ready, n - U + 1)
                            dve.wait_ge(rk_step, n * C_RK + 4)
                            dve.reduce_sum(attr_h[:], prod[:].rearrange("p (h f) -> p h f", h=HEADS), AX.X).then_inc(sum_ready, 1)
                            dve.wait_ge(sum_ready, n + 1)
                            dve.tensor_copy(att[:, v].rearrange("p (h f) -> p h f", h=HEADS),
                                            attr_h[:].rearrange("p (h o) -> p h o", o=1).to_broadcast([P, HEADS, DK])).then_inc(att_ready, 1)
                        if u == 3 and (not isinstance(i, int) or 1 <= i <= EG):
                            first_half(i - 1)
                        if u == 0 and (not isinstance(i, int) or 2 <= i):
                            second_half(i - 2)

                    def first_half(g):
                        s0 = g * C_GR
                        dve.tensor_copy(run[:, :, 0], run[:, :, U * P]).then_inc(group_step, 1)
                        dve.wait_ge(reset_in, g * 16 + 16)
                        dve.wait_ge(attT_ready, g * U + U)
                        dve.wait_ge(group_step, s0 + 1)
                        dve.tensor_tensor_scan(run[:, 0, 1:U * P + 1], reset[:], attT[:], run[:, 0, 0:1], ALU.add, ALU.max).then_inc(group_step, 1)
                        dve.wait_ge(group_step, s0 + 2)
                        dve.tensor_tensor(diff[:, 0], run[:, 0, 0:U * P], reset[:], ALU.add).then_inc(group_step, 1)
                        dve.tensor_tensor(diff[:, 1], attT[:], run[:, 0, 1:U * P + 1], ALU.subtract).then_inc(diff_ready, 1)
                        dve.wait_ge(group_step, s0 + 3)
                        dve.tensor_tensor(diff[:, 0], diff[:, 0], run[:, 0, 1:U * P + 1], ALU.subtract).then_inc(diff_ready, 1)

                    def second_half(g):
                        s0 = g * C_GR
                        dve.wait_ge(exp_ready, g + 1)
                        dve.tensor_tensor_scan(run[:, 2, 1:U * P + 1], expd[:, 0], expd[:, 1], run[:, 2, 0:1], ALU.mult, ALU.add).then_inc(sum2_step, 1)
                        dve.tensor_tensor(wm[:], expd[:, 1], msgT[:], ALU.mult).then_inc(group_step, 1)
                        dve.wait_ge(sum2_step, g * 3 + 1)
                        dve.tensor_scalar_add(den[:], run[:, 2, 1:U * P + 1], 1e-16).then_inc(sum2_step, 1)
                        dve.wait_ge(group_step, s0 + 4)
                        dve.tensor_tensor_scan(run[:, 1, 1:U * P + 1], expd[:, 0], wm[:], run[:, 1, 0:1], ALU.mult, ALU.add).then_inc(group_step, 1)
                        dve.wait_ge(sum2_step, g * 3 + 2)
                        dve.reciprocal(den[:], den[:]).then_inc(sum2_step, 1)
                        dve.wait_ge(sum2_step, g * 3 + 3)
                        dve.wait_ge(group_step, s0 + 5)
                        dve.tensor_tensor(agg[:, bass.ds(g * U * P, U * P)], run[:, 1, 1:U * P + 1], den[:], ALU.mult).then_inc(group_done, 1)
                    edge_steps(dve, step, 5)
            clear()
        rows_phase(True)

        agg_ctx.close()
        R = 14

        def conv_phase(second):
            name = "conv2" if second else "conv1"
            ctx = ExitStack()
            with ctx:
                def lb(n, shape, dt):
                    return ctx.enter_context(nc.sbuf_tensor(f"{name}_{n}", shape, dt))

                def lp(n, shape, dt):
                    return ctx.enter_context(nc.psum_tensor(f"{name}_{n}", shape, dt))

                ls, clear = phase_sems(name + "_")

                table, w, b_all = (t1, w_2, b2_all) if second else (ta, w_1, b1_all)
                idx = lb("idx", [P, ET], I32)
                ring = lb("ring", [P, R, 1], I32)
                oring = lb("oring", [P, R, 1], I32)
                row = lb("row", [P, R, D], F32)
                sT = lb("sT", [P, R, P], F32)
                keep = lb("keep", [P, R, P], F32)
                res = lb("res", [P, R, D], F32)
                rx = lb("rx", [P, R, D], F32)
                pT = lp("pT", [P, 2, 512], F32)
                pm = lp("pm", [P, 2, 512], F32)
                idx_ready, ring_set, scaled = ls("idx_ready"), ls("ring_set"), ls("scaled")
                got = [ls(f"got{u}") for u in range(R)]
                keep_in = [ls(f"keep_in{u}") for u in range(R)]
                stored = [ls(f"stored{u}") for u in range(R)]
                t_ready, s_ready, m_ready, v_ready, res_ready = (
                    ls("t_ready"), ls("s_ready"), ls("m_ready"), ls("v_ready"), ls("res_ready"))
                x_in = [ls(f"x_in{u}") for u in range(R)] if second else None

                with nc.Block() as block:
                    @block.gpsimd
                    def _(pool):
                        pool.wait_ge(idx_ready, 1)
                        settle(pool, "pool")

                        def step(i, u):
                            g, v, n, real, again = lagged(i, u, 0, R)
                            if real:
                                if again:
                                    pool.wait_ge(t_ready, n - R + 1)
                                    settle(pool, "pool")
                                pool.tensor_copy(ring[:, v], idx[:, bass.ds(n, 1)]).then_inc(ring_set, 1)
                                if second:
                                    if again:
                                        pool.wait_ge(stored[v], g * 16)
                                        settle(pool, "pool")
                                    pool.tensor_copy(oring[:, v], out_i[:, bass.ds(n, 1)]).then_inc(ring_set, 1)
                                pool.wait_ge(ring_set, n * (1 + second) + 1 + second)
                                settle(pool, "pool")
                                pool.indirect_dma_start(out=row[:, v, :], out_offset=None, in_=table,
                                                        in_offset=bass.IndirectOffsetOnAxis(ap=ring[:, v], axis=0)).then_inc(got[v], 16)
                            g, v, n, real, again = lagged(i, u, 8, R)
                            if second and real:
                                pool.wait_ge(res_ready, n + 1)
                                settle(pool, "pool")
                                pool.indirect_dma_start(out=out, out_offset=bass.IndirectOffsetOnAxis(ap=oring[:, v], axis=0),
                                                        in_=res[:, v, :], in_offset=None, bounds_check=N - 1,
                                                        oob_is_err=False).then_inc(stored[v], 16)
                        edge_steps(pool, step, 8 if second else 0, R)
                        if second:
                            for u in range(R):
                                pool.wait_ge(stored[u], 16 * (ET // R))

                    @block.sync
                    def _(sp):
                        def step(i, u):
                            g, v, n, real, again = lagged(i, u, 0, R)
                            if real:
                                if again:
                                    sp.wait_ge(s_ready, n - R + 1)
                                    settle(sp, "sp")
                                sp.dma_start(keep[:, v], keep_row[bass.ds(n * P, P)].partition_broadcast(P)).then_inc(keep_in[v], 16)
                                if second:
                                    if again:
                                        sp.wait_ge(res_ready, n - R + 1)
                                        settle(sp, "sp")
                                    sp.dma_start(rx[:, v], x1_rows[bass.ds(n * P, P)]).then_inc(x_in[v], 16)
                            g, v, n, real, again = lagged(i, u, 8, R)
                            if real and not second:
                                sp.wait_ge(res_ready, n + 1)
                                settle(sp, "sp")
                                sp.dma_start(t1[bass.ds(n * P, P)], res[:, v]).then_inc(stored[v], 16)
                        edge_steps(sp, step, 8, R)
                        if not second:
                            for u in range(R):
                                sp.wait_ge(stored[u], 16 * (ET // R))

                    @block.scalar
                    def _(act):
                        def step(i, u):
                            g, v, n, real, again = lagged(i, u, 0, R)
                            if second and real:
                                act.wait_ge(got[v], g * 16 + 16)
                                settle(act, "act")
                                nc.scalar.activation(row[:, v], row[:, v], ACT.Copy, scale=ats[:, bass.ds(n, 1), 0]).then_inc(scaled, 1)
                            g, v, n, real, again = lagged(i, u, 2, R)
                            if not second and real:
                                act.wait_ge(v_ready, n + 1)
                                nc.scalar.activation(res[:, v], res[:, v], ACT.Relu).then_inc(res_ready, 1)
                        edge_steps(act, step, 2, R)

                    @block.tensor
                    def _(pe):
                        def step(i, u):
                            g, v, n, real, again = lagged(i, u, 0, R)
                            if real:
                                if second:
                                    pe.wait_ge(scaled, n + 1)
                                else:
                                    pe.wait_ge(got[v], g * 16 + 16)
                                if not isinstance(n, int) or n >= 2:
                                    pe.wait_ge(s_ready, n - 1)
                                nc.tensor.transpose(pT[:, v % 2, 0:P], row[:, v], ident[:]).then_inc(t_ready, 1)
                            g, v, n, real, again = lagged(i, u, 1, R)
                            if real:
                                pe.wait_ge(s_ready, n + 1)
                                if not isinstance(n, int) or n >= 2:
                                    pe.wait_ge(v_ready, n - 1)
                                nc.tensor.matmul(pm[:, v % 2, 0:D], sT[:, v], w[:], start=True, stop=True).then_inc(m_ready, 1)
                        edge_steps(pe, step, 1, R)

                    @block.vector
                    def _(dve):
                        dve.tensor_scalar(idx[:], ats[:, :, 2], float(EP) if second else float(EP + NP), None, ALU.min).then_inc(idx_ready, 1)

                        def step(i, u):
                            g, v, n, real, again = lagged(i, u, 0, R)
                            if real:
                                dve.wait_ge(t_ready, n + 1)
                                dve.wait_ge(keep_in[v], g * 16 + 16)
                                if again:
                                    dve.wait_ge(m_ready, n - R + 1)
                                if isinstance(n, int) and n == 0:
                                    before = 0.0
                                else:
                                    dve.wait_ge(s_ready, n)
                                    before = sT[:, (v - 1) % R, P - 1:P]
                                dve.tensor_tensor_scan(sT[:, v], keep[:, v], pT[:, v % 2, 0:P], before, ALU.mult, ALU.add).then_inc(s_ready, 1)
                            g, v, n, real, again = lagged(i, u, 2, R)
                            if real:
                                dve.wait_ge(m_ready, n + 1)
                                if again:
                                    dve.wait_ge(stored[v], g * 16)
                                dve.scalar_tensor_tensor(res[:, v], pm[:, v % 2, 0:D], ats[:, bass.ds(n, 1), 3], b_all[:], ALU.mult, ALU.add).then_inc(v_ready, 1)
                                if second:
                                    dve.wait_ge(x_in[v], g * 16 + 16)
                                    dve.wait_ge(v_ready, n + 1)
                                    dve.scalar_tensor_tensor(res[:, v], res[:, v], 0.0, rx[:, v], ALU.max, ALU.add).then_inc(res_ready, 1)
                        edge_steps(dve, step, 2, R)
                clear()

        conv_phase(False)
        conv_phase(True)


_INS = ['x', 'src', 'dst', 'edge_type_4', 'node_type_3', 'L0_gnn_Wk', 'L0_gnn_bk', 'L0_gnn_Wq', 'L0_gnn_bq', 'L0_gnn_Wv',
        'L0_gnn_bv', 'L0_gnn_Wa', 'L0_gnn_ba', 'L0_gnn_rel_pri', 'L0_gnn_rel_att', 'L0_gnn_rel_msg', 'L0_gnn_skip',
        'L0_gnn_ln_g', 'L0_gnn_ln_b', 'L1_gnn_W1', 'L1_gnn_b1', 'L1_gnn_W2', 'L1_gnn_b2']
_OUTS = [((N, D), 'float32')]


def kernel(**inputs):
    import numpy as _np
    import concourse.bacc as _bacc
    from concourse import mybir as _mybir
    from concourse.bass_utils import run_bass_kernel_spmd as _run

    nc = _bacc.Bacc("TRN2", target_bir_lowering=False, num_devices=1)
    arrays, args = {}, []
    for name in _INS:
        a = _np.ascontiguousarray(inputs[name])
        arrays[f"in_{name}_dram"] = a
        args.append(nc.dram_tensor(f"in_{name}_dram", a.shape, _mybir.dt.from_np(a.dtype), kind="ExternalInput").ap())
    for i, (shape, dtype) in enumerate(_OUTS):
        dt = _mybir.dt.from_np(_np.dtype(dtype))
        args.append(nc.dram_tensor(f"out_{i}_dram", shape, dt, kind="ExternalOutput").ap())
    hgt_then_graphconv(nc, *args)
    r = _run(nc, [arrays], core_ids=[0])
    got = tuple(r.results[0][f"out_{i}_dram"] for i in range(len(_OUTS)))
    return got[0]
```

```python
from contextlib import ExitStack

import concourse.bass as bass
from concourse import mybir

F32 = mybir.dt.float32
BF16 = mybir.dt.bfloat16
FP16 = mybir.dt.float16
I32 = mybir.dt.int32
ALU = mybir.AluOpType
ACT = mybir.ActivationFunctionType
AX = mybir.AxisListType

P = 128
D = 128
N = 50000
E = 25000
TYPES = 3
RELS = 4
HEADS = 8
DK = D // HEADS
ET = -(-E // P)
EP = ET * P
HALF = ET // 2
U = 4
EG = ET // U
NT = -(-N // P)
NP = NT * P
LO = NT
NG = 17
NGROUPS = NT // NG
GN = NG * P
LASTN = N - (NGROUPS - 1) * GN
LASTFULL = LASTN // NG
LASTREST = LASTN - LASTFULL * NG
TG = 7
TGROUPS = ET // TG
RW = 136
C_RSTD, C_NMR, C_TYPE, C_SO, C_SI, C_IDX = 128, 129, 130, 133, 134, 135
SKIP = 100000
RESET = -1.0e38
EPS = 1e-5
SPLIT = 3
K9 = TYPES * SPLIT
CW = 129
GW = 256

assert ET == 2 * HALF and ET == U * EG and NT == NG * NGROUPS and ET == TG * TGROUPS


def bcast(ap, shape):
    return ap.to_broadcast(shape)


def hgt_then_graphconv(nc, x, src, dst, edge_type, node_type, Wk, bk, Wq, bq, Wv, bv, Wa, ba, rel_pri, rel_att,
                       rel_msg, skip, ln_g, ln_b, W1, b1, W2, b2, out):
    top = ExitStack()
    with top, nc.allow_non_contiguous_dma(reason="small parameter and index lists"):
        def dram(name, shape, dt):
            return nc.dram_tensor(name, shape, dt, kind="Internal").ap()

        xt = dram("xt", [NP, RW], F32)
        xd_rows = dram("xd_rows", [EP, RW], F32)
        ta = dram("ta", [EP + NP, D], F32)
        t1 = dram("t1", [EP + 1, D], F32)
        x1_rows = dram("x1_rows", [EP, D], F32)
        attr = dram("attr", [3, NP], F32)
        reset_row = dram("reset_row", [EP], F32)
        rel_row = dram("rel_row", [ET, RELS, P], BF16)
        keep_row = dram("keep_row", [EP], F32)
        dst_pad = dram("dst_pad", [EP + P], I32)
        src_pad = dram("src_pad", [EP + P], I32)
        et_pad = dram("et_pad", [EP + P], I32)
        type_pad = dram("type_pad", [NP], I32)

        def sb_in(ctx):
            return lambda name, shape, dt: ctx.enter_context(nc.sbuf_tensor(name, shape, dt))

        def ps_in(ctx):
            return lambda name, shape, dt: ctx.enter_context(nc.psum_tensor(name, shape, dt))

        def sem_in(ctx):
            return lambda name: ctx.enter_context(nc.semaphore(name))

        def phase_sems(prefix=""):
            held = []

            def take(name):
                held.append(nc.alloc_semaphore(prefix + name))
                return held[-1]

            def clear():
                nc.all_engine_barrier()
                nc.clear_and_free_semaphores(held)
                nc.all_engine_barrier()
            return take, clear

        sb, sem = sb_in(top), sem_in(top)
        ident = sb("ident", [P, P], F32)
        identb = sb("identb", [P, P], BF16)
        ends_i = sb("ends_i", [P, ET, 2], I32)
        out_i = sb("out_i", [P, ET], I32)
        kk9 = sb("kk9", [P, K9], F32)
        typ9 = sb("typ9", [K9, 1], F32)
        a3 = sb("a3", [P, TYPES], F32)
        w_kv = sb("w_kv", [P, TYPES, 2, D], F32)
        w_q = sb("w_q", [P, TYPES, D], F32)
        w_a = sb("w_a", [P, TYPES, D], F32)
        rel_k = sb("rel_k", [P, RELS, D], F32)
        rel_v = sb("rel_v", [P, RELS, D], F32)
        w_1 = sb("w_1", [P, D], F32)
        w_2 = sb("w_2", [P, D], F32)
        b1_all = sb("b1_all", [P, D], F32)
        b2_all = sb("b2_all", [P, D], F32)
        rb2_all = sb("rb2_all", [P, D], F32)
        ones3 = sb("ones3", [SPLIT, P], BF16)
        bias3 = sb("bias3", [SPLIT, TYPES * 3 * D], BF16)
        tab9 = sb("tab9", [K9, CW + GW], BF16)
        ats = sb("ats", [P, ET, 4], F32)
        iota3 = sb("iota3", [P, 4], F32)
        count = sb("count", [1, 1], I32)

        def edge_groups(eng, body):
            body(0, True, False)
            with eng.Fori(1, EG - 1) as i:
                body(i, False, False)
            body(EG - 1, False, True)

        def aggregate(st, tmp, mean, var, link):
            nc.vector.tensor_tensor(tmp[:, 0], st[:, :, 1], st[:, :, 4], ALU.add)
            nc.vector.tensor_tensor(tmp[:, 1], st[:, :, 1], st[:, :, 4], ALU.subtract)
            link(nc.vector.tensor_tensor(tmp[:, 2], st[:, :, 2], st[:, :, 5], ALU.add))
            nc.vector.tensor_scalar(mean, tmp[:, 0], 0.5, None, ALU.mult)
            nc.vector.tensor_scalar(tmp[:, 2], tmp[:, 2], 1.0 / D, EPS, ALU.mult, ALU.add)
            link(nc.vector.scalar_tensor_tensor(tmp[:, 1], tmp[:, 1], 0.25, tmp[:, 1], ALU.mult, ALU.mult))
            return nc.vector.tensor_tensor(var, tmp[:, 1], tmp[:, 2], ALU.add)

        turn = {}

        def settle(eng, name):
            if name not in turn:
                turn[name] = sem(f"turn_{name}")
            eng.sem_inc(turn[name], 1)

        def sort_edges():
            with ExitStack() as ctx:
                lb = sb_in(ctx)
                ls, clear = phase_sems("sort_")
                col_i = lb("col_i", [P, 3, ET], I32)
                col_f = lb("col_f", [P, ET], F32)
                all_i = lb("all_i", [P, P], I32)
                all_f = lb("all_f", [P, EP], F32)
                less = lb("less", [P, EP], BF16)
                same = lb("same", [P, P], F32)
                earlier = lb("earlier", [P, P], F32)
                rank = lb("rank", [P, 3], F32)
                place = lb("place", [P, 1], I32)
                moved = lb("moved", [P, 3], I32)
                cols_in, row_in, row_set, tri, step_v, sent = (
                    ls("cols_in"), ls("row_in"), ls("row_set"), ls("tri"), ls("step_v"), ls("sent"))
                ready = ls("ready")
                K = 7
                with nc.Block() as block:
                    @block.sync
                    def _(sp):
                        sp.dma_start(all_i[:], dst_pad[1:1 + P].partition_broadcast(P)).then_inc(row_in, 16)
                        with sp.Fori(1, ET) as t:
                            sp.wait_ge(row_set, t)
                            settle(sp, "sp")
                            sp.dma_start(all_i[:], dst_pad[bass.ds(t * P + 1, P)].partition_broadcast(P)).then_inc(row_in, 16)

                    @block.scalar
                    def _(act):
                        for k, pad in enumerate((dst_pad, src_pad, et_pad)):
                            act.dma_start(col_i[:, k], pad[1:1 + EP].rearrange("(t p) -> p t", p=P)).then_inc(cols_in, 16)

                    @block.tensor
                    def _(pe):
                        pe.wait_ge(cols_in, 48)
                        pe.nop()

                    @block.gpsimd
                    def _(pool):
                        pool.memset(earlier[:], 1.0).then_inc(tri, 1)
                        pool.wait_ge(tri, 1)
                        pool.affine_select(out=earlier[:], in_=earlier[:], compare_op=ALU.is_ge, fill=0.0, base=-1,
                                           pattern=[[-1, P]], channel_multiplier=1).then_inc(tri, 1)
                        with pool.Fori(0, ET) as t:
                            pool.wait_ge(ready, t + 1)
                            settle(pool, "pool")
                            for k, pad in enumerate((dst_pad, src_pad, et_pad)):
                                pool.indirect_dma_start(out=pad.rearrange("(n o) -> n o", o=1),
                                                        out_offset=bass.IndirectOffsetOnAxis(ap=place[:], axis=0),
                                                        in_=moved[:, k:k + 1], in_offset=None).then_inc(sent, 16)
                        pool.wait_ge(sent, 48 * ET)

                    @block.vector
                    def _(dve):
                        with dve.Fori(0, ET) as t:
                            dve.wait_ge(row_in, t * 16 + 16)
                            dve.tensor_scalar(all_f[:, bass.ds(t * P, P)], all_i[:], 0.5, None, ALU.add).then_inc(row_set, 1)
                        dve.wait_ge(cols_in, 48)
                        dve.wait_ge(tri, 2)
                        dve.tensor_scalar(col_f[:], col_i[:, 0], 0.25, None, ALU.add).then_inc(row_set, 1)
                        dve.wait_ge(row_set, ET + 1)

                        def tile(t, first):
                            n = [0]

                            def link(ins):
                                n[0] += 1
                                ins.then_inc(step_v, 1)
                                dve.wait_ge(step_v, t * K + n[0])

                            d = col_f[:, bass.ds(t, 1)]
                            link(dve.tensor_scalar(less[:], all_f[:], d, 0.0, ALU.is_lt, ALU.add, accum_out=rank[:, 0:1]))
                            link(dve.tensor_scalar(rank[:, 2:3], d, 0.25, None, ALU.add))
                            link(dve.scalar_tensor_tensor(same[:], all_f[:, bass.ds(t * P, P)], rank[:, 2:3], earlier[:], ALU.is_equal, ALU.mult))
                            link(dve.reduce_sum(rank[:, 1:2], same[:], AX.X))
                            if not first:
                                dve.wait_ge(sent, t * 48)
                            link(dve.scalar_tensor_tensor(place[:], rank[:, 0:1], 1.0, rank[:, 1:2], ALU.add, ALU.add))
                            link(dve.tensor_copy(moved[:], col_i[:, :, bass.ds(t, 1)].rearrange("p k o -> p (k o)")))
                            dve.sem_inc(ready, 1)
                            link(dve.tensor_scalar(all_f[:, bass.ds(t * P, P)], all_f[:, bass.ds(t * P, P)], -0.5, None, ALU.add))
                            assert n[0] == K
                        tile(0, True)
                        with dve.Fori(1, ET) as t:
                            tile(t, False)
                clear()

        with ExitStack() as ctx:
            lb, lp = sb_in(ctx), ps_in(ctx)
            ls, clear = phase_sems("list_")
            pad_i = lb("pad_i", [1, 2, P], I32)
            pair_i = lb("pair_i", [P, 2, ET], I32)
            pair_f = lb("pair_f", [P, 2, ET], F32)
            falls = lb("falls", [P, ET], F32)
            falls_p = lb("falls_p", [P, 1], F32)
            ones = lb("ones", [P, 1], F32)
            total = lp("total", [1, 1], F32)
            padded = ls("padded")
            pads_set = ls("pads_set")
            pairs_in = ls("pairs_in")
            falls_step = ls("falls_step")
            summed = ls("summed")
            with nc.Block() as block:
                @block.sync
                def _(sp):
                    for pad, given in ((dst_pad, dst), (src_pad, src), (et_pad, edge_type)):
                        sp.dma_start(pad[1:1 + E].rearrange("(a b) -> a b", b=25),
                                     given.rearrange("(a b) -> a b", b=25)).then_inc(padded, 16)
                    sp.wait_ge(pads_set, 3)
                    for pad, k in ((dst_pad, 0), (src_pad, 0), (et_pad, 1)):
                        sp.dma_start(pad[0:1].rearrange("(o b) -> o b", o=1), pad_i[:, 1, 0:1]).then_inc(padded, 16)
                        sp.dma_start(pad[1 + E:EP + 3].rearrange("(o b) -> o b", o=1),
                                     pad_i[:, k, 0:EP + 2 - E]).then_inc(padded, 16)
                    sp.dma_start(type_pad[0:N].rearrange("(a b) -> a b", b=50),
                                 node_type.rearrange("(a b) -> a b", b=50)).then_inc(padded, 16)
                    sp.dma_start(type_pad[N:NP].rearrange("(o b) -> o b", o=1), pad_i[:, 1, 1:1 + NP - N]).then_inc(padded, 16)
                    sp.wait_ge(padded, 16 * 11)
                    for k in range(2):
                        sp.dma_start(pair_i[:, k], dst_pad[1 + k:1 + k + EP].rearrange("(p t) -> p t", p=P)).then_inc(pairs_in, 16)

                @block.gpsimd
                def _(pool):
                    pool.memset(pad_i[:, 0], N).then_inc(pads_set, 1)
                    pool.memset(pad_i[:, 1, 0:1], -1).then_inc(pads_set, 1)
                    pool.memset(pad_i[:, 1, 1:P], 0).then_inc(pads_set, 1)

                @block.vector
                def _(dve):
                    dve.memset(ones[:], 1.0).then_inc(falls_step, 1)
                    dve.wait_ge(pairs_in, 32)
                    dve.tensor_copy(pair_f[:], pair_i[:]).then_inc(falls_step, 1)
                    dve.wait_ge(falls_step, 2)
                    dve.tensor_tensor(falls[:], pair_f[:, 0], pair_f[:, 1], ALU.is_gt).then_inc(falls_step, 1)
                    dve.wait_ge(falls_step, 3)
                    dve.reduce_sum(falls_p[:], falls[:], AX.X).then_inc(falls_step, 1)
                    dve.wait_ge(summed, 1)
                    dve.tensor_copy(count[:], total[:]).then_inc(falls_step, 1)
                    dve.wait_ge(falls_step, 5)

                @block.tensor
                def _(pe):
                    pe.wait_ge(falls_step, 4)
                    nc.tensor.matmul(total[:], falls_p[:], ones[:], start=True, stop=True).then_inc(summed, 1)
            clear()
        falling = nc.values_load(count[0:1, 0:1], min_val=0, max_val=EP)
        with nc.If(falling > 0):
            sort_edges()

        with ExitStack() as ctx:
            lb, lp = sb_in(ctx), ps_in(ctx)
            ls, clear = phase_sems()
            rows = lb("rows", [HALF, 5, 2, P], I32)
            rowf = lb("rowf", [HALF, 5, 2, P], F32)
            flag = lb("flag", [HALF, 3, 2, P], F32)
            rel_flag = lb("rel_flag", [HALF, RELS, 2, P], BF16)
            cols = lb("cols", [P, 4, ET], F32)
            hilo = lb("hilo", [P, 2, 2, ET], F32)
            hi_i = lb("hi_i", [P, 2, ET], I32)
            iota_i = lb("iota_i", [P, LO], I32)
            iota_h = lb("iota_h", [P, LO], FP16)
            kk_i = lb("kk_i", [P, K9], I32)
            row_i = lb("row_i", [K9, 1], I32)
            rowk = lb("rowk", [K9, 4], F32)
            rowk_i = lb("rowk_i", [K9, 1], I32)
            hot_hi = lb("hot_hi", [P, U, 2, P], BF16)
            hot_lo = lb("hot_lo", [P, U, 2, LO], BF16)
            deg = lb("deg", [P, 2, LO], F32)
            node_f = lb("node_f", [P, LO], F32)
            node_i = lb("node_i", [P, LO], I32)
            cum = lb("cum", [P, LO], F32)
            has = lb("has", [P, LO], F32)
            zero = lb("zero", [P, LO], F32)
            power = lb("power", [P, 2, LO], F32)
            at3 = lb("at3", [P, 3, LO], F32)
            upper = lb("upper", [P, P], F32)
            pri = lb("pri", [P, RELS], F32)
            bias_f = lb("bias_f", [SPLIT, TYPES * 3 * D], F32)
            bias_r = lb("bias_r", [SPLIT, TYPES * 3 * D], F32)
            bias_p = lb("bias_p", [SPLIT, SPLIT, TYPES * 3 * D], BF16)
            tab_f = lb("tab_f", [K9, CW + GW], F32)
            tab_r = lb("tab_r", [K9, CW + GW], F32)
            tab_p = lb("tab_p", [K9, SPLIT, CW + GW], BF16)
            sk9 = lb("sk9", [K9, 1], F32)
            t1d = lb("t1d", [1, D], F32)
            tp = [lp(f"tp{i}", [P, 4, HALF], F32) for i in range(2)]
            hist = [lp(f"hist{i}", [P, LO], F32) for i in range(2)]
            offs = lp("offs", [P, 1], F32)
            rows_in = ls("rows_in")
            weights_in = ls("weights_in")
            rel_zero = ls("rel_zero")
            pool_c = ls("pool_c")
            vec = ls("vec")
            exps = ls("exps")
            sk_in = ls("sk_in")
            rows_ready = ls("rows_ready")
            tps = ls("tps")
            hots = ls("hots")
            hists = ls("hists")
            tot_ready = ls("tot_ready")
            offs_ready = ls("offs_ready")
            powed = ls("powed")
            deg_ready = ls("deg_ready")
            flags_ready = ls("flags_ready")
            stored = ls("stored")
            with nc.Block() as block:
                @block.sync
                def _(sp):
                    for k, (pad, at) in enumerate(((dst_pad, 1), (dst_pad, 0), (dst_pad, 2), (src_pad, 1), (et_pad, 1))):
                        sp.dma_start(rows[:, k], pad[at:at + EP].rearrange("(c q r) -> q c r", c=2, q=HALF)).then_inc(rows_in, 16)
                    sp.wait_ge(flags_ready, 1)
                    sp.dma_start(reset_row.rearrange("(c q r) -> q c r", c=2, q=HALF), flag[:, 0]).then_inc(stored, 16)
                    sp.dma_start(keep_row.rearrange("(c q r) -> q c r", c=2, q=HALF), flag[:, 1]).then_inc(stored, 16)
                    for c in range(2):
                        sp.dma_start(rel_row[c * HALF:(c + 1) * HALF], rel_flag[:, :, c]).then_inc(stored, 16)
                    sp.wait_ge(deg_ready, 1)
                    for k in range(3):
                        sp.dma_start(attr[k].rearrange("(p l) -> p l", p=P), at3[:, k]).then_inc(stored, 16)
                    sp.wait_ge(stored, 16 * 7)

                @block.scalar
                def _(act):
                    for t in range(TYPES):
                        act.dma_start(w_kv[:, t, 0], Wk[t]).then_inc(weights_in, 16)
                        act.dma_start(w_kv[:, t, 1], Wv[t]).then_inc(weights_in, 16)
                        act.dma_start(w_q[:, t], Wq[t]).then_inc(weights_in, 16)
                        act.dma_start(w_a[:, t], Wa[t]).then_inc(weights_in, 16)
                    act.dma_start(w_1[:], W1).then_inc(weights_in, 16)
                    act.dma_start(w_2[:], W2).then_inc(weights_in, 16)
                    act.dma_start(b1_all[:], b1.partition_broadcast(P)).then_inc(weights_in, 16)
                    act.dma_start(b2_all[:], b2.partition_broadcast(P)).then_inc(weights_in, 16)
                    act.dma_start(a3[:], skip.partition_broadcast(P)).then_inc(sk_in, 16)
                    for t in range(TYPES):
                        r9 = slice(SPLIT * t, SPLIT * t + SPLIT)
                        act.dma_start(sk9[r9], skip[t:t + 1].partition_broadcast(SPLIT)).then_inc(sk_in, 16)
                        act.dma_start(tab_f[r9, 0:D], ba[t].partition_broadcast(SPLIT)).then_inc(weights_in, 16)
                        act.dma_start(tab_f[r9, CW:CW + D], ln_g[t].partition_broadcast(SPLIT)).then_inc(weights_in, 16)
                        act.dma_start(tab_f[r9, CW + D:CW + GW], ln_b[t].partition_broadcast(SPLIT)).then_inc(weights_in, 16)
                        at = 2 * D * t
                        act.dma_start(bias_f[:, at:at + D], bk[t].partition_broadcast(SPLIT)).then_inc(weights_in, 16)
                        act.dma_start(bias_f[:, at + D:at + 2 * D], bv[t].partition_broadcast(SPLIT)).then_inc(weights_in, 16)
                        at = 2 * D * TYPES + D * t
                        act.dma_start(bias_f[:, at:at + D], bq[t].partition_broadcast(SPLIT)).then_inc(weights_in, 16)
                    act.wait_ge(rel_zero, 2)
                    for h in range(HEADS):
                        hs = slice(DK * h, DK * h + DK)
                        act.dma_start(rel_k[hs, :, hs], rel_att[:, h].rearrange("r d f -> d r f")).then_inc(weights_in, 16)
                        act.dma_start(rel_v[hs, :, hs], rel_msg[:, h].rearrange("r d f -> d r f")).then_inc(weights_in, 16)
                        act.dma_start(pri[hs, :], rel_pri[:, h].partition_broadcast(DK)).then_inc(weights_in, 16)
                    act.wait_ge(sk_in, 16 * 4)
                    nc.scalar.activation(a3[:], a3[:], ACT.Exp, scale=-1.0).then_inc(exps, 1)
                    nc.scalar.activation(sk9[:], sk9[:], ACT.Exp, scale=-1.0).then_inc(exps, 1)
                    act.wait_ge(tot_ready, 1)
                    nc.scalar.activation(power[:], deg[:], ACT.Sqrt).then_inc(powed, 1)

                @block.gpsimd
                def _(pool):
                    pool.memset(rel_k[:], 0.0).then_inc(rel_zero, 1)
                    pool.memset(rel_v[:], 0.0).then_inc(rel_zero, 1)
                    pool.memset(ident[:], 0.0).then_inc(pool_c, 1)
                    pool.memset(identb[:], 0.0).then_inc(pool_c, 1)
                    pool.memset(upper[:], 1.0).then_inc(pool_c, 1)
                    pool.wait_ge(pool_c, 3)
                    for m in (ident, identb):
                        pool.affine_select(out=m[:], in_=m[:], compare_op=ALU.not_equal, fill=1.0, base=0,
                                           pattern=[[-1, P]], channel_multiplier=1).then_inc(pool_c, 1)
                    pool.affine_select(out=upper[:], in_=upper[:], compare_op=ALU.is_ge, fill=0.0, base=-1,
                                       pattern=[[1, P]], channel_multiplier=-1).then_inc(pool_c, 1)
                    pool.iota(iota_i[:], [[1, LO]], base=0, channel_multiplier=0).then_inc(pool_c, 1)
                    pool.iota(kk_i[:], [[1, TYPES], [0, SPLIT]], base=0, channel_multiplier=0).then_inc(pool_c, 1)
                    pool.iota(row_i[:], [[1, 1]], base=0, channel_multiplier=1).then_inc(pool_c, 1)
                    pool.iota(node_i[:], [[1, LO]], base=EP, channel_multiplier=LO).then_inc(pool_c, 1)

                @block.vector
                def _(dve):
                    n = [0]

                    def link(ins):
                        n[0] += 1
                        ins.then_inc(vec, 1)
                        dve.wait_ge(vec, n[0])

                    dve.memset(zero[:], 0.0).then_inc(vec, 1)
                    dve.memset(ones3[:], 1.0).then_inc(vec, 1)
                    n[0] = 2
                    dve.wait_ge(pool_c, 10)
                    dve.tensor_copy(iota_h[:], iota_i[:]).then_inc(vec, 1)
                    dve.tensor_copy(iota3[:], iota_i[:, 0:4]).then_inc(vec, 1)
                    dve.tensor_copy(kk9[:], kk_i[:]).then_inc(vec, 1)
                    dve.tensor_copy(node_f[:], node_i[:]).then_inc(vec, 1)
                    n[0] += 4
                    link(dve.tensor_copy(rowk[:, 0:1], row_i[:]))
                    link(dve.tensor_scalar(rowk_i[:], rowk[:, 0:1], -1.0, 1.0 / SPLIT, ALU.add, ALU.mult))
                    link(dve.tensor_copy(typ9[:], rowk_i[:]))
                    link(dve.scalar_tensor_tensor(rowk[:, 1:2], typ9[:], -float(SPLIT), rowk[:, 0:1], ALU.mult, ALU.add))
                    dve.wait_ge(rows_in, 16 * 5)
                    link(dve.tensor_copy(rowf[:], rows[:]))
                    link(dve.tensor_tensor(flag[:, 1], rowf[:, 0], rowf[:, 1], ALU.is_equal))
                    link(dve.tensor_scalar(flag[:, 0], flag[:, 1], -RESET, RESET, ALU.mult, ALU.add))
                    link(dve.tensor_tensor(flag[:, 2], rowf[:, 0], rowf[:, 2], ALU.is_equal))
                    for r in range(RELS):
                        link(dve.tensor_scalar(rel_flag[:, r], rowf[:, 4], float(r), None, ALU.is_equal))
                    dve.scalar_tensor_tensor(rowf[:, 1], flag[:, 2], float(SKIP), rowf[:, 0], ALU.mult,
                                             ALU.add).then_inc(flags_ready, 1)
                    dve.wait_ge(tps, 8)
                    for c in range(2):
                        dve.tensor_copy(cols[:, :, c * HALF:(c + 1) * HALF], tp[c][:]).then_inc(vec, 1)
                    n[0] += 2
                    dve.wait_ge(vec, n[0])
                    for to, k in ((ends_i[:, :, 1], 0), (out_i[:], 1), (ends_i[:, :, 0], 2)):
                        dve.tensor_copy(to, cols[:, k]).then_inc(vec, 1)
                    n[0] += 3
                    for s, k in ((0, 2), (1, 0)):
                        link(dve.tensor_scalar(hi_i[:, s], cols[:, k], -(LO - 1) / 2.0, 1.0 / LO, ALU.add, ALU.mult))
                        link(dve.tensor_copy(hilo[:, s, 0], hi_i[:, s]))
                        link(dve.scalar_tensor_tensor(hilo[:, s, 1], hilo[:, s, 0], -float(LO), cols[:, k], ALU.mult, ALU.add))

                    def hot(g, first, last):
                        for u in range(U):
                            t = g * U + u
                            if not first:
                                dve.wait_ge(hists, t - U + 1)
                            for s in range(2):
                                dve.tensor_scalar(hot_hi[:, u, s], iota_h[:, 0:P], hilo[:, s, 0, bass.ds(t, 1)], None,
                                                  ALU.is_equal).then_inc(hots, 1)
                                dve.tensor_scalar(hot_lo[:, u, s], iota_h[:], hilo[:, s, 1, bass.ds(t, 1)], None,
                                                  ALU.is_equal).then_inc(hots, 1)
                    edge_groups(dve, hot)
                    dve.wait_ge(exps, 2)
                    link(dve.tensor_scalar_add(a3[:], a3[:], 1.0))
                    link(dve.reciprocal(a3[:], a3[:]))
                    link(dve.tensor_scalar_add(sk9[:], sk9[:], 1.0))
                    link(dve.reciprocal(sk9[:], sk9[:]))
                    dve.wait_ge(weights_in, 16 * (16 + 18 + 3 * HEADS))
                    link(dve.tensor_scalar(pri[:], pri[:], DK ** -0.5, None, ALU.mult))
                    for r in range(RELS):
                        link(dve.tensor_scalar(rel_k[:, r], rel_k[:, r], pri[:, r:r + 1], None, ALU.mult))
                    link(dve.tensor_scalar_max(rb2_all[:], b2_all[:], 0.0))
                    link(dve.tensor_scalar_max(t1d[:], b1_all[0:1], 0.0))
                    link(dve.tensor_scalar(tab_f[:, 0:D], tab_f[:, 0:D], sk9[:], None, ALU.mult))
                    link(dve.tensor_scalar(tab_f[:, D:CW], sk9[:], -1.0, 1.0, ALU.mult, ALU.add))
                    for f, r, p, o, part in ((bias_f, bias_r, bias_p, bias3, 0), (tab_f, tab_r, tab_p, tab9, 1)):
                        link(dve.tensor_copy(p[:, 0], f[:]))
                        link(dve.tensor_tensor(r[:], f[:], p[:, 0], ALU.subtract))
                        link(dve.tensor_copy(p[:, 1], r[:]))
                        link(dve.tensor_tensor(r[:], r[:], p[:, 1], ALU.subtract))
                        link(dve.tensor_copy(p[:, 2], r[:]))
                        rows_n = f.shape[0]
                        for k in range(SPLIT):
                            link(dve.tensor_scalar(rowk[0:rows_n, 2:3], rowk[0:rows_n, part:part + 1], float(k), None, ALU.is_equal))
                            if k == 0:
                                link(dve.tensor_scalar(o[:], p[:, k], rowk[0:rows_n, 2:3], None, ALU.mult))
                            else:
                                link(dve.scalar_tensor_tensor(o[:], p[:, k], rowk[0:rows_n, 2:3], o[:], ALU.mult, ALU.add))
                    dve.wait_ge(hists, ET)
                    for s in range(2):
                        link(dve.tensor_scalar_max(deg[:, s], hist[s][:], 1.0))
                    dve.tensor_scalar_min(has[:], hist[1][:], 1.0).then_inc(vec, 1)
                    n[0] += 1
                    link(dve.tensor_tensor_scan(cum[:], hist[1][:], zero[:], 0.0, ALU.add, ALU.add))
                    dve.sem_inc(tot_ready, 1)
                    dve.wait_ge(offs_ready, 1)
                    link(dve.tensor_scalar(cum[:], cum[:], offs[:], -1.0, ALU.add, ALU.add))
                    link(dve.tensor_tensor(cum[:], cum[:], node_f[:], ALU.subtract))
                    link(dve.tensor_tensor(cum[:], cum[:], has[:], ALU.mult))
                    link(dve.tensor_tensor(at3[:, 2], cum[:], node_f[:], ALU.add))
                    dve.wait_ge(powed, 1)
                    link(dve.reciprocal(power[:], power[:]))
                    link(dve.tensor_tensor(at3[:, 0:2], power[:], power[:], ALU.mult))
                    link(dve.tensor_tensor(at3[:, 0:2], at3[:, 0:2], deg[:], ALU.mult))
                    link(dve.tensor_scalar(at3[:, 0:2], at3[:, 0:2], -0.5, 1.5, ALU.mult, ALU.add))
                    link(dve.tensor_tensor(at3[:, 0:2], at3[:, 0:2], power[:], ALU.mult))
                    dve.sem_inc(deg_ready, 1)

                @block.tensor
                def _(pe):
                    pe.wait_ge(pool_c, 6)
                    pe.wait_ge(flags_ready, 1)
                    for c in range(2):
                        for k, at in enumerate((0, 1, 3, 4)):
                            nc.tensor.transpose(tp[c][:, k], rowf[:, at, c], ident[0:HALF, 0:HALF]).then_inc(tps, 1)

                    def product(g, first, last):
                        for u in range(U):
                            t = g * U + u
                            pe.wait_ge(hots, 4 * t + 4)
                            for s in range(2):
                                m = nc.tensor.matmul(hist[s][:], hot_hi[:, u, s], hot_lo[:, u, s],
                                                     start=first and u == 0, stop=last and u == U - 1)
                            m.then_inc(hists, 1)
                    edge_groups(pe, product)
                    pe.wait_ge(tot_ready, 1)
                    nc.tensor.matmul(offs[:], upper[:], cum[:, LO - 1:LO], start=True, stop=True).then_inc(offs_ready, 1)
            with nc.Block() as block:
                @block.sync
                def _(sp):
                    sp.dma_start(t1[EP:EP + 1], t1d[:]).then_inc(stored, 16)
                    sp.wait_ge(stored, 16 * 8)
            clear()

        def node_groups(eng, body):
            body(0, 0, True, False)
            body(1, 1, True, False)
            with eng.Fori(1, (NGROUPS - 1) // 2) as i:
                body(2 * i, 0, False, False)
                body(2 * i + 1, 1, False, False)
            body(NGROUPS - 1, 0, False, True)

        with ExitStack() as ctx:
            lb = sb_in(ctx)
            ls, clear = phase_sems()
            xr = [lb(f"xr{b}", [P, NG, RW], F32) for b in range(2)]
            ar = [lb(f"ar{b}", [P, 3, NG], F32) for b in range(2)]
            ty = [lb(f"ty{b}", [P, NG], I32) for b in range(2)]
            st = [lb(f"st{b}", [P, NG, 6], F32) for b in range(2)]
            mv = [lb(f"mv{b}", [P, NG], F32) for b in range(2)]
            ve = [lb(f"ve{b}", [P, NG], F32) for b in range(2)]
            mh = lb("mh", [P, NG], F32)
            tmp = lb("tmp", [P, 3, NG], F32)
            half_set = ls("half_set")
            loaded = [ls(f"loaded{b}") for b in range(2)]
            written = [ls(f"written{b}") for b in range(2)]
            stats = ls("stats")
            var_ready = ls("var_ready")
            rstd_ready = ls("rstd_ready")
            row_ready = ls("row_ready")
            pad_set = ls("pad_set")
            with nc.Block() as block:
                @block.sync
                def _(sp):
                    def load(g, b, first, last):
                        if not first:
                            sp.wait_ge(written[b], wr(g, b))
                        if not last:
                            sp.dma_start(xr[b][:, :, 0:D], x[bass.ds(g * GN, GN)].rearrange("(p j) d -> p j d", p=P)).then_inc(loaded[b], 16)
                            sp.dma_start(ty[b][:], node_type[bass.ds(g * GN, GN)].rearrange("(p j) -> p j", p=P)).then_inc(loaded[b], 16)
                        else:
                            sp.wait_ge(pad_set, 1)
                            n0 = g * GN
                            n1 = n0 + LASTFULL * NG
                            sp.dma_start(xr[b][0:LASTFULL, :, 0:D], x[n0:n1].rearrange("(p j) d -> p j d", j=NG)).then_inc(loaded[b], 16)
                            sp.dma_start(xr[b][LASTFULL:LASTFULL + 1, 0:LASTREST, 0:D], x[n1:N].rearrange("(p j) d -> p j d", p=1)).then_inc(loaded[b], 16)
                            sp.dma_start(ty[b][0:LASTFULL], node_type[n0:n1].rearrange("(p j) -> p j", j=NG)).then_inc(loaded[b], 16)
                            sp.dma_start(ty[b][LASTFULL:LASTFULL + 1, 0:LASTREST], node_type[n1:N].rearrange("(p j) -> p j", p=1)).then_inc(loaded[b], 16)
                        sp.dma_start(ar[b][:], attr[:, bass.ds(g * GN, GN)].rearrange("k (p j) -> p k j", p=P)).then_inc(loaded[b], 16)

                    def wr(g, b):
                        return (g - b) * 8

                    node_groups(sp, load)

                @block.scalar
                def _(act):
                    def write(g, b, first, last):
                        act.wait_ge(row_ready, g + 1)
                        act.dma_start(xt[bass.ds(g * GN, GN)].rearrange("(p j) w -> p j w", p=P), xr[b][:]).then_inc(written[b], 16)
                    node_groups(act, write)
                    act.wait_ge(written[0], 16 * (NGROUPS // 2 + 1))
                    act.wait_ge(written[1], 16 * (NGROUPS // 2))

                @block.gpsimd
                def _(pool):
                    pool.memset(mh[:], -0.5).then_inc(half_set, 1)
                    pool.wait_ge(half_set, 1)

                    def rstd(g, b, first, last):
                        pool.wait_ge(var_ready, g + 1)
                        settle(pool, "pool")
                        pool.tensor_tensor(xr[b][:, :, C_RSTD], ve[b][:], mh[:], ALU.pow).then_inc(rstd_ready, 1)
                    node_groups(pool, rstd)

                @block.vector
                def _(dve):
                    def norm(g, b, first, last):
                        if last:
                            dve.wait_ge(written[b], 16 * (g // 2))
                            dve.memset(xr[b][:], 0.0).then_inc(stats, 1)
                            dve.memset(ty[b][:], 0).then_inc(stats, 1)
                            dve.wait_ge(stats, 6 * g + 2)
                            dve.sem_inc(pad_set, 1)
                        s0 = g * 6 + (2 if last else 0)
                        dve.wait_ge(loaded[b], (g - b) * 24 + (16 * 5 if last else 48))
                        for j in range(NG):
                            i = dve.bn_stats(st[b][:, j], xr[b][:, j, 0:D])
                        i.then_inc(stats, 1)
                        dve.wait_ge(stats, s0 + 1)

                        k = [s0 + 1]

                        def link(ins):
                            k[0] += 1
                            ins.then_inc(stats, 1)
                            dve.wait_ge(stats, k[0])
                        aggregate(st[b], tmp, mv[b][:], ve[b][:], link).then_inc(var_ready, 1)
                        dve.tensor_tensor(xr[b][:, :, C_TYPE:C_TYPE + TYPES],
                                          ty[b][:].rearrange("p (j o) -> p j o", o=1).to_broadcast([P, NG, TYPES]),
                                          iota3[:, 0:TYPES].rearrange("p (o t) -> p o t", o=1).to_broadcast([P, NG, TYPES]),
                                          ALU.is_equal).then_inc(stats, 1)
                        dve.tensor_copy(xr[b][:, :, C_SO:C_IDX + 1].rearrange("p j k -> p k j"), ar[b][:]).then_inc(stats, 1)
                        dve.wait_ge(rstd_ready, g + 1)
                        dve.scalar_tensor_tensor(xr[b][:, :, C_NMR], mv[b][:], -1.0, xr[b][:, :, C_RSTD], ALU.mult,
                                                 ALU.mult).then_inc(stats, 1)
                        dve.wait_ge(stats, s0 + 6)
                        dve.sem_inc(row_ready, 1)
                    node_groups(dve, norm)
            clear()

        def rows_phase(edges):
            G, groups = (TG, TGROUPS) if edges else (NG, NGROUPS)
            name = "edge" if edges else "node"
            CB = 1 if edges else 3
            banks = 4 if edges else 6
            cols = 4 * D if edges else CW
            parts = -(-G // CB)
            pairs = -(-G // 2)
            ctx = ExitStack()
            with ctx:
                def lb(n, shape, dt):
                    return ctx.enter_context(nc.sbuf_tensor(f"{name}_{n}", shape, dt))

                def lp(n, shape, dt):
                    return ctx.enter_context(nc.psum_tensor(f"{name}_{n}", shape, dt))

                ls, clear = phase_sems(name + "_")

                three = range(3)
                xr = [lb(f"xr{b}", [P, G, RW], F32) for b in three]
                hb = [lb(f"hb{b}", [P, G, D], F32) for b in three]
                rs = [lb(f"rs{b}", [P, G, D], F32) for b in three]
                hs = [lb(f"hs{b}", [P, G, D], F32) for b in three]
                ot = [lb(f"ot{b}", [P, G, D], F32) for b in three]
                oh = [lb(f"oh{b}", [K9, G * P], BF16) for b in three]
                st = lb("st", [P, G, 6], F32)
                tmp = lb("tmp", [P, 3, G], F32)
                mean = [[lb(f"mean{k}{b}", [P, G], F32) for b in three] for k in range(2)]
                var = [[lb(f"var{k}{b}", [P, G], F32) for b in three] for k in range(2)]
                rstd = [[lb(f"rstd{k}{b}", [P, G], F32) for b in three] for k in range(2)]
                nmr = [[lb(f"nmr{k}{b}", [P, G], F32) for b in three] for k in range(2)]
                sc3 = [lb(f"sc3{b}", [P, G], F32) for b in three]
                mh = lb("mh", [P, G], F32)
                if edges:
                    gl = [lb(f"gl{b}", [P, G * P], F32) for b in three]
                    oc = lb("oc", [P, G, TYPES, SPLIT], BF16)
                    am = lb("am", [P, G, TYPES], F32)
                    om = lb("om", [P, G], F32)
                    ohp = lp("ohp", [K9, G * P], BF16)
                else:
                    t9 = [lb(f"t9{b}", [K9, G * P], I32) for b in three]
                pc = lp("pc", [P, banks, 512], F32)
                pg = lp("pg", [P, 2, 2, GW], F32)
                loaded = [ls(f"loaded{b}") for b in three]
                half_set, gl_done, h_done, oc_ready, ohp_ready, oh_ready = (
                    ls("half_set"), ls("gl_done"), ls("h_done"), ls("oc_ready"), ls("ohp_ready"), ls("oh_ready"))
                c_ready, c_read, c1, c2 = ls("c_ready"), ls("c_read"), ls("c1"), ls("c2")
                var2_ready, rstd2_ready, nm2_ready, y_done = ls("var2"), ls("rstd2"), ls("nm2"), ls("y_done")
                g_ready, g_read = ls("g_ready"), ls("g_read")
                var3_ready, rstd3_ready, nm3_ready, hs_done, ot_done = (
                    ls("var3"), ls("rstd3"), ls("nm3"), ls("hs_done"), ls("ot_done"))
                hs_out = [ls(f"hs_out{b}") for b in three]
                ot_out = [ls(f"ot_out{b}") for b in three]
                per_load = 16 if edges else 32

                def steps(eng, body):
                    for i in range(2):
                        for b in three:
                            body(i, b)
                    with eng.Fori(2, (groups - 1) // 3) as i:
                        for b in three:
                            body(i, b)
                    for g in range((groups - 1) // 3 * 3, groups + 1):
                        body(g // 3, g % 3)

                def real(g):
                    return not isinstance(g, int) or 0 <= g < groups

                def later(g, k):
                    return not isinstance(g, int) or g >= k

                with nc.Block() as block:
                    @block.sync
                    def _(sp):
                        def load(g, b):
                            if later(g, 3):
                                sp.wait_ge(nm3_ready, g - 2)
                                settle(sp, "sp")
                                sp.wait_ge(h_done, (g - 2) * G)
                                settle(sp, "sp")
                            if edges:
                                sp.dma_start(xr[b][:], xd_rows[bass.ds(g * (G * P), G * P)].rearrange("(t p) w -> p t w", p=P)).then_inc(loaded[b], 16)
                            else:
                                sp.dma_start(xr[b][:], xt[bass.ds(g * GN, GN)].rearrange("(p j) w -> p j w", p=P)).then_inc(loaded[b], 16)
                                if later(g, 3):
                                    sp.wait_ge(oh_ready, g - 2)
                                    settle(sp, "sp")
                                sp.dma_start(t9[b][:], type_pad[bass.ds(g * GN, GN)].partition_broadcast(K9)).then_inc(loaded[b], 16)

                        def step(i, b):
                            g = i * 3 + b
                            p = (b - 1) % 3
                            ip = i - (b == 0)
                            if isinstance(g, int) and g == 0:
                                load(0, 0)
                            if real(g + 1):
                                load(g + 1, (b + 1) % 3)
                            if real(g - 1):
                                sp.wait_ge(ot_done, g)
                                settle(sp, "sp")
                                if edges:
                                    sp.dma_start(x1_rows[bass.ds((g - 1) * (G * P), G * P)].rearrange("(t p) w -> p t w", p=P), ot[p][:]).then_inc(ot_out[p], 16)
                                elif isinstance(g, int) and g == groups:
                                    n0 = (g - 1) * GN
                                    n1 = n0 + LASTFULL * NG
                                    sp.dma_start(out[n0:n1].rearrange("(p j) d -> p j d", j=NG), ot[p][0:LASTFULL]).then_inc(ot_out[p], 16)
                                    sp.dma_start(out[n1:N].rearrange("(p j) d -> p j d", p=1), ot[p][LASTFULL:LASTFULL + 1, 0:LASTREST]).then_inc(ot_out[p], 16)
                                else:
                                    sp.dma_start(out[bass.ds((g - 1) * GN, GN)].rearrange("(p j) d -> p j d", p=P), ot[p][:]).then_inc(ot_out[p], 16)
                        steps(sp, step)
                        for b in three:
                            n = (groups - b + 2) // 3
                            sp.wait_ge(hs_out[b], 16 * n)
                            sp.wait_ge(ot_out[b], 16 * (n + (not edges and (groups - 1) % 3 == b)))

                    @block.gpsimd
                    def _(pool):
                        pool.memset(mh[:], -0.5).then_inc(half_set, 1)
                        pool.wait_ge(half_set, 1)

                        def step(i, b):
                            g = i * 3 + b
                            p = (b - 1) % 3
                            ip = i - (b == 0)
                            if real(g):
                                pool.wait_ge(var2_ready, g + 1)
                                settle(pool, "pool")
                                pool.tensor_tensor(rstd[0][b][:], var[0][b][:], mh[:], ALU.pow).then_inc(rstd2_ready, 1)
                            if real(g - 1):
                                pool.wait_ge(var3_ready, g)
                                settle(pool, "pool")
                                pool.tensor_tensor(rstd[1][p][:], var[1][p][:], mh[:], ALU.pow).then_inc(rstd3_ready, 1)
                        steps(pool, step)

                    @block.scalar
                    def _(act):
                        def clipped(i, g, b):
                            act.wait_ge(loaded[b], i * per_load + per_load)
                            if later(g, 3):
                                act.wait_ge(c_read, (g - 2) * parts)
                            for j in range(G):
                                nc.scalar.activation(hb[b][:, j], xr[b][:, j, 0:D], ACT.Relu, bias=xr[b][:, j, C_NMR:C_NMR + 1],
                                                     scale=xr[b][:, j, C_RSTD:C_RSTD + 1]).then_inc(h_done, 1)
                            if edges:
                                settle(act, "act")
                                nc.scalar.activation(gl[b][:], agg[:, bass.ds(g * (G * P), G * P)], ACT.Gelu).then_inc(gl_done, 1)

                        def step(i, b):
                            g = i * 3 + b
                            p = (b - 1) % 3
                            ip = i - (b == 0)
                            if isinstance(g, int) and g == 0:
                                clipped(0, 0, 0)
                            if edges and real(g):
                                act.wait_ge(ohp_ready, g + 1)
                                if later(g, 3):
                                    act.wait_ge(g_ready, (g - 2) * pairs)
                                nc.scalar.activation(oh[b][:], ohp[:], ACT.Copy).then_inc(oh_ready, 1)
                            if real(g + 1):
                                clipped(i + (b == 2), g + 1, (b + 1) % 3)
                            if real(g):
                                act.wait_ge(nm2_ready, g + 1)
                                for j in range(G):
                                    nc.scalar.activation(rs[b][:, j], rs[b][:, j], ACT.Identity, bias=nmr[0][b][:, j:j + 1],
                                                         scale=rstd[0][b][:, j:j + 1]).then_inc(y_done, 1)
                            if real(g - 1):
                                act.wait_ge(nm3_ready, g)
                                if later(g, 4):
                                    act.wait_ge(hs_out[p], ip * 16)
                                for j in range(G):
                                    m = nc.scalar.activation(hs[p][:, j], rs[p][:, j], ACT.Relu, bias=nmr[1][p][:, j:j + 1],
                                                             scale=sc3[p][:, j:j + 1])
                                m.then_inc(hs_done, 1)
                                act.wait_ge(hs_done, g)
                                settle(act, "act")
                                if edges:
                                    act.dma_start(ta[bass.ds((g - 1) * (G * P), G * P)].rearrange("(t p) d -> p t d", p=P), hs[p][:]).then_inc(hs_out[p], 16)
                                else:
                                    act.dma_start(ta[bass.ds((g - 1) * GN + EP, GN)].rearrange("(p j) d -> p j d", p=P), hs[p][:]).then_inc(hs_out[p], 16)
                        steps(act, step)

                    @block.tensor
                    def _(pe):
                        def step(i, b):
                            g = i * 3 + b
                            p = (b - 1) % 3
                            ip = i - (b == 0)
                            if real(g):
                                if edges:
                                    pe.wait_ge(oc_ready, g + 1)
                                    if later(g, 1):
                                        pe.wait_ge(oh_ready, g)
                                    for j in range(G):
                                        m = nc.tensor.transpose(ohp[:, j * P:(j + 1) * P], oc[:, j].rearrange("p t k -> p (t k)"), identb[:])
                                    m.then_inc(ohp_ready, 1)
                                    pe.wait_ge(gl_done, g + 1)
                                pe.wait_ge(oh_ready, g + 1)
                                for k in range(parts):
                                    bank = k % banks
                                    if k >= banks:
                                        pe.wait_ge(c_read, g * parts + k - banks + 1)
                                    elif later(g, 1):
                                        pe.wait_ge(c_read, g * parts)
                                    for j in range(k * CB, min(G, k * CB + CB)):
                                        at = (j % CB) * cols
                                        lhs = oh[b][:, j * P:(j + 1) * P] if edges else oh[b][:, bass.DynSlice(j, P, step=G)]
                                        if edges:
                                            nc.tensor.matmul(pc[:, bank, D:4 * D], gl[b][:, j * P:(j + 1) * P], w_a[:], start=True, stop=True)
                                        m = nc.tensor.matmul(pc[:, bank, at:at + (D if edges else CW)], lhs, tab9[:, 0:D if edges else CW], start=True, stop=True)
                                    m.then_inc(c_ready, 1)
                            if real(g - 1):
                                for k in range(pairs):
                                    if k >= 2:
                                        pe.wait_ge(g_read, (g - 1) * pairs + k - 1)
                                    elif later(g, 2):
                                        pe.wait_ge(g_read, (g - 1) * pairs)
                                    for j in range(2 * k, min(G, 2 * k + 2)):
                                        lhs = oh[p][:, j * P:(j + 1) * P] if edges else oh[p][:, bass.DynSlice(j, P, step=G)]
                                        m = nc.tensor.matmul(pg[:, k % 2, j % 2], lhs, tab9[:, CW:CW + GW], start=True, stop=True)
                                    m.then_inc(g_ready, 1)
                        steps(pe, step)

                    @block.vector
                    def _(dve):
                        K1 = 3 + (G * TYPES + 3 if edges else 0)
                        K2 = 5 + pairs

                        def chain(sem_, base, count, total):
                            def link(ins):
                                count[0] += 1
                                assert count[0] <= total
                                ins.then_inc(sem_, 1)
                                dve.wait_ge(sem_, base + count[0])
                            return link

                        def first_half(i, g, b):
                            k = [0]
                            link = chain(c1, g * K1, k, K1)
                            dve.wait_ge(loaded[b], i * per_load + per_load)
                            if edges:
                                if later(g, 1):
                                    dve.wait_ge(ohp_ready, g)
                                hot = xr[b][:, :, C_TYPE:C_TYPE + TYPES]
                                dve.tensor_copy(oc[:], hot.rearrange("p j (t o) -> p j t o", o=1).to_broadcast([P, G, TYPES, SPLIT])).then_inc(oc_ready, 1)
                                link(dve.tensor_tensor(am[:], hot, a3[:].rearrange("p (o t) -> p o t", o=1).to_broadcast([P, G, TYPES]), ALU.mult))
                                link(dve.reduce_sum(om[:], am[:], AX.X))
                                link(dve.tensor_scalar(om[:], om[:], -1.0, 1.0, ALU.mult, ALU.add))
                            else:
                                if later(g, 3):
                                    dve.wait_ge(g_ready, (g - 2) * pairs)
                                dve.tensor_scalar(oh[b][:], t9[b][:], typ9[:], None, ALU.is_equal).then_inc(oh_ready, 1)
                            if later(g, 3):
                                dve.wait_ge(hs_done, g - 2)
                            for q in range(parts):
                                dve.wait_ge(c_ready, g * parts + q + 1)
                                for j in range(q * CB, min(G, q * CB + CB)):
                                    at = (j % CB) * cols
                                    dve.wait_ge(h_done, g * G + j + 1)
                                    keep = om[:, j:j + 1] if edges else pc[:, q % banks, at + D:at + CW]
                                    m = dve.scalar_tensor_tensor(rs[b][:, j], hb[b][:, j], keep, pc[:, q % banks, at:at + D], ALU.mult, ALU.add)
                                    if edges:
                                        for t in range(TYPES):
                                            link(m)
                                            m = dve.scalar_tensor_tensor(rs[b][:, j], pc[:, q % banks, D * (t + 1):D * (t + 2)], am[:, j, t:t + 1], rs[b][:, j], ALU.mult, ALU.add)
                                m.then_inc(c_read, 1)
                            dve.wait_ge(c_read, g * parts + parts)
                            for j in range(G):
                                m = dve.bn_stats(st[:, j], rs[b][:, j])
                            link(m)
                            aggregate(st, tmp, mean[0][b][:], var[0][b][:], link).then_inc(var2_ready, 1)

                        def slope(g, b):
                            dve.wait_ge(rstd2_ready, g + 1)
                            dve.scalar_tensor_tensor(nmr[0][b][:], mean[0][b][:], -1.0, rstd[0][b][:], ALU.mult, ALU.mult).then_inc(nm2_ready, 1)

                        def second_half(i, g, b, between):
                            k = [0]
                            link = chain(c2, g * K2, k, K2)
                            for q in range(pairs):
                                js = slice(2 * q, min(G, 2 * q + 2))
                                w = min(G, 2 * q + 2) - 2 * q
                                dve.wait_ge(g_ready, g * pairs + q + 1)
                                dve.wait_ge(y_done, g * G + min(G, 2 * q + 2))
                                link(dve.tensor_tensor(rs[b][:, js], rs[b][:, js], pg[:, q % 2, 0:w, 0:D], ALU.mult))
                                dve.tensor_tensor(rs[b][:, js], rs[b][:, js], pg[:, q % 2, 0:w, D:GW], ALU.add).then_inc(g_read, 1)
                            dve.wait_ge(g_read, g * pairs + pairs)
                            between()
                            link(dve.tensor_tensor(rs[b][:], rs[b][:], xr[b][:, :, 0:D], ALU.add))
                            for j in range(G):
                                m = dve.bn_stats(st[:, j], rs[b][:, j])
                            link(m)
                            aggregate(st, tmp, mean[1][b][:], var[1][b][:], link).then_inc(var3_ready, 1)
                            if later(g, 3):
                                dve.wait_ge(ot_out[b], i * 16)
                            if edges:
                                dve.tensor_copy(ot[b][:], rs[b][:]).then_inc(ot_done, 1)
                            else:
                                dve.tensor_tensor(ot[b][:], rs[b][:], rb2_all[:].rearrange("p (o d) -> p o d", o=1).to_broadcast([P, G, D]), ALU.add).then_inc(ot_done, 1)
                            dve.wait_ge(rstd3_ready, g + 1)
                            link(dve.tensor_tensor(sc3[b][:], rstd[1][b][:], xr[b][:, :, C_SO], ALU.mult))
                            dve.scalar_tensor_tensor(nmr[1][b][:], mean[1][b][:], -1.0, sc3[b][:], ALU.mult, ALU.mult).then_inc(nm3_ready, 1)
                            assert k[0] == K2

                        def step(i, b):
                            g = i * 3 + b
                            p = (b - 1) % 3
                            ip = i - (b == 0)
                            if real(g):
                                first_half(i, g, b)
                            if real(g - 1):
                                second_half(ip, g - 1, p, (lambda: slope(g, b)) if real(g) else (lambda: None))
                            elif real(g):
                                slope(g, b)
                        steps(dve, step)
                clear()

        rows_phase(False)

        agg_ctx = ExitStack()
        agg = sb_in(agg_ctx)("agg", [P, EP], F32)

        def edge_steps(eng, body, lag, ring=U):
            head = -(-(lag + ring) // ring)
            for i in range(head):
                for u in range(ring):
                    body(i, u)
            with eng.Fori(head, ET // ring) as i:
                for u in range(ring):
                    body(i, u)
            for n in range(ET, ET + lag):
                body(n // ring, n % ring)

        def lagged(i, u, k, ring=U):
            gi, v = i + (u - k) // ring, (u - k) % ring
            n = gi * ring + v
            if isinstance(i, int):
                return gi, v, n, 0 <= n < ET, n >= ring
            return gi, v, n, True, True

        with ExitStack() as ctx:
            lb, lp = sb_in(ctx), ps_in(ctx)
            ls, clear = phase_sems()
            W = 2 * P
            K18 = 2 * K9
            index = lb("index", [P, U, 2], I32)
            xs = lb("xs", [P, U, RW], F32)
            xd = lb("xd", [P, U, RW], F32)
            hh = lb("hh", [P, 2, 2, D], F32)
            types = lb("types", [P, U, 2, TYPES, SPLIT], F32)
            hm = lb("hm", [P, 2, 2, TYPES, D], F32)
            hT = lb("hT", [P, U, 2, TYPES, P], F32)
            typesT = lb("typesT", [K18, U, P], BF16)
            rel_in = lb("rel_in", [P, U, RELS, P], BF16)
            kvm = lb("kvm", [P, U, 2, RELS, P], F32)
            qT = lb("qT", [P, U, P], F32)
            prod = lb("prod", [P, 2, P], F32)
            bias18 = lb("bias18", [K18, 3, D], BF16)
            head_1 = lb("head_1", [P, HEADS], F32)
            head_sum = lb("head_sum", [P, P], F32)
            reset = lb("reset", [P, 2, W], F32)
            run = lb("run", [P, 3, W + 1], F32)
            diff = lb("diff", [P, 2, W], F32)
            expd = lb("expd", [P, 2, W], F32)
            wm = lb("wm", [P, W], F32)
            den = lb("den", [P, W], F32)
            tpb = lp("tpb", [P, 2, 4, P], F32)
            kv = lp("kv", [P, 2, P], F32)
            key = lp("key", [P, P], F32)
            att = [lp(f"att{h}", [P, W], F32) for h in range(2)]
            msg = [lp(f"msg{h}", [P, W], F32) for h in range(2)]
            idx_set = ls("idx_set")
            bias_zero, bias_in = ls("bias_zero"), ls("bias_in")
            got = [ls(f"got{u}") for u in range(U)]
            spilled = [ls(f"spilled{u}") for u in range(U)]
            reset_in = [ls(f"reset_in{h}") for h in range(2)]
            rels_in = [ls(f"rels_in{h}") for h in range(2)]
            types_ready, ats_ready = ls("types_ready"), ls("ats_ready")
            h_ready, src_masked, dst_masked = ls("h_ready"), ls("src_masked"), ls("dst_masked")
            seen, hT_ready, proj_ready = ls("seen"), ls("hT_ready"), ls("proj_ready")
            q_seen, q_ready = ls("q_seen"), ls("q_ready")
            kvm_ready, key_ready, prod_ready = ls("kvm_ready"), ls("key_ready"), ls("prod_ready")
            att_ready, msg_ready = ls("att_ready"), ls("msg_ready")
            heads_set, diff_ready, exp_ready = ls("heads_set"), ls("diff_ready"), ls("exp_ready")
            pair_step, sum_step, wm_ready, pair_done = ls("pair_step"), ls("sum_step"), ls("wm_ready"), ls("pair_done")
            PAIRS = ET // 2

            with nc.Block() as block:
                @block.gpsimd
                def _(pool):
                    def step(i, u):
                        g, v, n, real, again = lagged(i, u, 0)
                        if real:
                            if again:
                                pool.wait_ge(src_masked, (n - U) * TYPES + TYPES)
                                pool.wait_ge(dst_masked, n - U + 1)
                                pool.wait_ge(types_ready, (n - U) * 2 + 2)
                                pool.wait_ge(ats_ready, (n - U) * 2 + 2)
                                pool.wait_ge(spilled[v], g * 16)
                                settle(pool, "pool")
                            pool.tensor_copy(index[:, v:v + 1], ends_i[:, bass.ds(n, 1)]).then_inc(idx_set, 1)
                            pool.wait_ge(idx_set, n + 1)
                            settle(pool, "pool")
                            for to, k in ((xs, 0), (xd, 1)):
                                pool.indirect_dma_start(
                                    out=to[:, v, :], out_offset=None, in_=xt,
                                    in_offset=bass.IndirectOffsetOnAxis(ap=index[:, v, k:k + 1], axis=0)).then_inc(got[v], 16)
                        g, v, n, real, again = lagged(i, u, 2)
                        if real:
                            pool.wait_ge(got[v], g * 32 + 32)
                            if again:
                                pool.wait_ge(seen, n - U + 1)
                            settle(pool, "pool")
                            for k, of in ((0, xs), (1, xd)):
                                pool.tensor_copy(types[:, v, k], of[:, v, C_TYPE:C_TYPE + TYPES].rearrange("p (t o) -> p t o", o=1)
                                                 .to_broadcast([P, TYPES, SPLIT])).then_inc(types_ready, 1)
                            pool.tensor_copy(ats[:, bass.ds(n, 1), 0:3], xs[:, v:v + 1, C_SO:C_IDX + 1]).then_inc(ats_ready, 1)
                            pool.tensor_copy(ats[:, bass.ds(n, 1), 3:4], xd[:, v:v + 1, C_SI:C_SI + 1]).then_inc(ats_ready, 1)
                    edge_steps(pool, step, 2)

                @block.sync
                def _(sp):
                    def step(i, u):
                        n = i * U + u
                        real = not isinstance(n, int) or n < ET
                        if u % 2 == 0:
                            h, m = u // 2, i * 2 + u // 2
                            if real:
                                if not isinstance(m, int) or m >= 2:
                                    sp.wait_ge(kvm_ready, m * 2 - 2)
                                    settle(sp, "sp")
                                sp.dma_start(rel_in[:, u:u + 2], rel_row[bass.ds(m * 2, 2)].partition_broadcast(P)).then_inc(rels_in[h], 16)
                            if not isinstance(m, int) or 2 <= m <= PAIRS + 1:
                                if not isinstance(m, int) or m >= 4:
                                    sp.wait_ge(diff_ready, (m - 3) * 2)
                                    settle(sp, "sp")
                                sp.dma_start(reset[:, h], reset_row[bass.ds((m - 2) * W, W)].partition_broadcast(P)).then_inc(reset_in[h], 16)
                        if real:
                            sp.wait_ge(got[u], i * 32 + 32)
                            settle(sp, "sp")
                            sp.dma_start(xd_rows[bass.ds(n * P, P)], xd[:, u]).then_inc(spilled[u], 16)
                    sp.wait_ge(bias_zero, 1)
                    for t in range(TYPES):
                        at = 2 * D * TYPES + D * t
                        sp.dma_start(bias18[SPLIT * t:SPLIT * t + SPLIT, 0:2], bias3[:, 2 * D * t:2 * D * (t + 1)].rearrange("k (a d) -> k a d", a=2)).then_inc(bias_in, 16)
                        sp.dma_start(bias18[K9 + SPLIT * t:K9 + SPLIT * t + SPLIT, 2], bias3[:, at:at + D]).then_inc(bias_in, 16)
                    edge_steps(sp, step, 3)
                    for u in range(U):
                        sp.wait_ge(spilled[u], 16 * EG)

                @block.scalar
                def _(act):
                    def step(i, u):
                        g, v, n, real, again = lagged(i, u, 0)
                        if real:
                            w = v % 2
                            act.wait_ge(got[v], g * 32 + 32)
                            if not isinstance(n, int) or n >= 2:
                                act.wait_ge(dst_masked, n - 1)
                            for k, of in ((1, xd), (0, xs)):
                                nc.scalar.activation(hh[:, w, k], of[:, v, 0:D], ACT.Relu, bias=of[:, v, C_NMR:C_NMR + 1],
                                                     scale=of[:, v, C_RSTD:C_RSTD + 1]).then_inc(h_ready, 1)
                            act.wait_ge(h_ready, n * 2 + 2)
                            if not isinstance(n, int) or n >= 2:
                                act.wait_ge(seen, n - 1)
                            for t in range(TYPES):
                                nc.scalar.activation(hm[:, v % 2, 0, t], hh[:, v % 2, 0], ACT.Copy,
                                                     scale=xs[:, v, C_TYPE + t:C_TYPE + t + 1]).then_inc(src_masked, 1)
                        g, v, n, real, again = lagged(i, u, 1)
                        if real:
                            act.wait_ge(seen, n + 1)
                            if again:
                                act.wait_ge(proj_ready, n - U + 1)
                                act.wait_ge(q_seen, n - U + 1)
                            nc.scalar.activation(hT[:, v], tpb[:, :, 0:3], ACT.Copy).then_inc(hT_ready, 1)
                            nc.scalar.activation(typesT[:, v], tpb[0:K18, 1, 3], ACT.Copy).then_inc(hT_ready, 1)
                        g, v, n, real, again = lagged(i, u, 2)
                        if real:
                            act.wait_ge(q_seen, n + 1)
                            if again:
                                act.wait_ge(prod_ready, n - U + 1)
                            nc.scalar.activation(qT[:, v], tpb[:, 0, 3], ACT.Copy).then_inc(q_ready, 1)
                        g, v, n, real, again = lagged(i, u, 6)
                        if real and v % 2 == 0:
                            m = g * 2 + v // 2
                            act.wait_ge(diff_ready, m * 2 + 2)
                            if not isinstance(m, int) or m >= 1:
                                act.wait_ge(pair_done, m)
                            nc.scalar.activation(expd[:], diff[:], ACT.Exp).then_inc(exp_ready, 1)
                    edge_steps(act, step, 7)

                @block.tensor
                def _(pe):
                    def step(i, u):
                        g, v, n, real, again = lagged(i, u, 2)
                        if real:
                            pe.wait_ge(hT_ready, n * 2 + 2)
                            if not isinstance(n, int) or n >= 1:
                                pe.wait_ge(q_ready, n)
                            for t in range(TYPES):
                                nc.tensor.matmul(tpb[:, 0, 3], w_q[:, t], hT[:, v, 1, t], start=t == 0, stop=False)
                            nc.tensor.matmul(tpb[:, 0, 3], bias18[:, 2], typesT[:, v], start=False, stop=True).then_inc(q_seen, 1)
                        g, v, n, real, again = lagged(i, u, 1)
                        if real:
                            w = v % 2
                            pe.wait_ge(src_masked, n * TYPES + TYPES)
                            pe.wait_ge(dst_masked, n + 1)
                            pe.wait_ge(types_ready, n * 2 + 2)
                            if not isinstance(n, int) or n >= 1:
                                pe.wait_ge(hT_ready, n * 2)
                            if not isinstance(n, int) or n >= 2:
                                pe.wait_ge(q_ready, n - 1)
                            for k in range(2):
                                for t in range(TYPES):
                                    nc.tensor.transpose(tpb[:, k, t], hm[:, w, k, t], ident[:])
                            nc.tensor.transpose(tpb[0:K18, 1, 3], types[:, v].rearrange("p a t k -> p (a t k)"), ident[:]).then_inc(seen, 1)
                        g, v, n, real, again = lagged(i, u, 2)
                        if real:
                            pe.wait_ge(hT_ready, n * 2 + 2)
                            if not isinstance(n, int) or n >= 1:
                                pe.wait_ge(kvm_ready, n)
                            for k in range(2):
                                for t in range(TYPES):
                                    nc.tensor.matmul(kv[:, k], w_kv[:, t, k], hT[:, v, 0, t], start=t == 0, stop=False)
                                m = nc.tensor.matmul(kv[:, k], bias18[:, k], typesT[:, v], start=False, stop=True)
                            m.then_inc(proj_ready, 1)
                        g, v, n, real, again = lagged(i, u, 3)
                        if real:
                            if not isinstance(n, int) or n >= 1:
                                pe.wait_ge(prod_ready, n)
                            pe.wait_ge(kvm_ready, n + 1)
                            for r in range(RELS):
                                m = nc.tensor.matmul(key[:], rel_k[:, r], kvm[:, v, 0, r], start=r == 0, stop=r == RELS - 1)
                            m.then_inc(key_ready, 1)
                        g, v, n, real, again = lagged(i, u, 5)
                        if real:
                            h, cs = v // 2, slice(v % 2 * P, v % 2 * P + P)
                            if v % 2 == 0 and again:
                                pe.wait_ge(wm_ready, g * 2 + h - 1)
                            for r in range(RELS):
                                m = nc.tensor.matmul(msg[h][:, cs], rel_v[:, r], kvm[:, v, 1, r], start=r == 0, stop=r == RELS - 1)
                            m.then_inc(msg_ready, 1)
                        g, v, n, real, again = lagged(i, u, 4)
                        if real:
                            h, cs = v // 2, slice(v % 2 * P, v % 2 * P + P)
                            pe.wait_ge(prod_ready, n + 1)
                            if v % 2 == 0 and again:
                                pe.wait_ge(diff_ready, (g * 2 + h - 1) * 2)
                            nc.tensor.matmul(att[h][:, cs], head_sum[:], prod[:, v % 2], start=True, stop=True).then_inc(att_ready, 1)
                    pe.wait_ge(heads_set, 2)
                    pe.wait_ge(bias_in, 16 * 2 * TYPES)
                    edge_steps(pe, step, 5)

                @block.vector
                def _(dve):
                    dve.memset(bias18[:], 0.0).then_inc(bias_zero, 1)
                    dve.reduce_sum(head_1[:], ident[:].rearrange("p (h f) -> p h f", h=HEADS), AX.X).then_inc(heads_set, 1)
                    dve.wait_ge(heads_set, 1)
                    dve.tensor_copy(head_sum[:].rearrange("p (h f) -> p h f", h=HEADS),
                                    head_1[:].rearrange("p (h o) -> p h o", o=1).to_broadcast([P, HEADS, DK])).then_inc(heads_set, 1)
                    dve.memset(run[:], 0.0).then_inc(heads_set, 1)
                    dve.wait_ge(heads_set, 3)
                    C_PAIR = 3

                    def step(i, u):
                        g, v, n, real, again = lagged(i, u, 0)
                        if real:
                            w = v % 2
                            dve.wait_ge(h_ready, n * 2 + 1)
                            if not isinstance(n, int) or n >= 2:
                                dve.wait_ge(seen, n - 1)
                            dve.tensor_tensor(hm[:, w, 1], hh[:, w, 1].rearrange("p (o d) -> p o d", o=1).to_broadcast([P, TYPES, D]),
                                              xd[:, v, C_TYPE:C_TYPE + TYPES].rearrange("p (t o) -> p t o", o=1).to_broadcast([P, TYPES, D]),
                                              ALU.mult).then_inc(dst_masked, 1)
                        g, v, n, real, again = lagged(i, u, 2)
                        if real:
                            dve.wait_ge(proj_ready, n + 1)
                            dve.wait_ge(rels_in[v // 2], g * 16 + 16)
                            if again:
                                dve.wait_ge(msg_ready, n - U + 1)
                            dve.tensor_tensor(kvm[:, v], kv[:].rearrange("p a (o e) -> p a o e", o=1).to_broadcast([P, 2, RELS, P]),
                                              rel_in[:, v].rearrange("p (o r) e -> p o r e", o=1).to_broadcast([P, 2, RELS, P]),
                                              ALU.mult).then_inc(kvm_ready, 1)
                        g, v, n, real, again = lagged(i, u, 3)
                        if real:
                            dve.wait_ge(key_ready, n + 1)
                            if not isinstance(n, int) or n >= 2:
                                dve.wait_ge(att_ready, n - 1)
                            dve.wait_ge(q_ready, n + 1)
                            dve.tensor_tensor(prod[:, v % 2], key[:], qT[:, v], ALU.mult).then_inc(prod_ready, 1)
                        g, v, n, real, again = lagged(i, u, 6)
                        if real and v % 2 == 0:
                            first_half(g * 2 + v // 2, v // 2)
                        g, v, n, real, again = lagged(i, u, 7)
                        if real and v % 2 == 0:
                            second_half(g * 2 + v // 2, v // 2)

                    def first_half(m, h):
                        s0 = m * C_PAIR
                        dve.tensor_copy(run[:, :, 0], run[:, :, W]).then_inc(pair_step, 1)
                        dve.wait_ge(reset_in[h], (m - h) * 8 + 16)
                        dve.wait_ge(att_ready, m * 2 + 2)
                        dve.wait_ge(pair_step, s0 + 1)
                        dve.tensor_tensor_scan(run[:, 0, 1:W + 1], reset[:, h], att[h][:], run[:, 0, 0:1], ALU.add, ALU.max).then_inc(pair_step, 1)
                        dve.wait_ge(pair_step, s0 + 2)
                        dve.tensor_tensor(diff[:, 0], run[:, 0, 0:W], reset[:, h], ALU.add).then_inc(pair_step, 1)
                        dve.tensor_tensor(diff[:, 1], att[h][:], run[:, 0, 1:W + 1], ALU.subtract).then_inc(diff_ready, 1)
                        dve.wait_ge(pair_step, s0 + 3)
                        dve.tensor_tensor(diff[:, 0], diff[:, 0], run[:, 0, 1:W + 1], ALU.subtract).then_inc(diff_ready, 1)

                    def second_half(m, h):
                        dve.wait_ge(exp_ready, m + 1)
                        dve.tensor_tensor_scan(run[:, 2, 1:W + 1], expd[:, 0], expd[:, 1], run[:, 2, 0:1], ALU.mult, ALU.add).then_inc(sum_step, 1)
                        dve.wait_ge(msg_ready, m * 2 + 2)
                        dve.tensor_tensor(wm[:], expd[:, 1], msg[h][:], ALU.mult).then_inc(wm_ready, 1)
                        dve.wait_ge(sum_step, m * 4 + 1)
                        dve.tensor_scalar_add(den[:], run[:, 2, 1:W + 1], 1e-16).then_inc(sum_step, 1)
                        dve.wait_ge(wm_ready, m + 1)
                        dve.tensor_tensor_scan(run[:, 1, 1:W + 1], expd[:, 0], wm[:], run[:, 1, 0:1], ALU.mult, ALU.add).then_inc(sum_step, 1)
                        dve.wait_ge(sum_step, m * 4 + 3)
                        dve.reciprocal(den[:], den[:]).then_inc(sum_step, 1)
                        dve.wait_ge(sum_step, m * 4 + 4)
                        dve.tensor_tensor(agg[:, bass.ds(m * W, W)], run[:, 1, 1:W + 1], den[:], ALU.mult).then_inc(pair_done, 1)
                    edge_steps(dve, step, 7)
            clear()
        rows_phase(True)

        agg_ctx.close()
        R = 14

        def conv_phase(second):
            name = "conv2" if second else "conv1"
            ctx = ExitStack()
            with ctx:
                def lb(n, shape, dt):
                    return ctx.enter_context(nc.sbuf_tensor(f"{name}_{n}", shape, dt))

                def lp(n, shape, dt):
                    return ctx.enter_context(nc.psum_tensor(f"{name}_{n}", shape, dt))

                ls, clear = phase_sems(name + "_")

                table, w, b_all = (t1, w_2, b2_all) if second else (ta, w_1, b1_all)
                idx = lb("idx", [P, ET], I32)
                ring = lb("ring", [P, R, 1], I32)
                oring = lb("oring", [P, R, 1], I32)
                row = lb("row", [P, R, D], F32)
                sT = lb("sT", [P, R, P], F32)
                keep = lb("keep", [P, R, P], F32)
                res = lb("res", [P, R, D], F32)
                rx = lb("rx", [P, R, D], F32)
                pT = lp("pT", [P, 2, 512], F32)
                pm = lp("pm", [P, 2, 512], F32)
                idx_ready, ring_set, scaled = ls("idx_ready"), ls("ring_set"), ls("scaled")
                got = [ls(f"got{u}") for u in range(R)]
                keep_in = [ls(f"keep_in{u}") for u in range(R)]
                stored = [ls(f"stored{u}") for u in range(R)]
                t_ready, s_ready, m_ready, v_ready, res_ready = (
                    ls("t_ready"), ls("s_ready"), ls("m_ready"), ls("v_ready"), ls("res_ready"))
                x_in = [ls(f"x_in{u}") for u in range(R)] if second else None

                with nc.Block() as block:
                    @block.gpsimd
                    def _(pool):
                        pool.wait_ge(idx_ready, 1)
                        settle(pool, "pool")

                        def step(i, u):
                            g, v, n, real, again = lagged(i, u, 0, R)
                            if real:
                                if again:
                                    pool.wait_ge(t_ready, n - R + 1)
                                    settle(pool, "pool")
                                pool.tensor_copy(ring[:, v], idx[:, bass.ds(n, 1)]).then_inc(ring_set, 1)
                                if second:
                                    if again:
                                        pool.wait_ge(stored[v], g * 16)
                                        settle(pool, "pool")
                                    pool.tensor_copy(oring[:, v], out_i[:, bass.ds(n, 1)]).then_inc(ring_set, 1)
                                pool.wait_ge(ring_set, n * (1 + second) + 1 + second)
                                settle(pool, "pool")
                                pool.indirect_dma_start(out=row[:, v, :], out_offset=None, in_=table,
                                                        in_offset=bass.IndirectOffsetOnAxis(ap=ring[:, v], axis=0)).then_inc(got[v], 16)
                            g, v, n, real, again = lagged(i, u, 8, R)
                            if second and real:
                                pool.wait_ge(res_ready, n + 1)
                                settle(pool, "pool")
                                pool.indirect_dma_start(out=out, out_offset=bass.IndirectOffsetOnAxis(ap=oring[:, v], axis=0),
                                                        in_=res[:, v, :], in_offset=None, bounds_check=N - 1,
                                                        oob_is_err=False).then_inc(stored[v], 16)
                        edge_steps(pool, step, 8 if second else 0, R)
                        if second:
                            for u in range(R):
                                pool.wait_ge(stored[u], 16 * (ET // R))

                    @block.sync
                    def _(sp):
                        def step(i, u):
                            g, v, n, real, again = lagged(i, u, 0, R)
                            if real:
                                if again:
                                    sp.wait_ge(s_ready, n - R + 1)
                                    settle(sp, "sp")
                                sp.dma_start(keep[:, v], keep_row[bass.ds(n * P, P)].partition_broadcast(P)).then_inc(keep_in[v], 16)
                                if second:
                                    if again:
                                        sp.wait_ge(res_ready, n - R + 1)
                                        settle(sp, "sp")
                                    sp.dma_start(rx[:, v], x1_rows[bass.ds(n * P, P)]).then_inc(x_in[v], 16)
                            g, v, n, real, again = lagged(i, u, 8, R)
                            if real and not second:
                                sp.wait_ge(res_ready, n + 1)
                                settle(sp, "sp")
                                sp.dma_start(t1[bass.ds(n * P, P)], res[:, v]).then_inc(stored[v], 16)
                        edge_steps(sp, step, 8, R)
                        if not second:
                            for u in range(R):
                                sp.wait_ge(stored[u], 16 * (ET // R))

                    @block.scalar
                    def _(act):
                        def step(i, u):
                            g, v, n, real, again = lagged(i, u, 0, R)
                            if second and real:
                                act.wait_ge(got[v], g * 16 + 16)
                                settle(act, "act")
                                nc.scalar.activation(row[:, v], row[:, v], ACT.Copy, scale=ats[:, bass.ds(n, 1), 0]).then_inc(scaled, 1)
                            g, v, n, real, again = lagged(i, u, 2, R)
                            if not second and real:
                                act.wait_ge(v_ready, n + 1)
                                nc.scalar.activation(res[:, v], res[:, v], ACT.Relu).then_inc(res_ready, 1)
                        edge_steps(act, step, 2, R)

                    @block.tensor
                    def _(pe):
                        def step(i, u):
                            g, v, n, real, again = lagged(i, u, 0, R)
                            if real:
                                if second:
                                    pe.wait_ge(scaled, n + 1)
                                else:
                                    pe.wait_ge(got[v], g * 16 + 16)
                                if not isinstance(n, int) or n >= 2:
                                    pe.wait_ge(s_ready, n - 1)
                                nc.tensor.transpose(pT[:, v % 2, 0:P], row[:, v], ident[:]).then_inc(t_ready, 1)
                            g, v, n, real, again = lagged(i, u, 1, R)
                            if real:
                                pe.wait_ge(s_ready, n + 1)
                                if not isinstance(n, int) or n >= 2:
                                    pe.wait_ge(v_ready, n - 1)
                                nc.tensor.matmul(pm[:, v % 2, 0:D], sT[:, v], w[:], start=True, stop=True).then_inc(m_ready, 1)
                        edge_steps(pe, step, 1, R)

                    @block.vector
                    def _(dve):
                        dve.tensor_scalar(idx[:], ats[:, :, 2], float(EP) if second else float(EP + NP), None, ALU.min).then_inc(idx_ready, 1)

                        def step(i, u):
                            g, v, n, real, again = lagged(i, u, 0, R)
                            if real:
                                dve.wait_ge(t_ready, n + 1)
                                dve.wait_ge(keep_in[v], g * 16 + 16)
                                if again:
                                    dve.wait_ge(m_ready, n - R + 1)
                                if isinstance(n, int) and n == 0:
                                    before = 0.0
                                else:
                                    dve.wait_ge(s_ready, n)
                                    before = sT[:, (v - 1) % R, P - 1:P]
                                dve.tensor_tensor_scan(sT[:, v], keep[:, v], pT[:, v % 2, 0:P], before, ALU.mult, ALU.add).then_inc(s_ready, 1)
                            g, v, n, real, again = lagged(i, u, 2, R)
                            if real:
                                dve.wait_ge(m_ready, n + 1)
                                if again:
                                    dve.wait_ge(stored[v], g * 16)
                                dve.scalar_tensor_tensor(res[:, v], pm[:, v % 2, 0:D], ats[:, bass.ds(n, 1), 3], b_all[:], ALU.mult, ALU.add).then_inc(v_ready, 1)
                                if second:
                                    dve.wait_ge(x_in[v], g * 16 + 16)
                                    dve.wait_ge(v_ready, n + 1)
                                    dve.scalar_tensor_tensor(res[:, v], res[:, v], 0.0, rx[:, v], ALU.max, ALU.add).then_inc(res_ready, 1)
                        edge_steps(dve, step, 2, R)
                clear()

        conv_phase(False)
        conv_phase(True)


_INS = ['x', 'src', 'dst', 'edge_type_4', 'node_type_3', 'L0_gnn_Wk', 'L0_gnn_bk', 'L0_gnn_Wq', 'L0_gnn_bq', 'L0_gnn_Wv',
        'L0_gnn_bv', 'L0_gnn_Wa', 'L0_gnn_ba', 'L0_gnn_rel_pri', 'L0_gnn_rel_att', 'L0_gnn_rel_msg', 'L0_gnn_skip',
        'L0_gnn_ln_g', 'L0_gnn_ln_b', 'L1_gnn_W1', 'L1_gnn_b1', 'L1_gnn_W2', 'L1_gnn_b2']
_OUTS = [((N, D), 'float32')]


def kernel(**inputs):
    import numpy as _np
    import concourse.bacc as _bacc
    from concourse import mybir as _mybir
    from concourse.bass_utils import run_bass_kernel_spmd as _run

    nc = _bacc.Bacc("TRN2", target_bir_lowering=False, num_devices=1)
    arrays, args = {}, []
    for name in _INS:
        a = _np.ascontiguousarray(inputs[name])
        arrays[f"in_{name}_dram"] = a
        args.append(nc.dram_tensor(f"in_{name}_dram", a.shape, _mybir.dt.from_np(a.dtype), kind="ExternalInput").ap())
    for i, (shape, dtype) in enumerate(_OUTS):
        dt = _mybir.dt.from_np(_np.dtype(dtype))
        args.append(nc.dram_tensor(f"out_{i}_dram", shape, dt, kind="ExternalOutput").ap())
    hgt_then_graphconv(nc, *args)
    r = _run(nc, [arrays], core_ids=[0])
    got = tuple(r.results[0][f"out_{i}_dram"] for i in range(len(_OUTS)))
    return got[0]
```
